# Optimizing a Trainium2 kernel written in Bass

```python
import numpy as np
import jax
import jax.numpy as jnp

def _softmax(x, axis=-1):
    return jax.nn.softmax(x, axis=axis)

def _gelu(x):
    return jax.nn.gelu(x, approximate=True)

def _silu(x):
    return jax.nn.silu(x)

def _sigmoid(x):
    return jax.nn.sigmoid(x)

def _layernorm(x, axis=-1, eps=1e-05):
    m = jnp.mean(x, axis=axis, keepdims=True)
    v = jnp.var(x, axis=axis, keepdims=True)
    return (x - m) / jnp.sqrt(v + eps)

def _scatter_add(tgt, idx, src, axis=0):
    return tgt.at[idx].add(src)

def _segment_sum(src, seg, n):
    return jax.ops.segment_sum(src, seg, n)
kernel_name = 'mk_flamingo_gated_d2_seqx_r4_b26777'

def setup_inputs(seed: int=0):
    np.random.seed(seed)
    _w = jnp.asarray

    def _rec_inputs():
        import jax
        import jax.numpy as jnp
        _rk = jax.random.key(seed)
        x = 7.22e-05 + 1 * jax.random.normal(jax.random.fold_in(_rk, 1), (4, 512, 256), jnp.float32)
        _lenS = 512 - jax.random.randint(jax.random.fold_in(_rk, 7), (4,), 0, max(1, 512 // 4) + 1, jnp.int32)
        _lenS2 = 512 - jax.random.randint(jax.random.fold_in(_rk, 8), (4,), 0, max(1, 512 // 4) + 1, jnp.int32)
        _ctx_1024P = jax.random.normal(jax.random.fold_in(_rk, 11), (4, 16, 256), jnp.float32)
        _ctx_1024c = jax.random.dirichlet(jax.random.fold_in(_rk, 511), 0.3 * jnp.ones((16,), jnp.float32), (4, 512))
        _ctx_1024t = jnp.einsum('bsk,bkd->bsd', _ctx_1024c, _ctx_1024P)
        _ctx_1024t = _ctx_1024t * jax.lax.rsqrt(jnp.mean(jnp.square(_ctx_1024t)) + 1e-12) * 0.953939
        ctx_1024 = 4.13588e-05 + 0.999923 * (_ctx_1024t + 0.3 * jax.random.normal(jax.random.fold_in(_rk, 611), (4, 512, 256), jnp.float32))
        _g = jax.random.normal(jax.random.fold_in(_rk, 9001), (2, 2), jnp.float32)
        _g = jnp.sign(_g) * jnp.maximum(jnp.abs(_g), 1.0) + (_g == 0) * 1.0
        g_xattn = _g[0]
        g_ffn = _g[1]
        return (x, ctx_1024, g_xattn, g_ffn)
    x, ctx_1024, g_xattn, g_ffn = _rec_inputs()

    def _L0_xattn_setup():
        import jax, jax.numpy as jnp
        import numpy as np
        B, T, D, H = (4, 512, 256, 1024)
        S = 64
        EPS = 1e-05

        def _layer_norm(x, gamma, beta):
            mu = jnp.mean(x, axis=-1, keepdims=True)
            var = jnp.mean(jnp.square(x - mu), axis=-1, keepdims=True)
            return (x - mu) * jax.lax.rsqrt(var + EPS) * gamma + beta

        def _aft_local(emb, wq, bq, wk, bk, wv, bv, wo, bo, pos_bias):
            q = emb @ wq + bq
            k = emb @ wk + bk
            v = emb @ wv + bv
            idx = jnp.arange(T)
            mask = (jnp.abs(idx[:, None] - idx[None, :]) < S).astype(pos_bias.dtype)
            w = pos_bias * mask
            max_k = jnp.max(k, axis=1, keepdims=True)
            max_w = jnp.max(w, axis=1, keepdims=True)
            ek = jnp.exp(k - max_k)
            ew = jnp.exp(w - max_w)
            num = jnp.einsum('tj,bjd->btd', ew, ek * v)
            den = jnp.einsum('tj,bjd->btd', ew, ek)
            y = jax.nn.sigmoid(q) * num / den
            return y @ wo + bo
        key = jax.random.key(seed)
        ks = jax.random.split(key, 16)
        sd = 0.02
        return {'x': jax.random.normal(ks[0], (B, T, D), jnp.float32), 'pos_encod': jax.random.normal(ks[1], (B, T, D), jnp.float32), 'wq': jax.random.normal(ks[2], (D, D), jnp.float32) * sd, 'bq': jnp.zeros((D,), jnp.float32), 'wk': jax.random.normal(ks[3], (D, D), jnp.float32) * sd, 'bk': jnp.zeros((D,), jnp.float32), 'wv': jax.random.normal(ks[4], (D, D), jnp.float32) * sd, 'bv': jnp.zeros((D,), jnp.float32), 'wo': jax.random.normal(ks[5], (D, D), jnp.float32) * sd, 'bo': jnp.zeros((D,), jnp.float32), 'pos_bias': jax.random.normal(ks[6], (T, T), jnp.float32) * sd, 'gamma': jnp.ones((D,), jnp.float32), 'beta': jnp.zeros((D,), jnp.float32), 'w1': jax.random.normal(ks[7], (D, H), jnp.float32) * sd, 'b1': jnp.zeros((H,), jnp.float32), 'w2': jax.random.normal(ks[8], (H, D), jnp.float32) * sd, 'b2': jnp.zeros((D,), jnp.float32)}
    _L0_xattn_all = _L0_xattn_setup()
    _L0_xattn_in = {k: v for k, v in _L0_xattn_all.items() if k in ('wq', 'bq', 'wk', 'bk', 'wv', 'bv', 'wo', 'bo', 'pos_bias', 'gamma', 'beta', 'w1', 'b1', 'w2', 'b2')}
    del _L0_xattn_all

    def _L0_ffn_setup():
        import jax, jax.numpy as jnp
        import numpy as np
        B, T, C = (2, 512, 256)
        E, F = (8, 256)
        FS = 512
        TOP_K = 2
        key = jax.random.key(seed)
        ks = jax.random.split(key, 6)
        s = lambda *d: 1.0 / np.sqrt(d[-1])
        return {'hidden_tensor': jax.random.normal(ks[0], (B, T, C), jnp.float32), 'w_router': jax.random.normal(ks[1], (E, C), jnp.float32) * s(C), 'w1_stack': jax.random.normal(ks[2], (E, F, C), jnp.float32) * s(C), 'w2_stack': jax.random.normal(ks[3], (E, C, F), jnp.float32) * s(F), 'ws1': jax.random.normal(ks[4], (FS, C), jnp.float32) * s(C), 'ws2': jax.random.normal(ks[5], (C, FS), jnp.float32) * s(FS)}
    _L0_ffn_all = _L0_ffn_setup()
    _L0_ffn_in = {k: v for k, v in _L0_ffn_all.items() if k in ('w_router', 'w1_stack', 'w2_stack', 'ws1', 'ws2')}
    del _L0_ffn_all

    def _L1_xattn_setup():
        import jax, jax.numpy as jnp
        import numpy as np
        D = 256
        NUM_ITERS = 3
        EPS = 1e-06
        SCALE = D ** (-0.5)

        def rmsnorm(x, w, eps=EPS):
            return x * jax.lax.rsqrt(jnp.mean(x * x, axis=-1, keepdims=True) + eps) * w

        def gru_cell(x, h, wih, whh, bih, bhh):
            gx = x @ wih.T + bih
            gh = h @ whh.T + bhh
            xr, xz, xn = jnp.split(gx, 3, axis=-1)
            hr, hz, hn = jnp.split(gh, 3, axis=-1)
            r = jax.nn.sigmoid(xr + hr)
            z = jax.nn.sigmoid(xz + hz)
            n = jnp.tanh(xn + r * hn)
            return (1.0 - z) * n + z * h
        key = jax.random.key(seed)
        ks = jax.random.split(key, 8)
        B, K, M, d = (8, 64, 1024, D)
        w_std = d ** (-0.5)
        return {'slots': jax.random.normal(ks[0], (B, K, d), jnp.float32), 'P': jax.random.normal(ks[1], (B, M, d), jnp.float32), 'Wq': jax.random.normal(ks[2], (d, d), jnp.float32) * w_std, 'Wk': jax.random.normal(ks[3], (d, d), jnp.float32) * w_std, 'Wv': jax.random.normal(ks[4], (d, d), jnp.float32) * w_std, 'gru_wih': jax.random.normal(ks[5], (3 * d, d), jnp.float32) * w_std, 'gru_whh': jax.random.normal(ks[6], (3 * d, d), jnp.float32) * w_std, 'gru_bih': jnp.zeros((3 * d,), jnp.float32), 'gru_bhh': jnp.zeros((3 * d,), jnp.float32), 'slot_norm_w': jnp.ones((d,), jnp.float32), 'input_norm_w': jnp.ones((d,), jnp.float32)}
    _L1_xattn_all = _L1_xattn_setup()
    _L1_xattn_in = {k: v for k, v in _L1_xattn_all.items() if k in ('Wq', 'Wk', 'Wv', 'gru_wih', 'gru_whh', 'gru_bih', 'gru_bhh', 'slot_norm_w', 'input_norm_w')}
    del _L1_xattn_all

    def _L1_ffn_setup():
        import jax, jax.numpy as jnp
        import numpy as np
        D_MODEL, D_FF, N_EXPERTS, TOP_K = (256, 512, 8, 2)
        B, S = (2, 512)
        key = jax.random.key(seed)
        ks = jax.random.split(key, 6)
        sd = 1.0 / np.sqrt(D_MODEL)
        sf = 1.0 / np.sqrt(D_FF)
        return {'x': jax.random.normal(ks[0], (B, S, D_MODEL), jnp.float32), 'router_w': jax.random.normal(ks[1], (N_EXPERTS, D_MODEL), jnp.float32) * sd, 'gate_w': jax.random.normal(ks[2], (N_EXPERTS, D_MODEL, D_FF), jnp.float32) * sd, 'gate_b': jnp.zeros((N_EXPERTS, D_FF), jnp.float32), 'up_w': jax.random.normal(ks[3], (N_EXPERTS, D_MODEL, D_FF), jnp.float32) * sd, 'up_b': jnp.zeros((N_EXPERTS, D_FF), jnp.float32), 'down_w': jax.random.normal(ks[4], (N_EXPERTS, D_FF, D_MODEL), jnp.float32) * sf, 'down_b': jnp.zeros((N_EXPERTS, D_MODEL), jnp.float32)}
    _L1_ffn_all = _L1_ffn_setup()
    _L1_ffn_in = {k: v for k, v in _L1_ffn_all.items() if k in ('router_w', 'gate_w', 'gate_b', 'up_w', 'up_b', 'down_w', 'down_b')}
    del _L1_ffn_all
    return {'x': x, 'ctx_1024': ctx_1024, 'g_xattn': g_xattn, 'g_ffn': g_ffn, 'L0_xattn_wq': _L0_xattn_in['wq'], 'L0_xattn_bq': _L0_xattn_in['bq'], 'L0_xattn_wk': _L0_xattn_in['wk'], 'L0_xattn_bk': _L0_xattn_in['bk'], 'L0_xattn_wv': _L0_xattn_in['wv'], 'L0_xattn_bv': _L0_xattn_in['bv'], 'L0_xattn_wo': _L0_xattn_in['wo'], 'L0_xattn_bo': _L0_xattn_in['bo'], 'L0_xattn_pos_bias': _L0_xattn_in['pos_bias'], 'L0_xattn_gamma': _L0_xattn_in['gamma'], 'L0_xattn_beta': _L0_xattn_in['beta'], 'L0_xattn_w1': _L0_xattn_in['w1'], 'L0_xattn_b1': _L0_xattn_in['b1'], 'L0_xattn_w2': _L0_xattn_in['w2'], 'L0_xattn_b2': _L0_xattn_in['b2'], 'L0_ffn_w_router': _L0_ffn_in['w_router'], 'L0_ffn_w1_stack': _L0_ffn_in['w1_stack'], 'L0_ffn_w2_stack': _L0_ffn_in['w2_stack'], 'L0_ffn_ws1': _L0_ffn_in['ws1'], 'L0_ffn_ws2': _L0_ffn_in['ws2'], 'L1_xattn_Wq': _L1_xattn_in['Wq'], 'L1_xattn_Wk': _L1_xattn_in['Wk'], 'L1_xattn_Wv': _L1_xattn_in['Wv'], 'L1_xattn_gru_wih': _L1_xattn_in['gru_wih'], 'L1_xattn_gru_whh': _L1_xattn_in['gru_whh'], 'L1_xattn_gru_bih': _L1_xattn_in['gru_bih'], 'L1_xattn_gru_bhh': _L1_xattn_in['gru_bhh'], 'L1_xattn_slot_norm_w': _L1_xattn_in['slot_norm_w'], 'L1_xattn_input_norm_w': _L1_xattn_in['input_norm_w'], 'L1_ffn_router_w': _L1_ffn_in['router_w'], 'L1_ffn_gate_w': _L1_ffn_in['gate_w'], 'L1_ffn_gate_b': _L1_ffn_in['gate_b'], 'L1_ffn_up_w': _L1_ffn_in['up_w'], 'L1_ffn_up_b': _L1_ffn_in['up_b'], 'L1_ffn_down_w': _L1_ffn_in['down_w'], 'L1_ffn_down_b': _L1_ffn_in['down_b']}

def reference(x, ctx_1024, g_xattn, g_ffn, L0_xattn_wq, L0_xattn_bq, L0_xattn_wk, L0_xattn_bk, L0_xattn_wv, L0_xattn_bv, L0_xattn_wo, L0_xattn_bo, L0_xattn_pos_bias, L0_xattn_gamma, L0_xattn_beta, L0_xattn_w1, L0_xattn_b1, L0_xattn_w2, L0_xattn_b2, L0_ffn_w_router, L0_ffn_w1_stack, L0_ffn_w2_stack, L0_ffn_ws1, L0_ffn_ws2, L1_xattn_Wq, L1_xattn_Wk, L1_xattn_Wv, L1_xattn_gru_wih, L1_xattn_gru_whh, L1_xattn_gru_bih, L1_xattn_gru_bhh, L1_xattn_slot_norm_w, L1_xattn_input_norm_w, L1_ffn_router_w, L1_ffn_gate_w, L1_ffn_gate_b, L1_ffn_up_w, L1_ffn_up_b, L1_ffn_down_w, L1_ffn_down_b):
    import jax
    import jax.numpy as jnp

    def _L0_xattn_ref(x, pos_encod, wq, bq, wk, bk, wv, bv, wo, bo, pos_bias, gamma, beta, w1, b1, w2, b2):
        import jax, jax.numpy as jnp
        import numpy as np
        B, T, D, H = (4, 512, 256, 1024)
        S = 64
        EPS = 1e-05

        def _layer_norm(x, gamma, beta):
            mu = jnp.mean(x, axis=-1, keepdims=True)
            var = jnp.mean(jnp.square(x - mu), axis=-1, keepdims=True)
            return (x - mu) * jax.lax.rsqrt(var + EPS) * gamma + beta

        def _aft_local(emb, wq, bq, wk, bk, wv, bv, wo, bo, pos_bias):
            q = emb @ wq + bq
            k = emb @ wk + bk
            v = emb @ wv + bv
            idx = jnp.arange(T)
            mask = (jnp.abs(idx[:, None] - idx[None, :]) < S).astype(pos_bias.dtype)
            w = pos_bias * mask
            max_k = jnp.max(k, axis=1, keepdims=True)
            max_w = jnp.max(w, axis=1, keepdims=True)
            ek = jnp.exp(k - max_k)
            ew = jnp.exp(w - max_w)
            num = jnp.einsum('tj,bjd->btd', ew, ek * v)
            den = jnp.einsum('tj,bjd->btd', ew, ek)
            y = jax.nn.sigmoid(q) * num / den
            return y @ wo + bo
        emb = x + pos_encod
        attn = _aft_local(emb, wq, bq, wk, bk, wv, bv, wo, bo, pos_bias)
        a = _layer_norm(attn + emb, gamma, beta)
        ff = jax.nn.relu(a @ w1 + b1) @ w2 + b2
        return _layer_norm(ff + a, gamma, beta)

    def _L0_ffn_ref(hidden_tensor, w_router, w1_stack, w2_stack, ws1, ws2):
        import jax, jax.numpy as jnp
        import numpy as np
        B, T, C = (2, 512, 256)
        E, F = (8, 256)
        FS = 512
        TOP_K = 2
        Bb, Tt, Cc = hidden_tensor.shape
        x = hidden_tensor.reshape(-1, Cc)
        t = x.shape[0]
        logits = x @ w_router.T
        probs = jax.nn.softmax(logits, axis=-1)
        expert_weight, expert_idx = jax.lax.top_k(probs, TOP_K)
        expert_weight = expert_weight / jnp.sum(expert_weight, axis=-1, keepdims=True)
        flat_e = expert_idx.reshape(-1)
        order = jnp.argsort(flat_e, stable=True)
        sorted_e = flat_e[order]
        flat_tok = jnp.repeat(jnp.arange(t), TOP_K)
        sorted_tok = flat_tok[order]
        sorted_w = expert_weight.reshape(-1)[order]
        counts = jnp.bincount(sorted_e, length=E)
        offsets = jnp.concatenate([jnp.zeros((1,), counts.dtype), jnp.cumsum(counts)])
        local_pos = jnp.arange(t * TOP_K) - offsets[sorted_e]
        cap = t * TOP_K
        binned = jnp.zeros((E, cap, Cc), x.dtype).at[sorted_e, local_pos].set(x[sorted_tok])
        inter = jnp.einsum('ecd,efd->ecf', binned, w1_stack)
        inter = jnp.square(jax.nn.relu(inter))
        outb = jnp.einsum('ecf,edf->ecd', inter, w2_stack)
        flat_out = outb[sorted_e, local_pos] * sorted_w[:, None]
        moe_out = jnp.zeros((t, Cc), x.dtype).at[sorted_tok].add(flat_out)
        moe_out = moe_out.reshape(Bb, Tt, Cc)
        sh = jnp.square(jax.nn.relu(jnp.einsum('btc,fc->btf', hidden_tensor, ws1)))
        shared_out = jnp.einsum('btf,cf->btc', sh, ws2)
        return shared_out + moe_out

    def _L1_xattn_ref(slots, P, Wq, Wk, Wv, gru_wih, gru_whh, gru_bih, gru_bhh, slot_norm_w, input_norm_w):
        import jax, jax.numpy as jnp
        import numpy as np
        D = 256
        NUM_ITERS = 3
        EPS = 1e-06
        SCALE = D ** (-0.5)

        def rmsnorm(x, w, eps=EPS):
            return x * jax.lax.rsqrt(jnp.mean(x * x, axis=-1, keepdims=True) + eps) * w

        def gru_cell(x, h, wih, whh, bih, bhh):
            gx = x @ wih.T + bih
            gh = h @ whh.T + bhh
            xr, xz, xn = jnp.split(gx, 3, axis=-1)
            hr, hz, hn = jnp.split(gh, 3, axis=-1)
            r = jax.nn.sigmoid(xr + hr)
            z = jax.nn.sigmoid(xz + hz)
            n = jnp.tanh(xn + r * hn)
            return (1.0 - z) * n + z * h
        Pn = rmsnorm(P, input_norm_w)
        k_proj = Pn @ Wk.T
        v_proj = Pn @ Wv.T
        for _ in range(NUM_ITERS):
            sn = rmsnorm(slots, slot_norm_w)
            q_proj = sn @ Wq.T
            scores = jnp.einsum('bkd,bmd->bkm', q_proj, k_proj) * SCALE
            attn = jax.nn.softmax(scores, axis=-2)
            attn = attn / (jnp.sum(attn, axis=-1, keepdims=True) + EPS)
            updates = jnp.einsum('bkm,bmd->bkd', attn, v_proj)
            slots = gru_cell(updates, slots, gru_wih, gru_whh, gru_bih, gru_bhh)
        return slots

    def _L1_ffn_ref(x, router_w, gate_w, gate_b, up_w, up_b, down_w, down_b):
        import jax, jax.numpy as jnp
        import numpy as np
        D_MODEL, D_FF, N_EXPERTS, TOP_K = (256, 512, 8, 2)
        B, S = (2, 512)
        b, s, d = x.shape
        xf = x.reshape(b * s, d)
        n = xf.shape[0]
        router_logits = xf @ router_w.T
        probs = jax.nn.softmax(router_logits, axis=-1)
        topv, topi = jax.lax.top_k(probs, TOP_K)
        mask = jnp.zeros_like(probs).at[jnp.arange(n)[:, None], topi].set(1.0)
        probs = probs * mask
        probs = probs / (probs.sum(axis=-1, keepdims=True) + 1e-09)
        g = jnp.einsum('nd,edf->nef', xf, gate_w) + gate_b
        u = jnp.einsum('nd,edf->nef', xf, up_w) + up_b
        h = jax.nn.silu(g) * u
        expert_out = jnp.einsum('nef,efd->ned', h, down_w) + down_b
        y = jnp.einsum('ne,ned->nd', probs, expert_out)
        return y.reshape(b, s, d)
    x = x + jnp.tanh(g_xattn[0]) * _L0_xattn_ref(_layernorm(x, axis=-1), ctx_1024, L0_xattn_wq, L0_xattn_bq, L0_xattn_wk, L0_xattn_bk, L0_xattn_wv, L0_xattn_bv, L0_xattn_wo, L0_xattn_bo, L0_xattn_pos_bias, L0_xattn_gamma, L0_xattn_beta, L0_xattn_w1, L0_xattn_b1, L0_xattn_w2, L0_xattn_b2)
    x = x + jnp.tanh(g_ffn[0]) * _L0_ffn_ref(_layernorm(x, axis=-1), L0_ffn_w_router, L0_ffn_w1_stack, L0_ffn_w2_stack, L0_ffn_ws1, L0_ffn_ws2)
    x = x + jnp.tanh(g_xattn[1]) * _L1_xattn_ref(_layernorm(x, axis=-1), ctx_1024, L1_xattn_Wq, L1_xattn_Wk, L1_xattn_Wv, L1_xattn_gru_wih, L1_xattn_gru_whh, L1_xattn_gru_bih, L1_xattn_gru_bhh, L1_xattn_slot_norm_w, L1_xattn_input_norm_w)
    x = x + jnp.tanh(g_ffn[1]) * _L1_ffn_ref(_layernorm(x, axis=-1), L1_ffn_router_w, L1_ffn_gate_w, L1_ffn_gate_b, L1_ffn_up_w, L1_ffn_up_b, L1_ffn_down_w, L1_ffn_down_b)
    return x

_drawn_inputs = setup_inputs


def setup_inputs(seed=0):
    import zlib

    import numpy as np

    out = dict(_drawn_inputs(seed))
    spreads = {'g_ffn': (-1.0, 0.6),
     'L0_xattn_bq': (0.0, 1.959),
     'L0_xattn_bk': (0.0, 2.0),
     'L0_xattn_bv': (0.0, 0.286),
     'L0_xattn_bo': (0.0, 0.1),
     'L0_xattn_gamma': (1.0, 0.2),
     'L0_xattn_beta': (0.0, 0.1),
     'L0_xattn_b1': (0.0, 0.1),
     'L0_xattn_b2': (0.0, 0.1),
     'L1_xattn_gru_bih': (0.0, 0.1),
     'L1_xattn_gru_bhh': (0.0, 0.274),
     'L1_xattn_slot_norm_w': (1.0, 0.6),
     'L1_xattn_input_norm_w': (1.0, 0.2),
     'L1_ffn_gate_b': (0.0, 0.414),
     'L1_ffn_up_b': (0.0, 0.411),
     'L1_ffn_down_b': (0.0, 0.1)}
    factors = {'L0_xattn_wq': 3.569, 'L0_xattn_wk': 5.483, 'L0_xattn_pos_bias': 176.416}
    for name, (base, spread) in spreads.items():
        noise = np.random.default_rng([zlib.crc32(name.encode()), seed]).standard_normal(out[name].shape)
        drawn = base * np.exp(spread * noise) if base else spread * noise
        out[name] = jnp.asarray(drawn.astype(out[name].dtype))
    for name, factor in factors.items():
        out[name] = (out[name] * factor).astype(out[name].dtype)
    return out
```

```python
from contextlib import ExitStack

import numpy as np
import concourse.bass as bass
from concourse import mybir
from concourse.alu_op_type import AluOpType as ALU

P = 128
F32 = mybir.dt.float32
F32R = mybir.dt.float32r
BF16 = mybir.dt.bfloat16
I32 = mybir.dt.int32
U32 = mybir.dt.uint32
ACT = mybir.ActivationFunctionType
AX = mybir.AxisListType.X

B, T, D = 4, 512, 256
TT = T // P
C = D // P
H = 1024
HC = H // P
BAND = 64
E = 8
FS = 512
SC = FS // P
F1 = 256
F2 = 512
G = 256
CAP = B * T
NG = B * T * 2 // G + E
XROWS = E * CAP + 1024 * 2
ITERS = 3
PAIRS = B // 2

COLS = {}
for _name, _n in (("bq", C), ("bk", C), ("bv", C), ("gamma", C), ("beta", C), ("b1", HC), ("w_in", C), ("w_slot", C),
                  ("bih", 3 * C), ("bhh", 3 * C), ("gate_b", E * F2 // P), ("up_b", E * F2 // P)):
    _at = sum(n for _, n in COLS.values())
    COLS[_name] = (_at, _n)
NCOLS = sum(n for _, n in COLS.values())
ROWS = {"bo": 0, "gamma": D, "beta": 2 * D, "b2": 3 * D, "g": 4 * D}
NROWS = 4 * D + 4


def build(nc, x, ctx_in, cols, rows, wq, wk, wv, wo, pos_bias, w1, w2, router1, m1_w1, m1_w2, ws1, ws2,
          Wq, Wk, Wv, wih, whh, router2, gate_w, up_w, down_w, down_b, out):
    top = ExitStack()
    with top:
        def sb(name, shape, dt=F32, where=None):
            return (where or top).enter_context(nc.sbuf_tensor(name, shape, dt))

        sems = {}

        def sem(name):
            if name not in sems:
                sems[name] = top.enter_context(nc.semaphore(name))
            return sems[name]

        x_base = nc.dram_tensor("x_base", (2, B, T, D), F32, kind="Internal").ap()
        routed = [nc.dram_tensor(f"routed{m}", (XROWS, D), F32, kind="Internal").ap() for m in range(2)]

        PS = top.enter_context(nc.psum_tensor("PS", [P, 8, 512], F32))
        ident = sb("ident", [P, P])
        ones = sb("ones", [P, P])
        tri = sb("tri", [P, P], BF16)
        ones_bf = sb("ones_bf", [P, P], BF16)
        zeros = sb("zeros", [P, 4 * D])
        colv = sb("colv", [P, NCOLS])
        rowv = sb("rowv", [P, NROWS])
        minus_half = sb("minus_half", [P, TT])
        hbq = sb("hbq", [P, C])
        tanh_g = sb("tanh_g", [P, 4])
        bb = sb("bb", [P, D])
        g1 = sb("g1", [P, D])
        be1 = sb("be1", [P, D])
        iota_e = sb("iota_e", [P, E])
        ebase = sb("ebase", [P, E])
        iota_g = sb("iota_g", [P, 32])
        rw = [sb(f"rw{m}", [P, C, E], F32R) for m in range(4)]
        dest = [sb(f"dest{m}", [P, B, TT, 2], I32) for m in range(2)]
        share = [sb(f"share{m}", [P, B, TT, 2]) for m in range(2)]
        carry = sb("carry", [P, TT + 1, E])
        table = [sb(f"table{m}", [1, 64], I32) for m in range(2)]
        tfi = sb("tfi", [1, 2, E], I32)
        two = range(2)
        X = [sb(f"X{h}", [P, TT, D]) for h in two]
        EMB = [sb(f"EMB{h}", [P, TT, D]) for h in two]
        S0 = [sb(f"S0{h}", [P, C, T]) for h in two]
        S1 = [sb(f"S1{h}", [P, TT, D]) for h in two]
        S2 = [sb(f"S2{h}", [P, TT, D]) for h in two]
        HB = [sb(f"HB{h}", [P, HC, T]) for h in two]
        RT = [sb(f"RT{h}", [P, 2, C, T], F32R) for h in two]
        st6 = [sb(f"st6{h}", [P, TT, 6]) for h in two]
        mv = [sb(f"mv{h}", [P, TT, 2]) for h in two]
        ve = [sb(f"ve{h}", [P, TT]) for h in two]
        rstd = [sb(f"rstd{h}", [P, TT]) for h in two]
        kb = [sb(f"kb{h}", [P, 2, C]) for h in two]
        RTM = [sb(f"RTM{h}", [P, 8, TT, E]) for h in two]
        rix = [sb(f"rix{h}", [P, TT, E], U32) for h in two]
        rbf = [sb(f"rbf{h}", [P, 2, TT, E], BF16) for h in two]

        ONCE = {"act": ("tanh_g", "hbq", "w3_hi", "ew", "gt_hi", "hbg"),
                "dve": ("w3_split", "bb", "g1", "be1", "row_max", "wmax", "ewT", "gt_lo", "gbias"),
                "pe": ("ewT_ps", "gt_ps")}

        def once(ins, name):
            who = next(k for k in ONCE if name in ONCE[k])
            ins.then_inc(sem(f"{who}_once"), 1)

        def after(eng, name):
            who = next(k for k in ONCE if name in ONCE[k])
            eng.wait_ge(sem(f"{who}_once"), ONCE[who].index(name) + 1)

        def col(name, i=0, n=1):
            return colv[:, COLS[name][0] + i:COLS[name][0] + i + n]

        def row(name, n=D):
            return rowv[:, ROWS[name]:ROWS[name] + n]

        def tiles(ap):
            return ap.unsqueeze(1).to_broadcast([P, TT, D])

        def bank(h, k):
            return PS[:, 4 * h + k, :]

        def banks(h, k, n=2):
            return PS[:, 4 * h + k:4 * h + k + n, :]

        def token_banks(h, k):
            return banks(h, k).rearrange("p b (a d) -> p (b a) d", d=D)

        def product(pe, out_, a, b, first=True, last=True):
            pe.matmul(out_, a[1], b[0], start=first, stop=False)
            pe.matmul(out_, a[0], b[1], start=False, stop=False)
            return pe.matmul(out_, a[0], b[0], start=False, stop=last)

        part_a = ExitStack()
        W3 = sb("W3", [P, 2, 3, C, D], F32R, part_a)
        W1 = sb("W1", [P, 2, C, H], F32R, part_a)
        WS1 = sb("WS1", [P, 2, C, FS], F32R, part_a)
        WO = sb("WO", [P, C, D], F32, part_a)
        W2 = sb("W2", [P, HC, D], F32, part_a)
        WS2 = sb("WS2", [P, SC, D], F32, part_a)
        EWT = sb("EWT", [P, TT, T], F32, part_a)
        wmax = sb("wmax", [P, TT], F32, part_a)
        part_m = [ExitStack(), ExitStack()]

        class Moe:
            pass

        moe = [Moe(), Moe()]

        def moe_buffers(m, f):
            w = moe[m]
            st = part_m[m]
            w.fc = f // P
            w.ups = m + 1
            w.cols = C * f * w.ups + w.fc * D
            w.raw = sb(f"raw{m}", [P, w.cols], F32, st)
            w.split = [sb(f"split{m}{i}", [P, 2, w.cols], F32R, st) for i in two]
            w.xg = sb(f"xg{m}", [P, G // P, D], F32, st)
            w.xt = sb(f"xt{m}", [P, 2, C, G], F32R, st)
            w.act = sb(f"act{m}", [P, 2, 2, G], F32, st)
            w.h = sb(f"h{m}", [P, w.fc, G], F32, st)
            w.hs = sb(f"hs{m}", [P, 2, w.fc, G], F32R, st)
            w.y = sb(f"y{m}", [P, G // P, D], F32, st)

        moe_buffers(0, F1)
        part_m[0].close()
        part_a.close()
        part_c = ExitStack()
        VW = sb("VW", [P, 2, C, D], F32R, part_c)
        GT = sb("GT", [P, 2, C, D], F32R, part_c)
        WIH = sb("WIH", [P, 2, C, 3 * D], F32R, part_c)
        WHH = sb("WHH", [P, 2, C, 3 * D], F32R, part_c)
        KK = [sb(f"KK{h}", [P, 2, C, T], F32R, part_c) for h in two]
        HT = [sb(f"HT{h}", [P, C, T], F32, part_c) for h in two]
        HTS = [sb(f"HTS{h}", [P, 2, C, T], F32R, part_c) for h in two]
        VP = [sb(f"VP{h}", [P, TT, D + 4], F32, part_c) for h in two]
        SM = [sb(f"SM{h}", [P, 5, TT], F32, part_c) for h in two]
        gbias = sb("gbias", [P, 3 * C], F32, part_c)
        raw_wih = HB[0][:, 0:3, :].rearrange("p a b -> p (a b)").rearrange("p (c o) -> p c o", c=C)
        raw_wv = HB[0][:, 3, :].rearrange("p (c o) -> p c o", c=C)
        raw_whh = HB[1][:, 0:3, :].rearrange("p a b -> p (a b)").rearrange("p (c o) -> p c o", c=C)
        raw_q = HB[1][:, 3, :].rearrange("p (c o) -> p c o", c=C)
        raw_k = HB[1][:, 4, :].rearrange("p (c o) -> p c o", c=C)
        rows_h = [HB[h][:, 4:8, :].rearrange("p a b -> p (a b)").rearrange("p (k j d) -> p k j d", k=2, d=D) for h in two]

        def gate_slot(h, d, k):
            if d == 0:
                return HB[h][:, 4 + k]
            return (S1[h][:, 0:2].rearrange("p j d -> p (j d)"), S1[h][:, 2:4].rearrange("p j d -> p (j d)"), S0[h][:, 0], S0[h][:, 1])[k]

        part_c.close()
        moe_buffers(1, F2)
        DB = sb("DB", [P, E, D], F32, part_m[1])
        hbg = sb("hbg", [P, E * F2 // P], F32, part_m[1])
        part_m[1].close()

        pairs = [(pair, 2 * pair + h, h) for pair in range(PAIRS) for h in two]
        of_pair = [[(n, h) for p_, n, h in pairs if p_ == pair] for pair in range(PAIRS)]

        slot_steps = [[((pair * ITERS + it) * 2 + h, it, n, h) for n, h in of_pair[pair]] for pair in range(PAIRS) for it in range(ITERS)]

        def slot_count(n, it):
            return n // 2 * 2 * (ITERS + 1) + 2 * it + n % 2 + 1

        def slot_lo_count(n, it):
            return n // 2 * 2 * ITERS + 2 * it + n % 2 + 1

        slot_hi_count = slot_lo_count

        def up_weights(m, w, u, c, f):
            at = (u * C + c) * w.fc * P + f * P
            return slice(at, at + P)

        def down_weights(m, w, f):
            at = w.ups * C * w.fc * P + f * D
            return slice(at, at + D)

        def expert_sources(m, e):
            srcs = (m1_w1, m1_w2) if m == 0 else (gate_w, up_w, down_w)
            at = 0
            for src in srcs:
                ap = src[e].rearrange("(c p) o -> p c o", p=P)
                n = ap.shape[1] * ap.shape[2]
                yield ap, at, n
                at += n

        def bounds(eng, m, e):
            return (eng.value_load(table[m][0:1, e:e + 1], min_val=0, max_val=NG - 1),
                    eng.value_load(table[m][0:1, E + e:E + e + 1], min_val=1, max_val=NG))

        def counted(eng, m):
            eng.wait_ge(sem(f"m{m}_table"), 1)

        def moe_end(eng, m, total):
            for name, value in (("xg", 16 * (total + 2)), ("turned", total + 1), ("xhi", total + 1), ("xlo", total + 1),
                                ("down", total), ("y", total + 1), ("yout", 16 * total + 1)):
                eng.wait_ge(sem(f"m{m}_{name}"), value)
                eng.sem_inc(sem("passed"), 1)

        def moe_sp(sp, m):
            w = moe[m]

            def raw_in(e):
                if e:
                    sp.wait_ge(sem(f"m{m}_lo"), e)
                for ap, at, n in expert_sources(m, e):
                    sp.dma_start(w.raw[:, at:at + n].rearrange("p (c o) -> p c o", c=ap.shape[1]), ap).then_inc(sem(f"m{m}_raw"), 16)

            def rows_of(src, t):
                r = sp.value_load(table[m][0:1, bass.ds(t + 2 * E, 1)], min_val=0, max_val=XROWS - G)
                return src[bass.ds(r, G), :].rearrange("(a p) d -> p a d", p=P)

            def group_in(t):
                sp.dma_start(w.xg[:], rows_of(routed[m], t)).then_inc(sem(f"m{m}_xg"), 16)

            raw_in(0)
            sp.wait_ge(sem(f"m{m}_table"), 1)
            for h in two:
                sp.wait_ge(sem(f"scattered{h}"), 16 * 2 * TT * PAIRS * (m + 1))
            group_in(0)
            sp.wait_ge(sem(f"m{m}_turned"), 1)
            group_in(1)
            for e in range(E):
                if e + 1 < E:
                    raw_in(e + 1)
                lo, hi = bounds(sp, m, e)
                with sp.Fori(lo, hi) as t:
                    counted(sp, m)
                    sp.wait_ge(sem(f"m{m}_turned"), t + 2)
                    group_in(t + 2)
                    counted(sp, m)
                    sp.wait_ge(sem(f"m{m}_y"), t + 2)
                    sp.dma_start(rows_of(routed[m], t), w.y[:]).then_inc(sem(f"m{m}_yout"), 16)
            moe_end(sp, m, hi)

        def moe_pool(pool, m):
            w = moe[m]
            for e in range(E):
                if e >= 2:
                    done = pool.value_load(table[m][0:1, e - 1:e], min_val=1, max_val=NG - 1)
                    counted(pool, m)
                    pool.wait_ge(sem(f"m{m}_down"), done)
                for ap, at, n in expert_sources(m, e):
                    pool.dma_start(w.split[e % 2][:, 0, at:at + n].rearrange("p (c o) -> p c o", c=ap.shape[1]), ap).then_inc(sem(f"m{m}_hi"), 16)
                k = len(list(expert_sources(m, e)))
                pool.wait_ge(sem(f"m{m}_hi"), 16 * k * (e + 1))
                pool.wait_ge(sem(f"m{m}_raw"), 16 * k * (e + 1))
                pool.tensor_tensor(w.split[e % 2][:, 1], w.raw[:], w.split[e % 2][:, 0].bitcast(F32), ALU.subtract).then_inc(sem(f"m{m}_lo"), 1)

        def moe_act(act, m):
            w = moe[m]

            def x_hi(n):
                act.wait_ge(sem(f"m{m}_turned"), n)
                act.activation(w.xt[:, 0], PS[:, 4, :].rearrange("p (c g) -> p c g", c=C), ACT.Copy).then_inc(sem(f"m{m}_xhi"), 1)

            x_hi(1)
            for e in range(E):
                lo, hi = bounds(act, m, e)
                with act.Fori(lo, hi) as t:
                    for f in range(w.fc):
                        act.wait_ge(sem(f"m{m}_up"), t * w.fc + f + 1)
                        if m == 0:
                            act.activation(w.act[:, f % 2, 0], PS[:, f, 0:G], ACT.Relu).then_inc(sem(f"m{m}_act"), 1)
                        else:
                            b = e * w.fc + f
                            act.activation(w.act[:, f % 2, 0], PS[:, f, 0:G], ACT.Tanh, bias=hbg[:, b:b + 1], scale=0.5)
                            act.activation(w.act[:, f % 2, 1], PS[:, f, 0:G], ACT.Identity, bias=hbg[:, b:b + 1], scale=0.5).then_inc(sem(f"m{m}_act"), 1)
                        if f:
                            act.wait_ge(sem(f"m{m}_h"), t * w.fc + f)
                            act.activation(w.hs[:, 0, f - 1], w.h[:, f - 1], ACT.Copy).then_inc(sem(f"m{m}_hhi"), 1)
                    act.wait_ge(sem(f"m{m}_h"), t * w.fc + w.fc)
                    act.activation(w.hs[:, 0, w.fc - 1], w.h[:, w.fc - 1], ACT.Copy).then_inc(sem(f"m{m}_hhi"), 1)
                    x_hi(t + 2)
            if m == 0:
                moe_end(act, m, hi)

        def moe_dve(dve, m):
            w = moe[m]

            def x_lo(n):
                dve.wait_ge(sem(f"m{m}_xhi"), n)
                dve.tensor_tensor(w.xt[:, 1], PS[:, 4, :].rearrange("p (c g) -> p c g", c=C), w.xt[:, 0].bitcast(F32),
                                  ALU.subtract).then_inc(sem(f"m{m}_xlo"), 1)

            x_lo(1)
            for e in range(E):
                lo, hi = bounds(dve, m, e)
                with dve.Fori(lo, hi) as t:
                    for f in range(w.fc):
                        dve.wait_ge(sem(f"m{m}_act"), t * w.fc + f + 1)
                        a = w.act[:, f % 2]
                        if m == 0:
                            dve.scalar_tensor_tensor(out=w.h[:, f], in0=PS[:, f, 0:G], scalar=0.0, in1=a[:, 0],
                                                     op0=ALU.max, op1=ALU.mult).then_inc(sem(f"m{m}_h"), 1)
                        else:
                            dve.scalar_tensor_tensor(out=a[:, 0], in0=a[:, 0], scalar=1.0, in1=a[:, 1],
                                                     op0=ALU.add, op1=ALU.mult).then_inc(sem(f"m{m}_silu"), 1)
                            dve.wait_ge(sem(f"m{m}_silu"), t * w.fc + f + 1)
                            dve.scalar_tensor_tensor(out=w.h[:, f], in0=PS[:, f, G:2 * G], scalar=col("up_b", e * w.fc + f),
                                                     in1=a[:, 0], op0=ALU.add, op1=ALU.mult).then_inc(sem(f"m{m}_h"), 1)
                        if f:
                            dve.wait_ge(sem(f"m{m}_hhi"), t * w.fc + f)
                            dve.tensor_tensor(w.hs[:, 1, f - 1], w.h[:, f - 1], w.hs[:, 0, f - 1].bitcast(F32), ALU.subtract).then_inc(sem(f"m{m}_hlo"), 1)
                    dve.wait_ge(sem(f"m{m}_hhi"), t * w.fc + w.fc)
                    dve.tensor_tensor(w.hs[:, 1, w.fc - 1], w.h[:, w.fc - 1], w.hs[:, 0, w.fc - 1].bitcast(F32), ALU.subtract).then_inc(sem(f"m{m}_hlo"), 1)
                    x_lo(t + 2)
                    dve.wait_ge(sem(f"m{m}_down"), t + 1)
                    dve.wait_ge(sem(f"m{m}_yout"), 16 * t + 1)
                    if m == 0:
                        dve.tensor_copy(w.y[:], PS[:, 5:7, 0:D]).then_inc(sem(f"m{m}_y"), 1)
                    else:
                        dve.tensor_tensor(w.y[:], PS[:, 5:7, 0:D], DB[:, e].unsqueeze(1).to_broadcast([P, G // P, D]),
                                          ALU.add).then_inc(sem(f"m{m}_y"), 1)
            moe_end(dve, m, hi)

        def moe_pe(pe, m):
            w = moe[m]

            def turn_rows(n):
                pe.wait_ge(sem(f"m{m}_xg"), 16 * n)
                for c in range(C):
                    for a in range(G // P):
                        ins = pe.transpose(PS[:, 4, c * G + a * P:c * G + (a + 1) * P], w.xg[:, a, c * P:(c + 1) * P], ident[:])
                ins.then_inc(sem(f"m{m}_turned"), 1)

            turn_rows(1)
            for e in range(E):
                s = w.split[e % 2]
                pe.wait_ge(sem(f"m{m}_lo"), e + 1)
                lo, hi = bounds(pe, m, e)
                with pe.Fori(lo, hi) as t:
                    pe.wait_ge(sem(f"m{m}_xlo"), t + 1)
                    for f in range(w.fc):
                        for u in range(w.ups):
                            for c in range(C):
                                at = up_weights(m, w, u, c, f)
                                ins = product(pe, PS[:, f, u * G:(u + 1) * G], (s[:, 0, at], s[:, 1, at]),
                                              (w.xt[:, 0, c], w.xt[:, 1, c]), c == 0, c == C - 1)
                        ins.then_inc(sem(f"m{m}_up"), 1)
                    turn_rows(t + 2)
                    pe.wait_ge(sem(f"m{m}_y"), t + 1)
                    for f in range(w.fc):
                        pe.wait_ge(sem(f"m{m}_hlo"), t * w.fc + f + 1)
                        at = down_weights(m, w, f)
                        for a in range(G // P):
                            tok = slice(a * P, (a + 1) * P)
                            ins = product(pe, PS[:, 5 + a, 0:D], (w.hs[:, 0, f, tok], w.hs[:, 1, f, tok]), (s[:, 0, at], s[:, 1, at]),
                                          f == 0, f == w.fc - 1)
                    ins.then_inc(sem(f"m{m}_down"), 1)
            if m == 0:
                moe_end(pe, m, hi)

        tf = HB[0][0:1, 4:8, :].rearrange("p a (b k) -> p (a b) k", k=32 * E)

        def table_pe(pe, m):
            pe.wait_ge(sem("total"), m + 1)
            pe.matmul(PS[:, 7, 0:E], ones_bf[:], rbf[0][:, 0, 0], start=True, stop=True).then_inc(sem("count_ps"), 1)

        def table_dve(dve, m, step, chained):
            step(dve.tensor_copy(rbf[0][:, 0, 0], carry[:, 0]))
            chained()
            step(dve.memset(carry[:, 0], 0.0))
            dve.memset(tf[:, 7], 0.0).then_inc(sem("total"), 1)
            dve.wait_ge(sem("count_ps"), m + 1)
            step(dve.tensor_scalar(tfi[:, 0], PS[0:1, 7, 0:E], float(G - 1), None, ALU.add))
            chained()
            step(dve.tensor_scalar(tfi[:, 1], tfi[:, 0], G.bit_length() - 1, None, ALU.logical_shift_right))
            chained()
            step(dve.tensor_copy(tf[:, 0, 0:E], tfi[:, 1]))
            chained()
            step(dve.tensor_scalar(tf[:, 1, 0:E], tf[:, 0, 0:E], 1.0, None, ALU.max))
            chained()
            step(dve.tensor_copy(tf[:, 2, 0:1], tf[:, 1, 0:1]))
            for e in range(1, E):
                chained()
                step(dve.tensor_tensor(tf[:, 2, e:e + 1], tf[:, 2, e - 1:e], tf[:, 1, e:e + 1], ALU.add))
            chained()
            step(dve.tensor_tensor(tf[:, 3, 0:E], tf[:, 2, 0:E], tf[:, 1, 0:E], ALU.subtract))
            shape = [1, 32, E]
            past = tf[:, 4].rearrange("p (t e) -> p t e", e=E)
            step(dve.tensor_tensor(past, iota_g[0:1].unsqueeze(2).to_broadcast(shape), tf[:, 2, 0:E].unsqueeze(1).to_broadcast(shape), ALU.is_ge))
            chained()
            step(dve.tensor_reduce(tf[:, 5, 0:32], past, AX, ALU.add))
            step(dve.tensor_tensor(tf[:, 6].rearrange("p (t e) -> p t e", e=E), past, tf[:, 1, 0:E].unsqueeze(1).to_broadcast(shape), ALU.mult))
            chained()
            step(dve.tensor_reduce(tf[:, 5, 32:64], tf[:, 6].rearrange("p (t e) -> p t e", e=E), AX, ALU.add))
            chained()
            step(dve.tensor_tensor(tf[:, 5, 64:96], iota_g[0:1], tf[:, 5, 32:64], ALU.subtract))
            step(dve.tensor_scalar(tf[:, 5, 0:32], tf[:, 5, 0:32], float(CAP), None, ALU.mult))
            chained()
            step(dve.scalar_tensor_tensor(out=tf[:, 5, 96:128], in0=tf[:, 5, 64:96], scalar=float(G), in1=tf[:, 5, 0:32], op0=ALU.mult, op1=ALU.add))
            chained()
            step(dve.tensor_copy(table[m][:, 0:E], tf[:, 3, 0:E]))
            step(dve.tensor_copy(table[m][:, E:2 * E], tf[:, 2, 0:E]))
            dve.tensor_copy(table[m][:, 2 * E:2 * E + 32], tf[:, 5, 96:128]).then_inc(sem(f"m{m}_table"), 1)

        block = top.enter_context(nc.Block())

        @block.sync
        def _(sp):
            sp.dma_start(rowv[:], rows.partition_broadcast(P)).then_inc(sem("const_in"), 16)
            sp.dma_start(colv[:], cols).then_inc(sem("const_in"), 16)

            def load_batch(n, h):
                if n >= 2:
                    sp.wait_ge(sem("batch_a"), n - 1)
                    sp.wait_ge(sem(f"x_out{h}"), 16 * (n // 2))
                sp.dma_start(X[h][:], x[n].rearrange("(j p) d -> p j d", p=P)).then_inc(sem(f"x_in{h}"), 16)
                sp.dma_start(S0[h][:].rearrange("p c t -> p (c t)").rearrange("p (j d) -> p j d", d=D),
                             ctx_in[n].rearrange("(j p) d -> p j d", p=P)).then_inc(sem(f"x_in{h}"), 16)

            load_batch(0, 0)
            for k, src in enumerate((wq, wk, wv)):
                sp.dma_start(HB[1][:, k].rearrange("p (c o) -> p c o", c=C), src.rearrange("(c p) o -> p c o", p=P)).then_inc(sem("w3_in"), 16)
            load_batch(1, 1)
            sp.dma_start(HB[0][:, 0:TT, :], pos_bias.rearrange("(i p) j -> p i j", p=P)).then_inc(sem("pb_in"), 16)
            sp.dma_start(HB[1][:, 3:7, :].rearrange("p a b -> p (a b)").rearrange("p (c o) -> p c o", c=C), w1.rearrange("(c p) o -> p c o", p=P)).then_inc(sem("w1_in"), 16)
            sp.dma_start(S2[0][:].rearrange("p j d -> p (j d)").rearrange("p (c o) -> p c o", c=C), ws1.rearrange("(c p) o -> p c o", p=P)).then_inc(sem("w1_in"), 16)
            sp.dma_start(HB[1][:, 7, 0:C * E].rearrange("p (c o) -> p c o", c=C), router1.rearrange("(c p) o -> p c o", p=P)).then_inc(sem("w1_in"), 16)
            sp.dma_start(HB[1][:, 7, C * E:2 * C * E].rearrange("p (c o) -> p c o", c=C), router2.rearrange("(c p) o -> p c o", p=P)).then_inc(sem("w1_in"), 16)
            sp.dma_start(WO[:], wo.rearrange("(c p) o -> p c o", p=P)).then_inc(sem("wplain_in"), 16)
            sp.dma_start(W2[:], w2.rearrange("(c p) o -> p c o", p=P)).then_inc(sem("wplain_in"), 16)
            sp.dma_start(WS2[:], ws2.rearrange("(c p) o -> p c o", p=P)).then_inc(sem("wplain_in"), 16)
            sp.wait_ge(sem("pool_c"), 1)

            def fill(m):
                for part in routed[m].rearrange("(k p r) d -> k p (r d)", k=4, p=P):
                    sp.dma_start(part.rearrange("p (r d) -> p r d", d=4 * D),
                                 zeros[:].unsqueeze(1).to_broadcast([P, XROWS // 4 // P // 4, 4 * D])).then_inc(sem(f"filled{m}"), 16)

            fill(0)
            for pair in range(PAIRS):
                if pair:
                    for n, h in of_pair[pair]:
                        load_batch(n, h)
                    fill(1)
                for n, h in of_pair[pair]:
                    sp.wait_ge(sem("batch_a"), n + 1)
                    sp.dma_start(x_base[0, n].rearrange("(j p) d -> p j d", p=P), X[h][:]).then_inc(sem(f"x_out{h}"), 16)
            for h in two:
                sp.wait_ge(sem(f"x_out{h}"), 16 * PAIRS)
            for dst, src in ((raw_wv, Wv), (raw_q, Wq), (raw_k, Wk), (raw_wih, wih), (raw_whh, whh)):
                sp.dma_start(dst, src.rearrange("(c p) o -> p c o", p=P)).then_inc(sem("cw_raw"), 16)
            moe_sp(sp, 0)
            for pair in range(PAIRS):
                for n, h in of_pair[pair]:
                    if pair:
                        sp.wait_ge(sem("batch_c"), n - 1)
                        sp.wait_ge(sem(f"x_out{h}"), 16 * (PAIRS + pair))
                        sp.wait_ge(sem("dest"), B + n - 1)
                    sp.dma_start(X[h][:], x_base[0, n].rearrange("(j p) d -> p j d", p=P)).then_inc(sem(f"x_in{h}"), 16)
                    sp.dma_start(S0[h][:].rearrange("p c t -> p (c t)").rearrange("p (j d) -> p j d", d=D),
                                 ctx_in[n].rearrange("(j p) d -> p j d", p=P)).then_inc(sem(f"x_in{h}"), 16)
                for n, h in of_pair[pair]:
                    sp.wait_ge(sem("batch_c"), n + 1)
                    sp.dma_start(x_base[1, n].rearrange("(j p) d -> p j d", p=P), X[h][:]).then_inc(sem(f"x_out{h}"), 16)
            for h in two:
                sp.wait_ge(sem(f"x_out{h}"), 16 * 2 * PAIRS)
            sp.wait_ge(sem("dest"), 2 * B)
            sp.dma_start(DB[:], down_b.rearrange("e d -> (e d)").partition_broadcast(P).rearrange("p (e d) -> p e d", d=D)).then_inc(sem("db_in"), 16)
            moe_sp(sp, 1)
            for pair in range(PAIRS):
                for n, h in of_pair[pair]:
                    if pair:
                        sp.wait_ge(sem(f"x_out{h}"), 16 * (2 * PAIRS + pair))
                    sp.dma_start(X[h][:], x_base[1, n].rearrange("(j p) d -> p j d", p=P)).then_inc(sem(f"x_in{h}"), 16)
                for n, h in of_pair[pair]:
                    sp.wait_ge(sem("combined"), B + n + 1)
                    sp.dma_start(out[n].rearrange("(j p) d -> p j d", p=P), X[h][:]).then_inc(sem(f"x_out{h}"), 16)
            for h in two:
                sp.wait_ge(sem(f"x_out{h}"), 16 * 3 * PAIRS)

        @block.gpsimd
        def _(pool):
            pool.memset(zeros[:], 0.0).then_inc(sem("pool_c"), 1)
            pool.memset(ident[:], 0.0).then_inc(sem("pool_c"), 1)
            pool.memset(ones[:], 1.0).then_inc(sem("pool_c"), 1)
            pool.memset(minus_half[:], -0.5).then_inc(sem("pool_c"), 1)
            pool.memset(ones_bf[:], 1.0).then_inc(sem("pool_c"), 1)
            pool.memset(carry[:], 0.0).then_inc(sem("pool_c"), 1)
            pool.iota(iota_e[:], pattern=[[1, E]], base=0, channel_multiplier=0, allow_small_or_imprecise_dtypes=True).then_inc(sem("pool_c"), 1)
            pool.iota(ebase[:], pattern=[[CAP, E]], base=0, channel_multiplier=0, allow_small_or_imprecise_dtypes=True).then_inc(sem("pool_c"), 1)
            pool.iota(iota_g[:], pattern=[[1, 32]], base=0, channel_multiplier=0, allow_small_or_imprecise_dtypes=True).then_inc(sem("pool_c"), 1)
            pool.wait_ge(sem("pool_c"), 9)
            pool.affine_select(out=ident[:], in_=ident[:], compare_op=ALU.not_equal, fill=1.0, base=0,
                               pattern=[[-1, P]], channel_multiplier=1).then_inc(sem("pool_c"), 1)
            pool.affine_select(out=tri[:], in_=ones_bf[:], compare_op=ALU.is_gt, fill=0.0, base=0,
                               pattern=[[1, P]], channel_multiplier=-1).then_inc(sem("pool_c"), 1)
            pool.wait_ge(sem("pool_c"), 11)

            ln = [0]

            def power(h):
                ln[0] += 1
                pool.wait_ge(sem("var_ready"), ln[0])
                pool.tensor_tensor(rstd[h][:], ve[h][:], minus_half[:], ALU.pow).then_inc(sem("rstd_ready"), 1)

            def scatter(m, n, h):
                pool.wait_ge(sem("dest"), m * B + n + 1)
                for j in range(TT):
                    for kk in range(2):
                        pool.indirect_dma_start(out=routed[m], out_offset=bass.IndirectOffsetOnAxis(ap=dest[m][:, n, j, kk:kk + 1], axis=0),
                                                in_=S2[h][:, j], in_offset=None).then_inc(sem(f"scattered{h}"), 16)

            for n, h in of_pair[0]:
                power(h)
            pool.wait_ge(sem("pb_in"), 16)
            band = HB[0][:, 0:TT, :]
            pool.affine_select(out=band, in_=band, compare_op=ALU.is_gt, fill=0.0, base=BAND,
                               pattern=[[-P, TT], [1, T]], channel_multiplier=-1).then_inc(sem("pool_c"), 1)
            pool.wait_ge(sem("pool_c"), 12)
            pool.affine_select(out=band, in_=band, compare_op=ALU.is_gt, fill=0.0, base=BAND,
                               pattern=[[P, TT], [-1, T]], channel_multiplier=1).then_inc(sem("pool_c"), 1)
            pool.wait_ge(sem("w1_in"), 64)
            raw_w1 = HB[1][:, 3:7, :].rearrange("p a b -> p (a b)").rearrange("p (c o) -> p c o", c=C)
            raw_ws1 = S2[0][:].rearrange("p j d -> p (j d)").rearrange("p (c o) -> p c o", c=C)
            raw_r = [HB[1][:, 7, m * C * E:(m + 1) * C * E].rearrange("p (c o) -> p c o", c=C) for m in two]
            split = [(raw_r[0], rw[0][:], rw[1][:]), (raw_r[1], rw[2][:], rw[3][:]),
                     (raw_w1, W1[:, 0], W1[:, 1]), (raw_ws1, WS1[:, 0], WS1[:, 1])]
            for raw, hi, lo in split:
                pool.tensor_copy(hi, raw).then_inc(sem("pool_c"), 1)
            for k, (raw, hi, lo) in enumerate(split):
                pool.wait_ge(sem("pool_c"), 13 + k + 1)
                pool.tensor_tensor(lo, raw, hi.bitcast(F32), ALU.subtract).then_inc(sem("w1_split"), 1)

            for pair in range(PAIRS):
                if pair:
                    for n, h in of_pair[pair]:
                        power(h)
                for n, h in of_pair[pair]:
                    pool.wait_ge(sem("inT_ps"), n + 1)
                    pool.tensor_tensor(EMB[h][:], EMB[h][:], tiles(row("bo")), ALU.add).then_inc(sem("embo"), 1)
                for n, h in of_pair[pair]:
                    power(h)
                for n, h in of_pair[pair]:
                    pool.wait_ge(sem("r_norm"), n + 1)
                    if n == 0:
                        after(pool, "be1")
                    pool.tensor_tensor(S1[h][:], S2[h][:], tiles(row("gamma")), ALU.mult).then_inc(sem("atok"), 1)
                    pool.wait_ge(sem("atok"), 2 * n + 1)
                    pool.tensor_tensor(S1[h][:], S1[h][:], tiles(bb[:]), ALU.add).then_inc(sem("atok"), 1)
                for n, h in of_pair[pair]:
                    pool.wait_ge(sem("aT_hi"), n + 1)
                    pool.tensor_tensor(RT[h][:, 1], S0[h][:], RT[h][:, 0].bitcast(F32), ALU.subtract).then_inc(sem("aT_lo"), 1)
                    pool.tensor_tensor(X[h][:], X[h][:], tiles(be1[:]), ALU.add).then_inc(sem("xbeta"), 1)
                for n, h in of_pair[pair]:
                    power(h)
                    power(h)
                for n, h in of_pair[pair]:
                    for f in range(SC):
                        pool.wait_ge(sem("sh_relu"), SC * n + f + 1)
                        pool.tensor_tensor(HB[h][:, f], HB[h][:, f], HB[h][:, f], ALU.mult).then_inc(sem("sh_sq"), 1)
                for n, h in of_pair[pair]:
                    if n == 0:
                        pool.wait_ge(sem("filled0"), 64)
                    scatter(0, n, h)
            pool.wait_ge(sem("m0_table"), 1)
            pool.wait_ge(sem("batch_a"), B)
            for dst, src in ((VW, Wv), (WIH, wih), (WHH, whh)):
                pool.dma_start(dst[:, 0], src.rearrange("(c p) o -> p c o", p=P)).then_inc(sem("cw_hi"), 16)
            moe_pool(pool, 0)

            def gather(m, n, h):
                for j in range(TT):
                    for kk in range(2):
                        pool.indirect_dma_start(out=rows_h[h][:, kk, j], out_offset=None, in_=routed[m],
                                                in_offset=bass.IndirectOffsetOnAxis(ap=dest[m][:, n, j, kk:kk + 1], axis=0))\
                            .then_inc(sem(f"rows{h}"), 16)

            def all_stored(m):
                total = pool.value_load(table[m][0:1, 2 * E - 1:2 * E], min_val=1, max_val=NG)
                moe_end(pool, m, total)

            pool.wait_ge(sem("cw_hi"), 48)
            pool.wait_ge(sem("cw_raw"), 80)
            pool.tensor_tensor(VW[:, 1], raw_wv, VW[:, 0].bitcast(F32), ALU.subtract).then_inc(sem("cw_lo"), 1)
            all_stored(0)
            for pair in range(PAIRS):
                for n, h in of_pair[pair]:
                    if n == 1:
                        after(pool, "gt_ps")
                    if pair:
                        pool.wait_ge(sem("batch_c"), n - 1)
                    gather(0, n, h)
                    power(h)
                    power(h)
                if pair == 0:
                    pool.tensor_tensor(WIH[:, 1], raw_wih, WIH[:, 0].bitcast(F32), ALU.subtract).then_inc(sem("cw_lo"), 1)
                    pool.tensor_tensor(WHH[:, 1], raw_whh, WHH[:, 0].bitcast(F32), ALU.subtract).then_inc(sem("cw_lo"), 1)
                for steps in slot_steps[pair * ITERS:(pair + 1) * ITERS]:
                    for q, it, n, h in steps:
                        power(h)
                    for q, it, n, h in steps:
                        for d in range(C):
                            pool.wait_ge(sem("n_gate"), C * q + d + 1)
                            pool.tensor_tensor(gate_slot(h, d, 0), HT[h][:, d], gate_slot(h, d, 3), ALU.subtract).then_inc(sem("h_minus_n"), 1)
                for n, h in of_pair[pair]:
                    power(h)
                for n, h in of_pair[pair]:
                    if n == 0:
                        pool.wait_ge(sem("filled1"), 64)
                    scatter(1, n, h)
            pool.wait_ge(sem("m1_table"), 1)
            moe_pool(pool, 1)
            all_stored(1)
            for pair in range(PAIRS):
                for n, h in of_pair[pair]:
                    if pair:
                        pool.wait_ge(sem("combined"), B + n - 1)
                    gather(1, n, h)

        @block.scalar
        def _(act):
            for m in two:
                act.sem_inc(sem(f"m{m}_y"), 1)
                act.sem_inc(sem(f"m{m}_yout"), 1)
            act.wait_ge(sem("const_in"), 32)
            once(act.activation(tanh_g[:], rowv[:, ROWS["g"]:ROWS["g"] + 4], ACT.Tanh), "tanh_g")
            once(act.activation(hbq[:], col("bq", 0, C), ACT.Copy, scale=0.5), "hbq")
            act.wait_ge(sem("w3_in"), 48)
            raw = HB[1][:, 0:3, :]
            once(act.activation(W3[:, 0].rearrange("p w c o -> p w (c o)"), raw, ACT.Copy), "w3_hi")

            def route(m, pair):
                for n, h in of_pair[pair]:
                    act.wait_ge(sem("xnT_ps"), m * B + n + 1)
                    act.activation(RT[h][:, 0], banks(h, 2), ACT.Copy).then_inc(sem("xnT_hi"), 1)
                for n, h in of_pair[pair]:
                    act.wait_ge(sem("rt_sub"), m * B + n + 1)
                    act.activation(RTM[h][:, 1], RTM[h][:, 0], ACT.Exp).then_inc(sem("rt_exp"), 1)

            for pair in range(PAIRS):
                for n, h in of_pair[pair]:
                    act.wait_ge(sem("inT_ps"), n + 1)
                    act.activation(RT[h][:, 0], banks(h, 0), ACT.Copy).then_inc(sem("inT_hi"), 1)
                for n, h in of_pair[pair]:
                    if n == 0:
                        after(act, "wmax")
                        for i in range(TT):
                            ins = act.activation(HB[0][:, i], HB[0][:, i], ACT.Exp, bias=wmax[:, i:i + 1])
                        once(ins, "ew")
                        after(act, "hbq")
                    if n == 0:
                        after(act, "ewT_ps")
                    if n == 1:
                        act.wait_ge(sem("w1_split"), 4)
                    act.wait_ge(sem("qk_ps"), 2 * n + 1)
                    for c in range(C):
                        ins = act.activation(HB[h][:, 6 + c], bank(h, c), ACT.Tanh, bias=hbq[:, c:c + 1], scale=0.5)
                    ins.then_inc(sem("th"), 1)
                    act.wait_ge(sem("kbias"), n + 1)
                    for c in range(C):
                        ins = act.activation(S0[h][:, c], bank(h, 2 + c), ACT.Exp, bias=kb[h][:, 1, c:c + 1])
                    ins.then_inc(sem("ekT"), 1)
                for n, h in of_pair[pair]:
                    act.wait_ge(sem("ek_ps"), n + 1)
                    act.activation(HB[h][:, 0:2], banks(h, 2), ACT.Copy).then_inc(sem("ek"), 1)
                for n, h in of_pair[pair]:
                    act.wait_ge(sem("aT_ps"), n + 1)
                    for c in range(C):
                        ins = act.activation(S0[h][:, c], bank(h, 2 + c), ACT.Identity, bias=col("beta", c), scale=col("gamma", c))
                    ins.then_inc(sem("aT"), 1)
                for n, h in of_pair[pair]:
                    for m in range(0, HC, 2):
                        act.wait_ge(sem("hid_ps"), HC * n + m + 1)
                        act.activation(HB[h][:, m], bank(h, m % 4), ACT.Relu, bias=col("b1", m)).then_inc(sem("hid_act"), 1)
                route(0, pair)
                for n, h in of_pair[pair]:
                    for f in range(SC):
                        act.wait_ge(sem("sh_ps"), SC * n + f + 1)
                        act.activation(HB[h][:, f], bank(h, 2 + f % 2), ACT.Relu).then_inc(sem("sh_relu"), 1)

            act.wait_ge(sem("m0_table"), 1)
            moe_act(act, 0)

            after(act, "gt_ps")
            once(act.activation(GT[:, 0], PS[:, 7, :].rearrange("p (c o) -> p c o", c=C), ACT.Copy), "gt_hi")
            for pair in range(PAIRS):
                for n, h in of_pair[pair]:
                    act.wait_ge(sem("inT_ps"), B + n + 1)
                    for c in range(C):
                        act.activation(S0[h][:, c], bank(h, c), ACT.Copy, scale=col("w_in", c))
                        ins = act.activation(RT[h][:, 0, c], bank(h, c), ACT.Copy, scale=col("w_in", c))
                    ins.then_inc(sem("inT_hi"), 1)
                    act.wait_ge(sem("aT_ps"), B + n + 1)
                    act.activation(HT[h][:], banks(h, 2), ACT.Copy).then_inc(sem("slot_new"), 1)
                    act.activation(HTS[h][:, 0], banks(h, 2), ACT.Copy).then_inc(sem("slot_hi"), 1)
                for n, h in of_pair[pair]:
                    act.wait_ge(sem("kk_ps"), n + 1)
                    act.wait_ge(sem("inT_lo"), B + n + 1)
                    for c in range(C):
                        act.activation(S0[h][:, c], bank(h, c), ACT.Copy, scale=col("w_slot", c))
                        ins = act.activation(KK[h][:, 0, c], bank(h, c), ACT.Copy, scale=col("w_slot", c))
                    ins.then_inc(sem("kk_hi"), 1)
                    act.wait_ge(sem("v_ps"), B + n + 1)
                    act.activation(EMB[h][:], token_banks(h, 2), ACT.Copy).then_inc(sem("v_out"), 1)
                for steps in slot_steps[pair * ITERS:(pair + 1) * ITERS]:
                    for q, it, n, h in steps:
                        if it == 0:
                            act.wait_ge(sem("kk_lo"), n + 1)
                            act.wait_ge(sem("slot_new"), slot_count(n, it))
                        else:
                            act.wait_ge(sem("slot_new"), slot_count(n, it))
                        act.activation(S0[h][:], HT[h][:], ACT.Square).then_inc(sem("slot_sq"), 1)
                    for q, it, n, h in steps:
                        act.wait_ge(sem("sn"), q + 1)
                        act.activation(RT[h][:, 0], S0[h][:], ACT.Copy).then_inc(sem("sn_hi"), 1)
                    for q, it, n, h in steps:
                        if q == 0:
                            act.wait_ge(sem("cw_lo"), 3)
                        for j in range(TT):
                            act.wait_ge(sem("smax"), TT * q + j + 1)
                            act.activation(HB[h][:, j], bank(h, j), ACT.Exp, bias=SM[h][:, 1, j:j + 1], scale=1.0 / 16,
                                           accum_out=SM[h][:, 2, j:j + 1]).then_inc(sem("sexp"), 1)
                    for q, it, n, h in steps:
                        act.wait_ge(sem("uT_ps"), q + 1)
                        act.activation(RT[h][:, 0], banks(h, 0), ACT.Copy).then_inc(sem("uT_hi"), 1)
                    for q, it, n, h in steps:
                        for d in range(C):
                            g = 4 * (C * q + d)
                            act.wait_ge(sem("gru_ps"), g + 1)
                            act.activation(gate_slot(h, d, 1), bank(h, 0), ACT.Identity, bias=gbias[:, 4 + d:5 + d], scale=0.5).then_inc(sem("hn_out"), 1)
                            act.wait_ge(sem("gru_ps"), g + 2)
                            act.activation(gate_slot(h, d, 0), bank(h, 2), ACT.Tanh, bias=gbias[:, d:d + 1], scale=0.5).then_inc(sem("r_out"), 1)
                            act.wait_ge(sem("gru_ps"), g + 4)
                            act.activation(gate_slot(h, d, 2), bank(h, 3), ACT.Tanh, bias=gbias[:, 2 + d:3 + d], scale=0.5).then_inc(sem("z_out"), 1)
                            act.wait_ge(sem("xn_out"), C * q + d + 1)
                            act.activation(gate_slot(h, d, 3), gate_slot(h, d, 3), ACT.Tanh, bias=col("bih", 4 + d)).then_inc(sem("n_gate"), 1)
                    if steps[0][1] < ITERS - 1:
                        for q, it, n, h in steps:
                            act.wait_ge(sem("slot_new"), slot_count(n, it + 1))
                            act.activation(HTS[h][:, 0], HT[h][:], ACT.Copy).then_inc(sem("slot_hi"), 1)
                route(1, pair)
            act.wait_ge(sem("m1_table"), 1)
            once(act.activation(hbg[:], col("gate_b", 0, E * F2 // P), ACT.Copy, scale=0.5), "hbg")
            after(act, "hbg")
            moe_act(act, 1)

        @block.vector
        def _(dve):
            k = [0]

            def step(ins):
                k[0] += 1
                ins.then_inc(sem("dve_step"), 1)

            def chained():
                dve.wait_ge(sem("dve_step"), k[0])

            ln = [0]

            def normalise(h, src, dst, eps, final):
                for j in range(TT):
                    ins = dve.bn_stats(st6[h][:, j], src[:, j])
                step(ins)
                chained()
                for j in range(TT):
                    ins = dve.bn_aggr(mv[h][:, j], st6[h][:, j])
                step(ins)
                chained()
                dve.tensor_scalar(ve[h][:], mv[h][:, :, 1], eps, None, ALU.add).then_inc(sem("var_ready"), 1)
                ln[0] += 1
                dve.wait_ge(sem("rstd_ready"), ln[0])
                for j in range(TT):
                    ins = dve.tensor_scalar(dst[:, j], src[:, j], mv[h][:, j, 0:1], rstd[h][:, j:j + 1], ALU.subtract, ALU.mult)
                final(ins)

            def lo_part(h, ps, name):
                dve.tensor_tensor(RT[h][:, 1], ps, RT[h][:, 0].bitcast(F32), ALU.subtract).then_inc(sem(name), 1)

            after(dve, "w3_hi")
            once(dve.tensor_tensor(W3[:, 1].rearrange("p w c o -> p w (c o)"), HB[1][:, 0:3, :],
                              W3[:, 0].rearrange("p w c o -> p w (c o)").bitcast(F32), ALU.subtract), "w3_split")
            after(dve, "tanh_g")
            once(dve.tensor_tensor(bb[:], row("beta"), row("b2"), ALU.add), "bb")
            once(dve.tensor_scalar(g1[:], row("gamma"), tanh_g[:, 0:1], None, ALU.mult), "g1")
            once(dve.tensor_scalar(be1[:], row("beta"), tanh_g[:, 0:1], None, ALU.mult), "be1")

            def choose(m, n, h, eps, gate):
                R = RTM[h]
                lg = bank(h, 0)[:, 0:TT * E].rearrange("p (j e) -> p j e", e=E)
                q = m * B + n
                dve.wait_ge(sem("logits_ps"), q + 1)
                step(dve.tensor_reduce(R[:, 7, :, 0], lg, AX, ALU.max))
                chained()
                dve.tensor_tensor(R[:, 0], lg, R[:, 7, :, 0:1].to_broadcast([P, TT, E]), ALU.subtract).then_inc(sem("rt_sub"), 1)
                dve.wait_ge(sem("rt_exp"), q + 1)
                step(dve.tensor_reduce(R[:, 7, :, 1], R[:, 1], AX, ALU.add))
                chained()
                step(dve.reciprocal(R[:, 7, :, 2], R[:, 7, :, 1]))
                chained()
                step(dve.tensor_tensor(R[:, 1], R[:, 1], R[:, 7, :, 2:3].to_broadcast([P, TT, E]), ALU.mult))
                chained()
                for j in range(TT):
                    ins = dve.max(R[:, 2, j], R[:, 1, j])
                step(ins)
                chained()
                for j in range(TT):
                    ins = dve.max_index(rix[h][:, j], R[:, 2, j], R[:, 1, j])
                step(ins)
                chained()
                step(dve.tensor_copy(R[:, 3, :, 0:2], rix[h][:, :, 0:2]))
                chained()
                for kk in range(2):
                    step(dve.tensor_tensor(R[:, 4 + kk], iota_e[:].unsqueeze(1).to_broadcast([P, TT, E]),
                                           R[:, 3, :, kk:kk + 1].to_broadcast([P, TT, E]), ALU.is_equal))
                step(dve.tensor_tensor(R[:, 7, :, 3], R[:, 2, :, 0], R[:, 2, :, 1], ALU.add))
                chained()
                step(dve.tensor_tensor(R[:, 6], R[:, 4], R[:, 5], ALU.add))
                step(dve.tensor_scalar(R[:, 7, :, 4], R[:, 7, :, 3], eps, None, ALU.add))
                chained()
                step(dve.tensor_copy(rbf[h][:, 0], R[:, 6]))
                for j in range(TT):
                    step(dve.tensor_tensor(carry[:, j + 1], carry[:, j], R[:, 6, j], ALU.add))
                    chained()
                dve.tensor_copy(rbf[h][:, 1], carry[:, 0:TT]).then_inc(sem("chosen"), 1)
                step(dve.reciprocal(R[:, 7, :, 5], R[:, 7, :, 4]))
                chained()
                step(dve.tensor_scalar(R[:, 7, :, 6], R[:, 7, :, 5], tanh_g[:, gate:gate + 1], None, ALU.mult))
                chained()
                step(dve.tensor_tensor(share[m][:, n], R[:, 2, :, 0:2], R[:, 7, :, 6:7].to_broadcast([P, TT, 2]), ALU.mult))
                dve.wait_ge(sem("chosen"), q + 1)
                step(dve.tensor_copy(carry[:, 0], carry[:, TT]))

            def place(m, n, h):
                R = RTM[h]
                q = m * B + n
                dve.wait_ge(sem("rank_ps"), q + 1)
                rank = bank(h, 1)[:, 0:TT * E].rearrange("p (j e) -> p j e", e=E)
                step(dve.tensor_tensor(R[:, 0], rank, ebase[:].unsqueeze(1).to_broadcast([P, TT, E]), ALU.add))
                chained()
                for kk in range(2):
                    step(dve.tensor_tensor(R[:, 4 + kk], R[:, 4 + kk], R[:, 0], ALU.mult))
                    chained()
                    step(dve.tensor_reduce(R[:, 3, :, kk], R[:, 4 + kk], AX, ALU.add))
                    chained()
                dve.tensor_copy(dest[m][:, n], R[:, 3, :, 0:2]).then_inc(sem("dest"), 1)

            def route(m, pair, eps, gate):
                for n, h in of_pair[pair]:
                    dve.wait_ge(sem("xnT_hi"), m * B + n + 1)
                    lo_part(h, banks(h, 2), "xnT_lo")
                for n, h in of_pair[pair]:
                    choose(m, n, h, eps, gate)
                for n, h in of_pair[pair]:
                    place(m, n, h)

            for pair in range(PAIRS):
                for n, h in of_pair[pair]:
                    dve.wait_ge(sem(f"x_in{h}"), 32 * (n // 2 + 1))
                    if n == 0:
                        dve.wait_ge(sem("pool_c"), 11)
                    if n >= 2:
                        dve.wait_ge(sem("embo"), n - 1)
                        dve.wait_ge(sem("ffn_ps"), n - 1)
                    normalise(h, X[h], S1[h], 1e-5, step)
                    chained()
                    dve.tensor_tensor(EMB[h][:], S1[h][:],
                                      S0[h][:].rearrange("p c t -> p (c t)").rearrange("p (j d) -> p j d", d=D), ALU.add)\
                       .then_inc(sem("emb"), 1)
                for n, h in of_pair[pair]:
                    dve.wait_ge(sem("inT_hi"), n + 1)
                    lo_part(h, banks(h, 0), "inT_lo")
                for n, h in of_pair[pair]:
                    if n == 0:
                        dve.wait_ge(sem("pool_c"), 13)
                        once(dve.tensor_reduce(wmax[:], HB[0][:, 0:TT, :], AX, ALU.max), "row_max")
                        after(dve, "row_max")
                        once(dve.tensor_scalar(wmax[:], wmax[:], -1.0, None, ALU.mult), "wmax")
                        after(dve, "ewT_ps")
                        once(dve.tensor_copy(EWT[:], banks(1, 0, 4)), "ewT")
                    dve.wait_ge(sem("qk_ps"), 2 * n + 2)
                    step(dve.tensor_reduce(kb[h][:, 0], banks(h, 2), AX, ALU.max))
                    chained()
                    step(dve.tensor_tensor(kb[h][:, 0], kb[h][:, 0], col("bk", 0, C), ALU.add))
                    chained()
                    dve.tensor_tensor(kb[h][:, 1], col("bk", 0, C), kb[h][:, 0], ALU.subtract).then_inc(sem("kbias"), 1)
                    dve.wait_ge(sem("th"), n + 1)
                    step(dve.tensor_scalar(HB[h][:, 6:8], HB[h][:, 6:8], 0.5, 0.5, ALU.mult, ALU.add))
                for n, h in of_pair[pair]:
                    dve.wait_ge(sem("v_ps"), n + 1)
                    dve.wait_ge(sem("ek"), n + 1)
                    dve.tensor_tensor(HB[h][:, 2:4], HB[h][:, 0:2], banks(h, 0), ALU.mult).then_inc(sem("ekv"), 1)
                for n, h in of_pair[pair]:
                    dve.wait_ge(sem("den_ps"), n + 1)
                    step(dve.reciprocal(S0[h][:], banks(h, 2)))
                    chained()
                    step(dve.tensor_tensor(S0[h][:], banks(h, 0), S0[h][:], ALU.mult))
                    chained()
                    for c in range(C):
                        ins = dve.scalar_tensor_tensor(out=HB[h][:, 4 + c], in0=S0[h][:, c], scalar=col("bv", c),
                                                       in1=HB[h][:, 6 + c], op0=ALU.add, op1=ALU.mult)
                    ins.then_inc(sem("yT"), 1)
                for n, h in of_pair[pair]:
                    dve.wait_ge(sem("attn_ps"), n + 1)
                    dve.wait_ge(sem("embo"), n + 1)
                    step(dve.tensor_tensor(S1[h][:], token_banks(h, 0), EMB[h][:], ALU.add))
                    chained()
                    if n < 2:
                        dve.wait_ge(sem("w1_split"), 4)
                    else:
                        dve.wait_ge(sem(f"scattered{h}"), 16 * 2 * TT * (n // 2))
                    normalise(h, S1[h], S2[h], 1e-5, lambda ins: ins.then_inc(sem("r_norm"), 1))
                for n, h in of_pair[pair]:
                    dve.wait_ge(sem("aT"), n + 1)
                    dve.tensor_copy(RT[h][:, 0], S0[h][:]).then_inc(sem("aT_hi"), 1)
                for n, h in of_pair[pair]:
                    for m in range(1, HC, 2):
                        dve.wait_ge(sem("hid_ps"), HC * n + m + 1)
                        dve.tensor_scalar(HB[h][:, m], bank(h, m % 4), col("b1", m), 0.0, ALU.add, ALU.max).then_inc(sem("hid_dve"), 1)
                for n, h in of_pair[pair]:
                    dve.wait_ge(sem("ffn_ps"), n + 1)
                    dve.wait_ge(sem("atok"), 2 * n + 2)
                    step(dve.tensor_tensor(S2[h][:], token_banks(h, 0), S1[h][:], ALU.add))
                    chained()
                    normalise(h, S2[h], S1[h], 1e-5, step)
                    chained()
                    dve.wait_ge(sem("xbeta"), n + 1)
                    step(dve.tensor_tensor(S1[h][:], S1[h][:], tiles(g1[:]), ALU.mult))
                    chained()
                    step(dve.tensor_tensor(X[h][:], X[h][:], S1[h][:], ALU.add))
                    chained()
                    normalise(h, X[h], S2[h], 1e-5, lambda ins: ins.then_inc(sem("xn"), 1))
                route(0, pair, 0.0, 2)
                for n, h in of_pair[pair]:
                    dve.wait_ge(sem("shared_ps"), n + 1)
                    dve.scalar_tensor_tensor(out=X[h][:].rearrange("p j d -> p (j d)"), in0=banks(h, 0).rearrange("p b t -> p (b t)"),
                                             scalar=tanh_g[:, 2:3],
                                             in1=X[h][:].rearrange("p j d -> p (j d)"), op0=ALU.mult, op1=ALU.add)\
                       .then_inc(sem("batch_a"), 1)
            table_dve(dve, 0, step, chained)
            dve.wait_ge(sem("m0_table"), 1)
            moe_dve(dve, 0)

            def combine(m, n, h):
                dve.wait_ge(sem(f"x_in{h}"), 32 * PAIRS + (32 * (n // 2 + 1) if m == 0 else 32 * PAIRS + 16 * (n // 2 + 1)))
                dve.wait_ge(sem(f"rows{h}"), 16 * 2 * TT * (m * PAIRS + n // 2 + 1))
                for kk in range(2):
                    for j in range(TT):
                        ins = dve.scalar_tensor_tensor(out=X[h][:, j], in0=rows_h[h][:, kk, j], scalar=share[m][:, n, j, kk:kk + 1],
                                                       in1=X[h][:, j], op0=ALU.mult, op1=ALU.add)
                        if kk == 1 and j == TT - 1:
                            ins.then_inc(sem("combined"), 1)
                        elif j == TT - 1:
                            step(ins)
                            chained()

            after(dve, "gt_hi")
            once(dve.tensor_tensor(GT[:, 1], PS[:, 7, :].rearrange("p (c o) -> p c o", c=C), GT[:, 0].bitcast(F32), ALU.subtract), "gt_lo")
            step(dve.tensor_tensor(gbias[:, 0:4], col("bih", 0, 4), col("bhh", 0, 4), ALU.add))
            chained()
            step(dve.tensor_scalar(gbias[:, 0:4], gbias[:, 0:4], 0.5, None, ALU.mult))
            once(dve.tensor_scalar(gbias[:, 4:6], col("bhh", 4, 2), 0.5, None, ALU.mult), "gbias")
            for pair in range(PAIRS):
                for n, h in of_pair[pair]:
                    combine(0, n, h)
                    dve.wait_ge(sem("combined"), n + 1)
                    normalise(h, X[h], S1[h], 1e-5, lambda ins: ins.then_inc(sem("slot0"), 1))
                    ctx_t = S0[h][:].rearrange("p c t -> p (c t)").rearrange("p (j d) -> p j d", d=D)
                    dve.wait_ge(sem("slot0"), n + 1)
                    for j in range(TT):
                        ins = dve.bn_stats(st6[h][:, j], ctx_t[:, j])
                    step(ins)
                    chained()
                    for j in range(TT):
                        ins = dve.bn_aggr(mv[h][:, j], st6[h][:, j])
                    step(ins)
                    chained()
                    step(dve.tensor_tensor(SM[h][:, 0], mv[h][:, :, 0], mv[h][:, :, 0], ALU.mult))
                    chained()
                    dve.scalar_tensor_tensor(out=ve[h][:], in0=mv[h][:, :, 1], scalar=1e-6, in1=SM[h][:, 0], op0=ALU.add, op1=ALU.add)\
                       .then_inc(sem("var_ready"), 1)
                    ln[0] += 1
                    dve.wait_ge(sem("rstd_ready"), ln[0])
                    for j in range(TT):
                        ins = dve.tensor_scalar(S2[h][:, j], ctx_t[:, j], rstd[h][:, j:j + 1], None, ALU.mult)
                    ins.then_inc(sem("pn"), 1)
                for n, h in of_pair[pair]:
                    dve.wait_ge(sem("inT_hi"), B + n + 1)
                    dve.tensor_tensor(RT[h][:, 1], S0[h][:], RT[h][:, 0].bitcast(F32), ALU.subtract).then_inc(sem("inT_lo"), 1)
                    dve.wait_ge(sem("slot_hi"), slot_hi_count(n, 0))
                    dve.tensor_tensor(HTS[h][:, 1], banks(h, 2), HTS[h][:, 0].bitcast(F32), ALU.subtract).then_inc(sem("slot_lo"), 1)
                for n, h in of_pair[pair]:
                    dve.wait_ge(sem("kk_hi"), n + 1)
                    dve.tensor_tensor(KK[h][:, 1], S0[h][:], KK[h][:, 0].bitcast(F32), ALU.subtract).then_inc(sem("kk_lo"), 1)
                for steps in slot_steps[pair * ITERS:(pair + 1) * ITERS]:
                    for q, it, n, h in steps:
                        dve.wait_ge(sem("ss_ps"), q + 1)
                        dve.tensor_scalar(ve[h][:], bank(h, 0)[:, 0:TT], 1.0 / D, 1e-6, ALU.mult, ALU.add).then_inc(sem("var_ready"), 1)
                        ln[0] += 1
                        dve.wait_ge(sem("rstd_ready"), ln[0])
                        for j in range(TT):
                            ins = dve.tensor_scalar(S1[h][:].rearrange("p j d -> p (j d)")[:, j * P:(j + 1) * P], ident[:], rstd[h][:, j:j + 1], None, ALU.mult)
                        ins.then_inc(sem("diag"), 1)
                    for q, it, n, h in steps:
                        dve.wait_ge(sem("rsb_ps"), q + 1)
                        dve.tensor_tensor(S0[h][:], HT[h][:], bank(h, 1).unsqueeze(1).to_broadcast([P, C, T]), ALU.mult).then_inc(sem("sn"), 1)
                    for q, it, n, h in steps:
                        dve.wait_ge(sem("sn_hi"), q + 1)
                        dve.tensor_tensor(RT[h][:, 1], S0[h][:], RT[h][:, 0].bitcast(F32), ALU.subtract).then_inc(sem("sn_lo"), 1)
                    for q, it, n, h in steps:
                        for j in range(TT):
                            dve.wait_ge(sem("score_ps"), TT * q + j + 1)
                            step(dve.tensor_reduce(SM[h][:, 0, j:j + 1], bank(h, j), AX, ALU.max))
                            chained()
                            dve.tensor_scalar(SM[h][:, 1, j:j + 1], SM[h][:, 0, j:j + 1], -1.0 / 16, None, ALU.mult).then_inc(sem("smax"), 1)
                        dve.wait_ge(sem("sexp"), TT * (q + 1))
                        if it == 0:
                            dve.wait_ge(sem("v_out"), n + 1)
                        step(dve.reciprocal(SM[h][:, 3], SM[h][:, 2]))
                        chained()
                        dve.tensor_copy(VP[h][:, :, D:D + 1], SM[h][:, 3].unsqueeze(2))
                        for j in range(TT):
                            ins = dve.tensor_scalar(VP[h][:, j, 0:D], EMB[h][:, j], SM[h][:, 3, j:j + 1], None, ALU.mult)
                        ins.then_inc(sem("vp"), 1)
                    for q, it, n, h in steps:
                        dve.wait_ge(sem("upd_ps"), q + 1)
                        step(dve.tensor_scalar(SM[h][:, 0], banks(h, 0, TT)[:, :, D], 1e-6, None, ALU.add))
                        chained()
                        step(dve.reciprocal(SM[h][:, 4], SM[h][:, 0]))
                        chained()
                        for j in range(TT):
                            ins = dve.tensor_scalar(S2[h][:, j], bank(h, j)[:, 0:D], SM[h][:, 4, j:j + 1], None, ALU.mult)
                        ins.then_inc(sem("upd"), 1)
                    for q, it, n, h in steps:
                        dve.wait_ge(sem("uT_hi"), q + 1)
                        lo_part(h, banks(h, 0), "uT_lo")
                    for q, it, n, h in steps:
                        for d in range(C):
                            g = 4 * (C * q + d)
                            dve.wait_ge(sem("r_out"), C * q + d + 1)
                            step(dve.scalar_tensor_tensor(out=gate_slot(h, d, 3), in0=gate_slot(h, d, 0), scalar=1.0, in1=gate_slot(h, d, 1), op0=ALU.add, op1=ALU.mult))
                            chained()
                            dve.wait_ge(sem("gru_ps"), g + 3)
                            dve.tensor_tensor(gate_slot(h, d, 3), bank(h, 1), gate_slot(h, d, 3), ALU.add).then_inc(sem("xn_out"), 1)
                        for d in range(C):
                            dve.wait_ge(sem("h_minus_n"), C * q + d + 1)
                            dve.wait_ge(sem("z_out"), C * q + d + 1)
                            step(dve.scalar_tensor_tensor(out=gate_slot(h, d, 1), in0=gate_slot(h, d, 2), scalar=1.0, in1=gate_slot(h, d, 0), op0=ALU.add, op1=ALU.mult))
                            chained()
                            ins = dve.scalar_tensor_tensor(out=HT[h][:, d], in0=gate_slot(h, d, 1), scalar=0.5, in1=gate_slot(h, d, 3), op0=ALU.mult, op1=ALU.add)
                        ins.then_inc(sem("slot_new"), 1)
                    if steps[0][1] < ITERS - 1:
                        for q, it, n, h in steps:
                            dve.wait_ge(sem("slot_hi"), slot_hi_count(n, it + 1))
                            dve.tensor_tensor(HTS[h][:, 1], HT[h][:], HTS[h][:, 0].bitcast(F32), ALU.subtract).then_inc(sem("slot_lo"), 1)
                for n, h in of_pair[pair]:
                    dve.wait_ge(sem("final_ps"), n + 1)
                    step(dve.scalar_tensor_tensor(out=X[h][:].rearrange("p j d -> p (j d)"), in0=banks(h, 0).rearrange("p b t -> p (b t)"),
                                                  scalar=tanh_g[:, 1:2], in1=X[h][:].rearrange("p j d -> p (j d)"), op0=ALU.mult, op1=ALU.add))
                    chained()
                    normalise(h, X[h], S2[h], 1e-5, lambda ins: ins.then_inc(sem("batch_c"), 1))
                route(1, pair, 1e-9, 3)
            table_dve(dve, 1, step, chained)
            dve.wait_ge(sem("m1_table"), 1)
            dve.wait_ge(sem("db_in"), 16)
            moe_dve(dve, 1)
            for pair in range(PAIRS):
                for n, h in of_pair[pair]:
                    combine(1, n, h)

        @block.tensor
        def _(pe):
            def turn(h, k, src, name):
                for c in range(C):
                    for j in range(TT):
                        ins = pe.transpose(bank(h, k + c)[:, j * P:(j + 1) * P], src[:, j, c * P:(c + 1) * P], ident[:])
                ins.then_inc(sem(name), 1)

            def parts(t, *at):
                return tuple(t[(slice(None), i) + at] for i in two)

            def logits(m, pair, ready):
                for n, h in of_pair[pair]:
                    pe.wait_ge(sem(ready), n + 1)
                    turn(h, 2, S2[h], "xnT_ps")
                for n, h in of_pair[pair]:
                    pe.wait_ge(sem("xnT_lo"), m * B + n + 1)
                    for j in range(TT):
                        for c in range(C):
                            ins = product(pe, bank(h, 0)[:, j * E:(j + 1) * E], parts(RT[h], c, slice(j * P, (j + 1) * P)),
                                          (rw[2 * m][:, c], rw[2 * m + 1][:, c]), c == 0, c == C - 1)
                    ins.then_inc(sem("logits_ps"), 1)

            def ranks(m, pair):
                for n, h in of_pair[pair]:
                    pe.wait_ge(sem("chosen"), m * B + n + 1)
                    pe.matmul(bank(h, 1)[:, 0:TT * E], tri[:], rbf[h][:, 0].rearrange("p j e -> p (j e)"), start=True, stop=False)
                    pe.matmul(bank(h, 1)[:, 0:TT * E], ones_bf[:], rbf[h][:, 1].rearrange("p j e -> p (j e)"), start=False, stop=True)\
                      .then_inc(sem("rank_ps"), 1)

            pe.wait_ge(sem("pool_c"), 11)
            for pair in range(PAIRS):
                for n, h in of_pair[pair]:
                    pe.wait_ge(sem("emb"), n + 1)
                    if n >= 2:
                        pe.wait_ge(sem("batch_a"), n - 1)
                    turn(h, 0, EMB[h], "inT_ps")
                if pair == 0:
                    after(pe, "w3_split")
                for n, h in of_pair[pair]:
                    if n == 1:
                        after(pe, "ewT")
                    pe.wait_ge(sem("inT_lo"), n + 1)
                    for w in range(2):
                        for c in range(C):
                            for c2 in range(C):
                                ins = product(pe, bank(h, 2 * w + c), parts(W3, w, c2, slice(c * P, (c + 1) * P)),
                                              parts(RT[h], c2), c2 == 0, c2 == C - 1)
                        ins.then_inc(sem("qk_ps"), 1)
                    if n == 0:
                        after(pe, "ew")
                        pe.wait_ge(sem("inT_lo"), 2)
                        for jc in range(TT):
                            for i in range(TT):
                                ins = pe.transpose(bank(1, jc)[:, i * P:(i + 1) * P], HB[0][:, i, jc * P:(jc + 1) * P], ident[:])
                        once(ins, "ewT_ps")
                for n, h in of_pair[pair]:
                    pe.wait_ge(sem("th"), n + 1)
                    for j in range(TT):
                        for c in range(C):
                            ins = product(pe, token_banks(h, 0)[:, j], parts(RT[h], c, slice(j * P, (j + 1) * P)),
                                          parts(W3, 2, c), c == 0, c == C - 1)
                    ins.then_inc(sem("v_ps"), 1)
                    pe.wait_ge(sem("ekT"), n + 1)
                    for j in range(TT):
                        for c in range(C):
                            ins = pe.transpose(token_banks(h, 2)[:, j, c * P:(c + 1) * P], S0[h][:, c, j * P:(j + 1) * P], ident[:])
                    ins.then_inc(sem("ek_ps"), 1)
                for n, h in of_pair[pair]:
                    pe.wait_ge(sem("ekv"), n + 1)
                    if n == 0:
                        after(pe, "ewT")
                    for b, src in ((0, 2), (2, 0)):
                        w = HB[h][:, src:src + 2].rearrange("p b (a d) -> p (b a) d", d=D)
                        for c in range(C):
                            for j in range(TT):
                                ins = pe.matmul(bank(h, b + c), w[:, j, c * P:(c + 1) * P], EWT[:, j], start=j == 0, stop=j == TT - 1)
                    ins.then_inc(sem("den_ps"), 1)
                for n, h in of_pair[pair]:
                    pe.wait_ge(sem("yT"), n + 1)
                    if n == 0:
                        pe.wait_ge(sem("wplain_in"), 48)
                    for j in range(TT):
                        for c in range(C):
                            ins = pe.matmul(token_banks(h, 0)[:, j], HB[h][:, 4 + c, j * P:(j + 1) * P], WO[:, c], start=c == 0, stop=c == C - 1)
                    ins.then_inc(sem("attn_ps"), 1)
                for n, h in of_pair[pair]:
                    pe.wait_ge(sem("r_norm"), n + 1)
                    turn(h, 2, S2[h], "aT_ps")
                for n, h in of_pair[pair]:
                    pe.wait_ge(sem("aT_lo"), n + 1)
                    for m in range(HC):
                        if m >= 4:
                            pe.wait_ge(sem("hid_dve" if m % 2 else "hid_act"), HC // 2 * n + (m - 4) // 2 + 1)
                        for c in range(C):
                            ins = product(pe, bank(h, m % 4), parts(W1, c, slice(m * P, (m + 1) * P)), parts(RT[h], c), c == 0, c == C - 1)
                        ins.then_inc(sem("hid_ps"), 1)
                for n, h in of_pair[pair]:
                    pe.wait_ge(sem("hid_act"), HC // 2 * (n + 1))
                    pe.wait_ge(sem("hid_dve"), HC // 2 * (n + 1))
                    for j in range(TT):
                        for m in range(HC):
                            ins = pe.matmul(token_banks(h, 0)[:, j], HB[h][:, m, j * P:(j + 1) * P], W2[:, m], start=m == 0, stop=m == HC - 1)
                    ins.then_inc(sem("ffn_ps"), 1)
                logits(0, pair, "xn")
                for n, h in of_pair[pair]:
                    for f in range(SC):
                        if f >= 2:
                            pe.wait_ge(sem("sh_relu"), SC * n + f - 1)
                        for c in range(C):
                            ins = product(pe, bank(h, 2 + f % 2), parts(WS1, c, slice(f * P, (f + 1) * P)), parts(RT[h], c), c == 0, c == C - 1)
                        ins.then_inc(sem("sh_ps"), 1)
                ranks(0, pair)
                for n, h in of_pair[pair]:
                    pe.wait_ge(sem("dest"), n + 1)
                    pe.wait_ge(sem("sh_sq"), SC * (n + 1))
                    for j in range(TT):
                        for f in range(SC):
                            ins = pe.matmul(token_banks(h, 0)[:, j], HB[h][:, f, j * P:(j + 1) * P], WS2[:, f], start=f == 0, stop=f == SC - 1)
                    ins.then_inc(sem("shared_ps"), 1)
            table_pe(pe, 0)
            pe.wait_ge(sem("m0_table"), 1)
            moe_pe(pe, 0)

            pe.wait_ge(sem("cw_raw"), 80)
            for c in range(C):
                for o in range(C):
                    ins = pe.matmul(PS[:, 7, c * D:(c + 1) * D], raw_k[:, o, c * P:(c + 1) * P], raw_q[:, o], start=o == 0, stop=o == C - 1)
            once(ins, "gt_ps")
            for pair in range(PAIRS):
                for n, h in of_pair[pair]:
                    if n == 1:
                        after(pe, "gt_lo")
                    pe.wait_ge(sem("slot0"), n + 1)
                    turn(h, 2, S1[h], "aT_ps")
                    pe.wait_ge(sem("pn"), n + 1)
                    turn(h, 0, S2[h], "inT_ps")
                for n, h in of_pair[pair]:
                    after(pe, "gt_lo")
                    pe.wait_ge(sem("inT_lo"), B + n + 1)
                    for c in range(C):
                        for c2 in range(C):
                            ins = product(pe, bank(h, c), parts(GT, c2, slice(c * P, (c + 1) * P)), parts(RT[h], c2), c2 == 0, c2 == C - 1)
                    ins.then_inc(sem("kk_ps"), 1)
                    pe.wait_ge(sem("cw_lo"), 1)
                    pe.wait_ge(sem("slot_lo"), slot_lo_count(n, 0))
                    for j in range(TT):
                        for c in range(C):
                            ins = product(pe, token_banks(h, 2)[:, j], parts(RT[h], c, slice(j * P, (j + 1) * P)), parts(VW, c), c == 0, c == C - 1)
                    ins.then_inc(sem("v_ps"), 1)
                for steps in slot_steps[pair * ITERS:(pair + 1) * ITERS]:
                    for q, it, n, h in steps:
                        pe.wait_ge(sem("slot_sq"), q + 1)
                        for j in range(TT):
                            for c in range(C):
                                ins = pe.matmul(bank(h, 0)[:, j:j + 1], S0[h][:, c, j * P:(j + 1) * P], ones[:, 0:1], start=c == 0, stop=c == C - 1)
                        ins.then_inc(sem("ss_ps"), 1)
                    for q, it, n, h in steps:
                        pe.wait_ge(sem("diag"), q + 1)
                        pe.matmul(bank(h, 1), ones[:], S1[h][:].rearrange("p j d -> p (j d)")[:, 0:T], start=True, stop=True).then_inc(sem("rsb_ps"), 1)
                    for q, it, n, h in steps:
                        pe.wait_ge(sem("sn_lo"), q + 1)
                        if it == 0:
                            pe.wait_ge(sem("v_out"), n + 1)
                        for j in range(TT):
                            for c in range(C):
                                ins = product(pe, bank(h, j), parts(KK[h], c, slice(j * P, (j + 1) * P)), parts(RT[h], c), c == 0, c == C - 1)
                            ins.then_inc(sem("score_ps"), 1)
                    for q, it, n, h in steps:
                        pe.wait_ge(sem("vp"), q + 1)
                        for j in range(TT):
                            for m in range(TT):
                                ins = pe.matmul(bank(h, j)[:, 0:D + 1], HB[h][:, m, j * P:(j + 1) * P], VP[h][:, m, 0:D + 1], start=m == 0, stop=m == TT - 1)
                        ins.then_inc(sem("upd_ps"), 1)
                    for q, it, n, h in steps:
                        pe.wait_ge(sem("upd"), q + 1)
                        turn(h, 0, S2[h], "uT_ps")
                    for q, it, n, h in steps:
                        if q == 0:
                            pe.wait_ge(sem("cw_lo"), 3)
                            after(pe, "gbias")
                        pe.wait_ge(sem("uT_lo"), q + 1)
                        pe.wait_ge(sem("slot_lo"), slot_lo_count(n, it))
                        for d in range(C):
                            g = C * q + d

                            def gates(b, terms, name):
                                if d:
                                    pe.wait_ge(sem(name), g)
                                k = [(w, o, src, c) for w, o, src in terms for c in range(C)]
                                for i, (w, o, src, c) in enumerate(k):
                                    ins = product(pe, bank(h, b), parts(w, c, slice(o * P, (o + 1) * P)), parts(src, c), i == 0, i == len(k) - 1)
                                ins.then_inc(sem("gru_ps"), 1)

                            gates(0, [(WHH, 4 + d, HTS[h])], "hn_out")
                            gates(2, [(WHH, d, HTS[h]), (WIH, d, RT[h])], "r_out")
                            gates(1, [(WIH, 4 + d, RT[h])], "xn_out")
                            gates(3, [(WHH, 2 + d, HTS[h]), (WIH, 2 + d, RT[h])], "z_out")
                for n, h in of_pair[pair]:
                    pe.wait_ge(sem("slot_new"), slot_count(n, ITERS))
                    for j in range(TT):
                        for c in range(C):
                            ins = pe.transpose(token_banks(h, 0)[:, j, c * P:(c + 1) * P], HT[h][:, c, j * P:(j + 1) * P], ident[:])
                    ins.then_inc(sem("final_ps"), 1)
                logits(1, pair, "batch_c")
                ranks(1, pair)
            table_pe(pe, 1)
            pe.wait_ge(sem("m1_table"), 1)
            moe_pe(pe, 1)


def lay_out(inputs):
    a = {k: np.asarray(v) for k, v in inputs.items()}
    c = np.ascontiguousarray

    def by_partition(v):
        return v.reshape(-1, P).T

    names = (("bq", "L0_xattn_bq"), ("bk", "L0_xattn_bk"), ("bv", "L0_xattn_bv"), ("gamma", "L0_xattn_gamma"),
             ("beta", "L0_xattn_beta"), ("b1", "L0_xattn_b1"), ("w_in", "L1_xattn_input_norm_w"),
             ("w_slot", "L1_xattn_slot_norm_w"), ("bih", "L1_xattn_gru_bih"), ("bhh", "L1_xattn_gru_bhh"),
             ("gate_b", "L1_ffn_gate_b"), ("up_b", "L1_ffn_up_b"))
    assert [n for n, _ in names] == list(COLS)
    return {
        "x": a["x"], "ctx_in": a["ctx_1024"],
        "cols": c(np.concatenate([by_partition(a[full]) for _, full in names], axis=1)),
        "rows": c(np.concatenate([a["L0_xattn_bo"], a["L0_xattn_gamma"], a["L0_xattn_beta"], a["L0_xattn_b2"],
                                  a["g_xattn"], a["g_ffn"]])),
        "wq": a["L0_xattn_wq"], "wk": a["L0_xattn_wk"], "wv": a["L0_xattn_wv"], "wo": a["L0_xattn_wo"],
        "pos_bias": a["L0_xattn_pos_bias"], "w1": a["L0_xattn_w1"], "w2": a["L0_xattn_w2"],
        "router1": c(a["L0_ffn_w_router"].T), "m1_w1": c(a["L0_ffn_w1_stack"].transpose(0, 2, 1)),
        "m1_w2": c(a["L0_ffn_w2_stack"].transpose(0, 2, 1)), "ws1": c(a["L0_ffn_ws1"].T), "ws2": c(a["L0_ffn_ws2"].T),
        "Wq": a["L1_xattn_Wq"], "Wk": a["L1_xattn_Wk"], "Wv": c(a["L1_xattn_Wv"].T),
        "wih": c(a["L1_xattn_gru_wih"].T), "whh": c(a["L1_xattn_gru_whh"].T), "router2": c(a["L1_ffn_router_w"].T),
        "gate_w": a["L1_ffn_gate_w"], "up_w": a["L1_ffn_up_w"], "down_w": a["L1_ffn_down_w"], "down_b": a["L1_ffn_down_b"],
    }


def program(nc, arrays):
    aps = {name: nc.dram_tensor(name, v.shape, mybir.dt.from_np(v.dtype), kind="ExternalInput").ap()
           for name, v in arrays.items()}
    build(nc, out=nc.dram_tensor("out", (B, T, D), F32, kind="ExternalOutput").ap(), **aps)


def kernel(**inputs):
    import concourse.bacc as _bacc
    from concourse.bass_utils import run_bass_kernel_spmd as _run

    arrays = lay_out(inputs)
    nc = _bacc.Bacc("TRN2", target_bir_lowering=False, num_devices=1)
    program(nc, arrays)
    r = _run(nc, [arrays], core_ids=[0])
    return r.results[0]["out"]
```

```python
from contextlib import ExitStack

import numpy as np
import concourse.bass as bass
from concourse import mybir
from concourse.alu_op_type import AluOpType as ALU

P = 128
F32 = mybir.dt.float32
F32R = mybir.dt.float32r
BF16 = mybir.dt.bfloat16
I32 = mybir.dt.int32
U32 = mybir.dt.uint32
ACT = mybir.ActivationFunctionType
AX = mybir.AxisListType.X

B, T, D = 4, 512, 256
TT = T // P
C = D // P
H = 1024
HC = H // P
BAND = 64
E = 8
FS = 512
SC = FS // P
F1 = 256
F2 = 512
G = 256
CAP = B * T + G
NG = B * T * 2 // G + E
XROWS = E * CAP + 2 * G
ITERS = 3
PAIRS = B // 2

ORDER_A = {
    "pe": "turn0 turn1 qk0 qk1 v0 v1 den0 num0 den1 attn0 num1 attn1 aT0 hid0 aT1 hid1 ffn0 ffn1 "
          "xnT0 logits0 up0 xnT1 logits1 rank0 up1 rank1 down0 down1",
    "act": "turn0 turn1 qk0 qk1 v0 v1 aT0 hid0 aT1 hid1 xnT0 up0 xnT1 logits0 logits1 up1",
    "dve": "turn0 turn1 qk0 qk1 v0 v1 den0 num0 den1 attn0 num1 aT0 attn1 hid0 aT1 hid1 ffn0 xnT0 ffn1 "
           "xnT1 logits0 rank0 logits1 rank1 in0 down0 in1 down1",
    "pool": "turn0 turn1 attn0 attn1 aT0 aT1 ffn0 ffn1 in0 down0 in1 down1",
    "sp": "in0 in1 down0 down1",
}

COLS = {}
for _name, _n in (("bq", C), ("bk", C), ("bv", C), ("gamma", C), ("beta", C), ("b1", HC), ("w_in", C), ("w_slot", C),
                  ("bih", 3 * C), ("bhh", 3 * C), ("gate_b", E * F2 // P), ("up_b", E * F2 // P)):
    _at = sum(n for _, n in COLS.values())
    COLS[_name] = (_at, _n)
NCOLS = sum(n for _, n in COLS.values())
ROWS = {"bo": 0, "gamma": D, "beta": 2 * D, "b2": 3 * D, "g": 4 * D}
NROWS = 4 * D + 4


def build(nc, x, ctx_in, cols, rows, wq, wk, wv, wo, pos_bias, w1, w2, router1, m1_w1, m1_w2, ws1, ws2,
          Wq, Wk, Wv, wih, whh, router2, gate_w, up_w, down_w, down_b, out):
    top = ExitStack()
    with top:
        def sb(name, shape, dt=F32, where=None):
            return (where or top).enter_context(nc.sbuf_tensor(name, shape, dt))

        sems = {}

        def sem(name):
            if name not in sems:
                sems[name] = top.enter_context(nc.semaphore(name))
            return sems[name]

        x_base = nc.dram_tensor("x_base", (2, B, T, D), F32, kind="Internal").ap()
        routed = [nc.dram_tensor(f"routed{m}", (XROWS, D), F32, kind="Internal").ap() for m in range(2)]
        outputs = nc.dram_tensor("outputs", (NG * G, D), F32, kind="Internal").ap()

        PS = top.enter_context(nc.psum_tensor("PS", [P, 8, 512], F32))
        ident = sb("ident", [P, P])
        ones = sb("ones", [P, P])
        tri = sb("tri", [P, P], BF16)
        ones_bf = sb("ones_bf", [P, P], BF16)
        zeros = sb("zeros", [P, G // P, D])
        colv = sb("colv", [P, NCOLS])
        rowv = sb("rowv", [P, NROWS])
        minus_half = sb("minus_half", [P, TT])
        hbq = sb("hbq", [P, C])
        tanh_g = sb("tanh_g", [P, 4])
        bb = sb("bb", [P, D])
        g1 = sb("g1", [P, D])
        be1 = sb("be1", [P, D])
        iota_e = sb("iota_e", [P, E])
        ebase = sb("ebase", [P, E])
        iota_g = sb("iota_g", [P, 32])
        rw = [sb(f"rw{m}", [P, C, E], F32R) for m in range(4)]
        dest = [sb(f"dest{m}", [P, B, TT, 2], I32) for m in range(2)]
        share = [sb(f"share{m}", [P, B, TT, 2]) for m in range(2)]
        carry = sb("carry", [P, TT + 1, E])
        expert_of = sb("expert_of", [P, B, TT, 2])
        source = sb("source", [P, B, TT, 2], I32)
        table = [sb(f"table{m}", [1, 64], I32) for m in range(2)]
        tfi = sb("tfi", [P, 2, E], I32)
        two = range(2)
        X = [sb(f"X{h}", [P, TT, D]) for h in two]
        EMB = [sb(f"EMB{h}", [P, TT, D]) for h in two]
        S0 = [sb(f"S0{h}", [P, C, T]) for h in two]
        S1 = [sb(f"S1{h}", [P, TT, D]) for h in two]
        S2 = [sb(f"S2{h}", [P, TT, D]) for h in two]
        HB = [sb(f"HB{h}", [P, HC, T]) for h in two]
        RT = [sb(f"RT{h}", [P, 2, C, T], F32R) for h in two]
        st6 = [sb(f"st6{h}", [P, TT, 6]) for h in two]
        mv = [sb(f"mv{h}", [P, TT, 2]) for h in two]
        ve = [sb(f"ve{h}", [P, TT]) for h in two]
        rstd = [sb(f"rstd{h}", [P, TT]) for h in two]
        kb = [sb(f"kb{h}", [P, 2, C]) for h in two]
        RTM = [sb(f"RTM{h}", [P, 8, TT, E]) for h in two]
        rix = [sb(f"rix{h}", [P, TT, E], U32) for h in two]
        rbf = [sb(f"rbf{h}", [P, 2, TT, E], BF16) for h in two]

        ONCE = {"act": ("tanh_g", "hbq", "w3_hi", "ew", "gt_hi", "hbg"),
                "dve": ("w3_split", "bb", "g1", "be1", "row_max", "wmax", "ewT", "gt_lo", "gbias"),
                "pe": ("ewT_ps", "gt_ps")}

        def once(ins, name):
            who = next(k for k in ONCE if name in ONCE[k])
            ins.then_inc(sem(f"{who}_once"), 1)

        def after(eng, name):
            who = next(k for k in ONCE if name in ONCE[k])
            eng.wait_ge(sem(f"{who}_once"), ONCE[who].index(name) + 1)

        def col(name, i=0, n=1):
            return colv[:, COLS[name][0] + i:COLS[name][0] + i + n]

        def row(name, n=D):
            return rowv[:, ROWS[name]:ROWS[name] + n]

        def tiles(ap):
            return ap.unsqueeze(1).to_broadcast([P, TT, D])

        def bank(h, k):
            return PS[:, 4 * h + k, :]

        def banks(h, k, n=2):
            return PS[:, 4 * h + k:4 * h + k + n, :]

        def token_banks(h, k):
            return banks(h, k).rearrange("p b (a d) -> p (b a) d", d=D)

        def product(pe, out_, a, b, first=True, last=True):
            pe.matmul(out_, a[1], b[0], start=first, stop=False)
            pe.matmul(out_, a[0], b[1], start=False, stop=False)
            return pe.matmul(out_, a[0], b[0], start=False, stop=last)

        part_a = ExitStack()
        W3 = sb("W3", [P, 2, 3, C, D], F32R, part_a)
        W1 = sb("W1", [P, 2, C, H], F32R, part_a)
        WS1 = sb("WS1", [P, 2, C, FS], F32R, part_a)
        WO = sb("WO", [P, C, D], F32, part_a)
        W2 = sb("W2", [P, HC, D], F32, part_a)
        WS2 = sb("WS2", [P, SC, D], F32, part_a)
        EWT = sb("EWT", [P, TT, T], F32, part_a)
        wmax = sb("wmax", [P, TT], F32, part_a)
        NX = sb("NX", [P, TT, D], F32, part_a)
        NC = sb("NC", [P, TT, D], F32, part_a)
        part_m = [ExitStack(), ExitStack()]

        class Moe:
            pass

        moe = [Moe(), Moe()]

        def moe_buffers(m, f):
            w = moe[m]
            st = part_m[m]
            w.fc = f // P
            w.ups = m + 1
            w.cols = C * f * w.ups + w.fc * D
            w.raw = sb(f"raw{m}", [P, w.cols], F32, st)
            w.split = [sb(f"split{m}{i}", [P, 2, w.cols], F32R, st) for i in two]
            w.xg = sb(f"xg{m}", [P, G // P, D], F32, st)
            w.xt = sb(f"xt{m}", [P, 2, C, G], F32R, st)
            w.act = sb(f"act{m}", [P, 2, w.ups, G], F32, st)
            w.h = sb(f"h{m}", [P, w.fc, G], F32, st)
            w.hs = sb(f"hs{m}", [P, 2, w.fc, G], F32R, st)
            w.y = sb(f"y{m}", [P, G // P, D], F32, st)

        moe_buffers(0, F1)
        part_m[0].close()
        part_a.close()
        part_c = ExitStack()
        VW = sb("VW", [P, 2, C, D], F32R, part_c)
        GT = sb("GT", [P, 2, C, D], F32R, part_c)
        WIH = sb("WIH", [P, 2, C, 3 * D], F32R, part_c)
        WHH = sb("WHH", [P, 2, C, 3 * D], F32R, part_c)
        KK = [sb(f"KK{h}", [P, 2, C, T], F32R, part_c) for h in two]
        HT = [sb(f"HT{h}", [P, C, T], F32, part_c) for h in two]
        HTS = [sb(f"HTS{h}", [P, 2, C, T], F32R, part_c) for h in two]
        VP = [sb(f"VP{h}", [P, TT, D + 4], F32, part_c) for h in two]
        SM = [sb(f"SM{h}", [P, 5, TT], F32, part_c) for h in two]
        gbias = sb("gbias", [P, 3 * C], F32, part_c)
        raw_wih = HB[0][:, 0:3, :].rearrange("p a b -> p (a b)").rearrange("p (c o) -> p c o", c=C)
        raw_wv = HB[0][:, 3, :].rearrange("p (c o) -> p c o", c=C)
        raw_whh = HB[1][:, 0:3, :].rearrange("p a b -> p (a b)").rearrange("p (c o) -> p c o", c=C)
        raw_q = HB[1][:, 3, :].rearrange("p (c o) -> p c o", c=C)
        raw_k = HB[1][:, 4, :].rearrange("p (c o) -> p c o", c=C)
        rows_h = [HB[h][:, 4:8, :].rearrange("p a b -> p (a b)").rearrange("p (k j d) -> p k j d", k=2, d=D) for h in two]

        def gate_slot(h, d, k):
            if d == 0:
                return HB[h][:, 4 + k]
            return (S1[h][:, 0:2].rearrange("p j d -> p (j d)"), S1[h][:, 2:4].rearrange("p j d -> p (j d)"), S0[h][:, 0], S0[h][:, 1])[k]

        part_c.close()
        moe_buffers(1, F2)
        DB = sb("DB", [P, E, D], F32, part_m[1])
        hbg = sb("hbg", [P, E * F2 // P], F32, part_m[1])
        part_m[1].close()

        pairs = [(pair, 2 * pair + h, h) for pair in range(PAIRS) for h in two]
        of_pair = [[(n, h) for p_, n, h in pairs if p_ == pair] for pair in range(PAIRS)]

        def stages_a(engine):
            for pair in range(PAIRS):
                for item in ORDER_A[engine].split():
                    stage, h = item[:-1], int(item[-1])
                    n = 2 * (pair + (stage == "in")) + h
                    if n < B:
                        yield stage, n, h

        slot_steps = [[((pair * ITERS + it) * 2 + h, it, n, h) for n, h in of_pair[pair]] for pair in range(PAIRS) for it in range(ITERS)]

        def slot_count(n, it):
            return n // 2 * 2 * (ITERS + 1) + 2 * it + n % 2 + 1

        def slot_lo_count(n, it):
            return n // 2 * 2 * ITERS + 2 * it + n % 2 + 1

        slot_hi_count = slot_lo_count

        def up_weights(m, w, u, c, f):
            at = (u * C + c) * w.fc * P + f * P
            return slice(at, at + P)

        def down_weights(m, w, f):
            at = w.ups * C * w.fc * P + f * D
            return slice(at, at + D)

        def expert_sources(m, e):
            srcs = (m1_w1, m1_w2) if m == 0 else (gate_w, up_w, down_w)
            at = 0
            for src in srcs:
                ap = src[e].rearrange("(c p) o -> p c o", p=P)
                n = ap.shape[1] * ap.shape[2]
                yield ap, at, n
                at += n

        def bounds(eng, m, e):
            return (eng.value_load(table[m][0:1, e:e + 1], min_val=0, max_val=NG - 1),
                    eng.value_load(table[m][0:1, E + e:E + e + 1], min_val=1, max_val=NG))

        def counted(eng, m):
            eng.wait_ge(sem(f"m{m}_table"), 1)

        def moe_end(eng, m, total):
            for name, value in (("xg", 16 * (total + 2)), ("turned", total + 1), ("xhi", total + 1), ("xlo", total + 1),
                                ("down", total), ("y", total + 1), ("yout", 16 * total + 1)):
                eng.wait_ge(sem(f"m{m}_{name}"), value)
                eng.sem_inc(sem("passed"), 1)

        def moe_sp(sp, m):
            w = moe[m]

            def raw_in(e):
                if e:
                    sp.wait_ge(sem(f"m{m}_lo"), e)
                for ap, at, n in expert_sources(m, e):
                    sp.dma_start(w.raw[:, at:at + n].rearrange("p (c o) -> p c o", c=ap.shape[1]), ap).then_inc(sem(f"m{m}_raw"), 16)

            def group_in(t):
                r = sp.value_load(table[m][0:1, bass.ds(t + 2 * E, 1)], min_val=0, max_val=XROWS - G)
                sp.dma_start(w.xg[:], routed[m][bass.ds(r, G), :].rearrange("(a p) d -> p a d", p=P)).then_inc(sem(f"m{m}_xg"), 16)

            raw_in(0)
            sp.wait_ge(sem(f"m{m}_table"), 1)
            for e in range(E):
                r = sp.value_load(table[m][0:1, 2 * E + 32 + e:2 * E + 33 + e], min_val=0, max_val=XROWS - G)
                sp.dma_start(routed[m][bass.ds(r, G), :].rearrange("(a p) d -> p a d", p=P), zeros[:]).then_inc(sem(f"filled{m}"), 16)
            sp.wait_ge(sem(f"filled{m}"), 16 * (2 + E))
            sp.wait_ge(sem("outputs_filled"), 48)
            for h in two:
                sp.wait_ge(sem(f"scattered{h}"), 16 * 2 * TT * PAIRS * (m + 1))
            group_in(0)
            sp.wait_ge(sem(f"m{m}_turned"), 1)
            group_in(1)
            for e in range(E):
                if e + 1 < E:
                    raw_in(e + 1)
                lo, hi = bounds(sp, m, e)
                with sp.Fori(lo, hi) as t:
                    counted(sp, m)
                    sp.wait_ge(sem(f"m{m}_turned"), t + 2)
                    group_in(t + 2)
                    counted(sp, m)
                    sp.wait_ge(sem(f"m{m}_y"), t + 2)
                    sp.dma_start(outputs[bass.ds(t * G, G), :].rearrange("(a p) d -> p a d", p=P), w.y[:]).then_inc(sem(f"m{m}_yout"), 16)
            moe_end(sp, m, hi)

        def moe_pool(pool, m):
            w = moe[m]
            for e in range(E):
                if e >= 2:
                    done = pool.value_load(table[m][0:1, e - 1:e], min_val=1, max_val=NG - 1)
                    counted(pool, m)
                    pool.wait_ge(sem(f"m{m}_down"), done)
                for ap, at, n in expert_sources(m, e):
                    pool.dma_start(w.split[e % 2][:, 0, at:at + n].rearrange("p (c o) -> p c o", c=ap.shape[1]), ap).then_inc(sem(f"m{m}_hi"), 16)
                k = len(list(expert_sources(m, e)))
                pool.wait_ge(sem(f"m{m}_hi"), 16 * k * (e + 1))
                pool.wait_ge(sem(f"m{m}_raw"), 16 * k * (e + 1))
                pool.tensor_tensor(w.split[e % 2][:, 1], w.raw[:], w.split[e % 2][:, 0].bitcast(F32), ALU.subtract).then_inc(sem(f"m{m}_lo"), 1)

        def moe_act(act, m):
            w = moe[m]

            def x_hi(n):
                act.wait_ge(sem(f"m{m}_turned"), n)
                act.activation(w.xt[:, 0], PS[:, 4, :].rearrange("p (c g) -> p c g", c=C), ACT.Copy).then_inc(sem(f"m{m}_xhi"), 1)

            x_hi(1)
            for e in range(E):
                lo, hi = bounds(act, m, e)
                with act.Fori(lo, hi) as t:
                    for f in range(w.fc):
                        act.wait_ge(sem(f"m{m}_up"), t * w.fc + f + 1)
                        if m == 0:
                            act.activation(w.act[:, f % 2, 0], PS[:, f, 0:G], ACT.Relu).then_inc(sem(f"m{m}_act"), 1)
                        else:
                            b = e * w.fc + f
                            act.activation(w.act[:, f % 2, 0], PS[:, f, 0:G], ACT.Tanh, bias=hbg[:, b:b + 1], scale=0.5)
                            act.activation(w.act[:, f % 2, 1], PS[:, f, 0:G], ACT.Identity, bias=hbg[:, b:b + 1], scale=0.5).then_inc(sem(f"m{m}_act"), 1)
                        if f:
                            act.wait_ge(sem(f"m{m}_h"), t * w.fc + f)
                            act.activation(w.hs[:, 0, f - 1], w.h[:, f - 1], ACT.Copy).then_inc(sem(f"m{m}_hhi"), 1)
                    act.wait_ge(sem(f"m{m}_h"), t * w.fc + w.fc)
                    act.activation(w.hs[:, 0, w.fc - 1], w.h[:, w.fc - 1], ACT.Copy).then_inc(sem(f"m{m}_hhi"), 1)
                    x_hi(t + 2)
            if m == 0:
                moe_end(act, m, hi)

        def moe_dve(dve, m):
            w = moe[m]

            def x_lo(n):
                dve.wait_ge(sem(f"m{m}_xhi"), n)
                dve.tensor_tensor(w.xt[:, 1], PS[:, 4, :].rearrange("p (c g) -> p c g", c=C), w.xt[:, 0].bitcast(F32),
                                  ALU.subtract).then_inc(sem(f"m{m}_xlo"), 1)

            x_lo(1)
            for e in range(E):
                lo, hi = bounds(dve, m, e)
                with dve.Fori(lo, hi) as t:
                    for f in range(w.fc):
                        dve.wait_ge(sem(f"m{m}_act"), t * w.fc + f + 1)
                        a = w.act[:, f % 2]
                        if m == 0:
                            dve.scalar_tensor_tensor(out=w.h[:, f], in0=PS[:, f, 0:G], scalar=0.0, in1=a[:, 0],
                                                     op0=ALU.max, op1=ALU.mult).then_inc(sem(f"m{m}_h"), 1)
                        else:
                            dve.scalar_tensor_tensor(out=a[:, 0], in0=a[:, 0], scalar=1.0, in1=a[:, 1],
                                                     op0=ALU.add, op1=ALU.mult).then_inc(sem(f"m{m}_silu"), 1)
                            dve.wait_ge(sem(f"m{m}_silu"), t * w.fc + f + 1)
                            dve.scalar_tensor_tensor(out=w.h[:, f], in0=PS[:, f, G:2 * G], scalar=col("up_b", e * w.fc + f),
                                                     in1=a[:, 0], op0=ALU.add, op1=ALU.mult).then_inc(sem(f"m{m}_h"), 1)
                        if f:
                            dve.wait_ge(sem(f"m{m}_hhi"), t * w.fc + f)
                            dve.tensor_tensor(w.hs[:, 1, f - 1], w.h[:, f - 1], w.hs[:, 0, f - 1].bitcast(F32), ALU.subtract).then_inc(sem(f"m{m}_hlo"), 1)
                    dve.wait_ge(sem(f"m{m}_hhi"), t * w.fc + w.fc)
                    dve.tensor_tensor(w.hs[:, 1, w.fc - 1], w.h[:, w.fc - 1], w.hs[:, 0, w.fc - 1].bitcast(F32), ALU.subtract).then_inc(sem(f"m{m}_hlo"), 1)
                    x_lo(t + 2)
                    dve.wait_ge(sem(f"m{m}_down"), t + 1)
                    dve.wait_ge(sem(f"m{m}_yout"), 16 * t + 1)
                    if m == 0:
                        dve.tensor_copy(w.y[:], PS[:, 5:7, 0:D]).then_inc(sem(f"m{m}_y"), 1)
                    else:
                        dve.tensor_tensor(w.y[:], PS[:, 5:7, 0:D], DB[:, e].unsqueeze(1).to_broadcast([P, G // P, D]),
                                          ALU.add).then_inc(sem(f"m{m}_y"), 1)
            moe_end(dve, m, hi)

        def moe_pe(pe, m):
            w = moe[m]

            def turn_rows(n):
                pe.wait_ge(sem(f"m{m}_xg"), 16 * n)
                for c in range(C):
                    for a in range(G // P):
                        ins = pe.transpose(PS[:, 4, c * G + a * P:c * G + (a + 1) * P], w.xg[:, a, c * P:(c + 1) * P], ident[:])
                ins.then_inc(sem(f"m{m}_turned"), 1)

            turn_rows(1)
            for e in range(E):
                s = w.split[e % 2]
                pe.wait_ge(sem(f"m{m}_lo"), e + 1)
                lo, hi = bounds(pe, m, e)
                with pe.Fori(lo, hi) as t:
                    pe.wait_ge(sem(f"m{m}_xlo"), t + 1)
                    for f in range(w.fc):
                        for u in range(w.ups):
                            for c in range(C):
                                at = up_weights(m, w, u, c, f)
                                ins = product(pe, PS[:, f, u * G:(u + 1) * G], (s[:, 0, at], s[:, 1, at]),
                                              (w.xt[:, 0, c], w.xt[:, 1, c]), c == 0, c == C - 1)
                        ins.then_inc(sem(f"m{m}_up"), 1)
                    turn_rows(t + 2)
                    pe.wait_ge(sem(f"m{m}_y"), t + 1)
                    for f in range(w.fc):
                        pe.wait_ge(sem(f"m{m}_hlo"), t * w.fc + f + 1)
                        at = down_weights(m, w, f)
                        for a in range(G // P):
                            tok = slice(a * P, (a + 1) * P)
                            ins = product(pe, PS[:, 5 + a, 0:D], (w.hs[:, 0, f, tok], w.hs[:, 1, f, tok]), (s[:, 0, at], s[:, 1, at]),
                                          f == 0, f == w.fc - 1)
                    ins.then_inc(sem(f"m{m}_down"), 1)
            if m == 0:
                moe_end(pe, m, hi)

        tf = HB[0][:, 4:8, :].rearrange("p a (b k) -> p (a b) k", k=32 * E)

        def table_pe(pe, m):
            pe.wait_ge(sem("total"), m + 1)
            pe.matmul(PS[:, 7, 0:E], ones_bf[:], rbf[0][:, 0, 0], start=True, stop=True).then_inc(sem("count_ps"), 1)

        def table_dve(dve, m, step, chained):
            dve.tensor_copy(rbf[0][:, 0, 0], carry[:, 0]).then_inc(sem("total"), 1)
            dve.wait_ge(sem("total"), m + 1)
            step(dve.memset(carry[:, 0], 0.0))
            dve.wait_ge(sem("count_ps"), m + 1)
            step(dve.tensor_scalar(tfi[:, 0], PS[:, 7, 0:E], float(G - 1), None, ALU.add))
            chained()
            step(dve.tensor_scalar(tfi[:, 1], tfi[:, 0], G.bit_length() - 1, None, ALU.logical_shift_right))
            chained()
            step(dve.tensor_tensor(tf[:, 7, 0:E], PS[:, 7, 0:E], ebase[:], ALU.add))
            step(dve.tensor_copy(tf[:, 0, 0:E], tfi[:, 1]))
            chained()
            step(dve.tensor_scalar(tf[:, 1, 0:E], tf[:, 0, 0:E], 1.0, None, ALU.max))
            chained()
            step(dve.tensor_copy(tf[:, 2, 0:1], tf[:, 1, 0:1]))
            for e in range(1, E):
                chained()
                step(dve.tensor_tensor(tf[:, 2, e:e + 1], tf[:, 2, e - 1:e], tf[:, 1, e:e + 1], ALU.add))
            chained()
            step(dve.tensor_tensor(tf[:, 3, 0:E], tf[:, 2, 0:E], tf[:, 1, 0:E], ALU.subtract))
            shape = [P, 32, E]
            past = tf[:, 4].rearrange("p (t e) -> p t e", e=E)
            step(dve.tensor_tensor(past, iota_g[:].unsqueeze(2).to_broadcast(shape), tf[:, 2, 0:E].unsqueeze(1).to_broadcast(shape), ALU.is_ge))
            chained()
            step(dve.tensor_reduce(tf[:, 5, 0:32], past, AX, ALU.add))
            step(dve.tensor_tensor(tf[:, 6].rearrange("p (t e) -> p t e", e=E), past, tf[:, 1, 0:E].unsqueeze(1).to_broadcast(shape), ALU.mult))
            chained()
            step(dve.tensor_reduce(tf[:, 5, 32:64], tf[:, 6].rearrange("p (t e) -> p t e", e=E), AX, ALU.add))
            chained()
            step(dve.tensor_tensor(tf[:, 5, 64:96], iota_g[:], tf[:, 5, 32:64], ALU.subtract))
            step(dve.tensor_scalar(tf[:, 5, 0:32], tf[:, 5, 0:32], float(CAP), None, ALU.mult))
            chained()
            step(dve.scalar_tensor_tensor(out=tf[:, 5, 96:128], in0=tf[:, 5, 64:96], scalar=float(G), in1=tf[:, 5, 0:32], op0=ALU.mult, op1=ALU.add))
            chained()
            step(dve.tensor_copy(table[m][:, 2 * E + 32:3 * E + 32], tf[0:1, 7, 0:E]))
            step(dve.tensor_copy(table[m][:, 0:E], tf[0:1, 3, 0:E]))
            step(dve.tensor_copy(table[m][:, E:2 * E], tf[0:1, 2, 0:E]))
            dve.tensor_copy(table[m][:, 2 * E:2 * E + 32], tf[0:1, 5, 96:128]).then_inc(sem(f"m{m}_table"), 1)
            step(dve.scalar_tensor_tensor(out=tf[:, 0, 0:E], in0=tf[:, 3, 0:E], scalar=float(G), in1=ebase[:], op0=ALU.mult, op1=ALU.subtract))
            which = tf[:, 4].rearrange("p (q e) -> p q e", e=E)
            shape = [P, B * TT * 2, E]
            step(dve.tensor_tensor(which, iota_e[:].unsqueeze(1).to_broadcast(shape),
                                   expert_of[:].rearrange("p n j k -> p (n j k)").unsqueeze(2).to_broadcast(shape), ALU.is_equal))
            chained()
            step(dve.tensor_tensor(which, which, tf[:, 0, 0:E].unsqueeze(1).to_broadcast(shape), ALU.mult))
            chained()
            step(dve.tensor_reduce(tf[:, 1, 0:B * TT * 2], which, AX, ALU.add))
            chained()
            dve.tensor_tensor(source[:].rearrange("p n j k -> p (n j k)"), tf[:, 1, 0:B * TT * 2],
                              dest[m][:].rearrange("p n j k -> p (n j k)"), ALU.add).then_inc(sem("source"), 1)

        block = top.enter_context(nc.Block())

        @block.sync
        def _(sp):
            sp.dma_start(rowv[:], rows.partition_broadcast(P)).then_inc(sem("const_in"), 16)
            sp.dma_start(colv[:], cols).then_inc(sem("const_in"), 16)

            def load_next(n):
                if n:
                    sp.wait_ge(sem("emb"), n)
                sp.dma_start(NX[:], x[n].rearrange("(j p) d -> p j d", p=P)).then_inc(sem("next_in"), 16)
                sp.dma_start(NC[:], ctx_in[n].rearrange("(j p) d -> p j d", p=P)).then_inc(sem("next_in"), 16)

            def load_residual(n, h):
                if n >= 2:
                    sp.wait_ge(sem(f"x_out{h}"), 16 * (n // 2))
                sp.dma_start(X[h][:], x[n].rearrange("(j p) d -> p j d", p=P)).then_inc(sem(f"x_in{h}"), 16)

            load_next(0)
            for k, src in enumerate((wq, wk, wv)):
                sp.dma_start(HB[1][:, k].rearrange("p (c o) -> p c o", c=C), src.rearrange("(c p) o -> p c o", p=P)).then_inc(sem("w3_in"), 16)
            load_next(1)
            sp.dma_start(HB[0][:, 0:TT, :], pos_bias.rearrange("(i p) j -> p i j", p=P)).then_inc(sem("pb_in"), 16)
            sp.dma_start(HB[1][:, 3:7, :].rearrange("p a b -> p (a b)").rearrange("p (c o) -> p c o", c=C), w1.rearrange("(c p) o -> p c o", p=P)).then_inc(sem("w1_in"), 16)
            sp.dma_start(S2[0][:].rearrange("p j d -> p (j d)").rearrange("p (c o) -> p c o", c=C), ws1.rearrange("(c p) o -> p c o", p=P)).then_inc(sem("w1_in"), 16)
            sp.dma_start(HB[1][:, 7, 0:C * E].rearrange("p (c o) -> p c o", c=C), router1.rearrange("(c p) o -> p c o", p=P)).then_inc(sem("w1_in"), 16)
            sp.dma_start(HB[1][:, 7, C * E:2 * C * E].rearrange("p (c o) -> p c o", c=C), router2.rearrange("(c p) o -> p c o", p=P)).then_inc(sem("w1_in"), 16)
            sp.dma_start(WO[:], wo.rearrange("(c p) o -> p c o", p=P)).then_inc(sem("wplain_in"), 16)
            sp.dma_start(W2[:], w2.rearrange("(c p) o -> p c o", p=P)).then_inc(sem("wplain_in"), 16)
            sp.dma_start(WS2[:], ws2.rearrange("(c p) o -> p c o", p=P)).then_inc(sem("wplain_in"), 16)
            sp.wait_ge(sem("pool_c"), 1)
            for m in two:
                for k in range(2):
                    sp.dma_start(routed[m][E * CAP + k * G:E * CAP + (k + 1) * G].rearrange("(a p) d -> p a d", p=P), zeros[:])\
                      .then_inc(sem(f"filled{m}"), 16)
            for k in range(3):
                sp.dma_start(outputs.rearrange("(k p q a) d -> k p q (a d)", k=3, p=P, a=G // P)[k],
                             zeros[:].rearrange("p a d -> p (a d)").unsqueeze(1).to_broadcast([P, NG // 3, G // P * D]))\
                  .then_inc(sem("outputs_filled"), 16)
            for n in two:
                load_residual(n, n)
            for stage, n, h in stages_a("sp"):
                if stage == "in":
                    load_next(n)
                elif stage == "down":
                    sp.wait_ge(sem("batch_a"), n + 1)
                    sp.dma_start(x_base[0, n].rearrange("(j p) d -> p j d", p=P), X[h][:]).then_inc(sem(f"x_out{h}"), 16)
                    if n + 2 < B:
                        load_residual(n + 2, h)
            for h in two:
                sp.wait_ge(sem(f"x_out{h}"), 16 * PAIRS)
            for dst, src in ((raw_wv, Wv), (raw_q, Wq), (raw_k, Wk), (raw_wih, wih), (raw_whh, whh)):
                sp.dma_start(dst, src.rearrange("(c p) o -> p c o", p=P)).then_inc(sem("cw_raw"), 16)
            moe_sp(sp, 0)
            for pair in range(PAIRS):
                for n, h in of_pair[pair]:
                    if pair:
                        sp.wait_ge(sem("batch_c"), n - 1)
                        sp.wait_ge(sem(f"x_out{h}"), 16 * (PAIRS + pair))
                        sp.wait_ge(sem("dest"), B + n - 1)
                    sp.dma_start(X[h][:], x_base[0, n].rearrange("(j p) d -> p j d", p=P)).then_inc(sem(f"x_in{h}"), 16)
                    sp.dma_start(S0[h][:].rearrange("p c t -> p (c t)").rearrange("p (j d) -> p j d", d=D),
                                 ctx_in[n].rearrange("(j p) d -> p j d", p=P)).then_inc(sem(f"x_in{h}"), 16)
                for n, h in of_pair[pair]:
                    sp.wait_ge(sem("batch_c"), n + 1)
                    sp.dma_start(x_base[1, n].rearrange("(j p) d -> p j d", p=P), X[h][:]).then_inc(sem(f"x_out{h}"), 16)
            for h in two:
                sp.wait_ge(sem(f"x_out{h}"), 16 * 2 * PAIRS)
            sp.wait_ge(sem("dest"), 2 * B)
            sp.dma_start(DB[:], down_b.rearrange("e d -> (e d)").partition_broadcast(P).rearrange("p (e d) -> p e d", d=D)).then_inc(sem("db_in"), 16)
            moe_sp(sp, 1)
            for pair in range(PAIRS):
                for n, h in of_pair[pair]:
                    if pair:
                        sp.wait_ge(sem(f"x_out{h}"), 16 * (2 * PAIRS + pair))
                    sp.dma_start(X[h][:], x_base[1, n].rearrange("(j p) d -> p j d", p=P)).then_inc(sem(f"x_in{h}"), 16)
                for n, h in of_pair[pair]:
                    sp.wait_ge(sem("combined"), B + n + 1)
                    sp.dma_start(out[n].rearrange("(j p) d -> p j d", p=P), X[h][:]).then_inc(sem(f"x_out{h}"), 16)
            for h in two:
                sp.wait_ge(sem(f"x_out{h}"), 16 * 3 * PAIRS)

        @block.gpsimd
        def _(pool):
            pool.memset(zeros[:], 0.0).then_inc(sem("pool_c"), 1)
            pool.memset(ident[:], 0.0).then_inc(sem("pool_c"), 1)
            pool.memset(ones[:], 1.0).then_inc(sem("pool_c"), 1)
            pool.memset(minus_half[:], -0.5).then_inc(sem("pool_c"), 1)
            pool.memset(ones_bf[:], 1.0).then_inc(sem("pool_c"), 1)
            pool.memset(carry[:], 0.0).then_inc(sem("pool_c"), 1)
            pool.iota(iota_e[:], pattern=[[1, E]], base=0, channel_multiplier=0, allow_small_or_imprecise_dtypes=True).then_inc(sem("pool_c"), 1)
            pool.iota(ebase[:], pattern=[[CAP, E]], base=0, channel_multiplier=0, allow_small_or_imprecise_dtypes=True).then_inc(sem("pool_c"), 1)
            pool.iota(iota_g[:], pattern=[[1, 32]], base=0, channel_multiplier=0, allow_small_or_imprecise_dtypes=True).then_inc(sem("pool_c"), 1)
            pool.wait_ge(sem("pool_c"), 9)
            pool.affine_select(out=ident[:], in_=ident[:], compare_op=ALU.not_equal, fill=1.0, base=0,
                               pattern=[[-1, P]], channel_multiplier=1).then_inc(sem("pool_c"), 1)
            pool.affine_select(out=tri[:], in_=ones_bf[:], compare_op=ALU.is_gt, fill=0.0, base=0,
                               pattern=[[1, P]], channel_multiplier=-1).then_inc(sem("pool_c"), 1)
            pool.wait_ge(sem("pool_c"), 11)

            ln = [0]

            def power(h):
                ln[0] += 1
                pool.wait_ge(sem("var_ready"), ln[0])
                pool.tensor_tensor(rstd[h][:], ve[h][:], minus_half[:], ALU.pow).then_inc(sem("rstd_ready"), 1)

            def scatter(m, n, h):
                pool.wait_ge(sem("dest"), m * B + n + 1)
                for j in range(TT):
                    for kk in range(2):
                        pool.indirect_dma_start(out=routed[m], out_offset=bass.IndirectOffsetOnAxis(ap=dest[m][:, n, j, kk:kk + 1], axis=0),
                                                in_=S2[h][:, j], in_offset=None).then_inc(sem(f"scattered{h}"), 16)

            for h in two:
                power(h)
            pool.wait_ge(sem("pb_in"), 16)
            band = HB[0][:, 0:TT, :]
            pool.affine_select(out=band, in_=band, compare_op=ALU.is_gt, fill=0.0, base=BAND,
                               pattern=[[-P, TT], [1, T]], channel_multiplier=-1).then_inc(sem("pool_c"), 1)
            pool.wait_ge(sem("pool_c"), 12)
            pool.affine_select(out=band, in_=band, compare_op=ALU.is_gt, fill=0.0, base=BAND,
                               pattern=[[P, TT], [-1, T]], channel_multiplier=1).then_inc(sem("pool_c"), 1)
            pool.wait_ge(sem("w1_in"), 64)
            raw_w1 = HB[1][:, 3:7, :].rearrange("p a b -> p (a b)").rearrange("p (c o) -> p c o", c=C)
            raw_ws1 = S2[0][:].rearrange("p j d -> p (j d)").rearrange("p (c o) -> p c o", c=C)
            raw_r = [HB[1][:, 7, m * C * E:(m + 1) * C * E].rearrange("p (c o) -> p c o", c=C) for m in two]
            split = [(raw_r[0], rw[0][:], rw[1][:]), (raw_r[1], rw[2][:], rw[3][:]),
                     (raw_w1, W1[:, 0], W1[:, 1]), (raw_ws1, WS1[:, 0], WS1[:, 1])]
            for raw, hi, lo in split:
                pool.tensor_copy(hi, raw).then_inc(sem("pool_c"), 1)
            for k, (raw, hi, lo) in enumerate(split):
                pool.wait_ge(sem("pool_c"), 13 + k + 1)
                pool.tensor_tensor(lo, raw, hi.bitcast(F32), ALU.subtract).then_inc(sem("w1_split"), 1)

            for stage, n, h in stages_a("pool"):
                if stage == "in":
                    power(h)
                elif stage == "turn":
                    pool.wait_ge(sem("inT_ps"), n + 1)
                    pool.tensor_tensor(EMB[h][:], EMB[h][:], tiles(row("bo")), ALU.add).then_inc(sem("embo"), 1)
                elif stage == "attn":
                    power(h)
                elif stage == "aT":
                    pool.wait_ge(sem("r_norm"), n + 1)
                    if n == 0:
                        after(pool, "be1")
                    pool.tensor_tensor(S1[h][:], S2[h][:], tiles(row("gamma")), ALU.mult).then_inc(sem("atok"), 1)
                    pool.wait_ge(sem("atok"), 2 * n + 1)
                    pool.tensor_tensor(S1[h][:], S1[h][:], tiles(bb[:]), ALU.add).then_inc(sem("atok"), 1)
                    pool.wait_ge(sem(f"x_in{h}"), 16 * (n // 2 + 1))
                    pool.tensor_tensor(X[h][:], X[h][:], tiles(be1[:]), ALU.add).then_inc(sem("xbeta"), 1)
                elif stage == "ffn":
                    power(h)
                    power(h)
                elif stage == "down":
                    scatter(0, n, h)
            pool.wait_ge(sem("m0_table"), 1)
            pool.wait_ge(sem("batch_a"), B)
            for dst, src in ((VW, Wv), (WIH, wih), (WHH, whh)):
                pool.dma_start(dst[:, 0], src.rearrange("(c p) o -> p c o", p=P)).then_inc(sem("cw_hi"), 16)
            moe_pool(pool, 0)

            def gather(m, n, h):
                for j in range(TT):
                    for kk in range(2):
                        pool.indirect_dma_start(out=rows_h[h][:, kk, j], out_offset=None, in_=outputs,
                                                in_offset=bass.IndirectOffsetOnAxis(ap=source[:, n, j, kk:kk + 1], axis=0))\
                            .then_inc(sem(f"rows{h}"), 16)

            def all_stored(m):
                pool.wait_ge(sem("source"), m + 1)
                total = pool.value_load(table[m][0:1, 2 * E - 1:2 * E], min_val=1, max_val=NG)
                moe_end(pool, m, total)

            pool.wait_ge(sem("cw_hi"), 48)
            pool.wait_ge(sem("cw_raw"), 80)
            pool.tensor_tensor(VW[:, 1], raw_wv, VW[:, 0].bitcast(F32), ALU.subtract).then_inc(sem("cw_lo"), 1)
            all_stored(0)
            for pair in range(PAIRS):
                for n, h in of_pair[pair]:
                    if n == 1:
                        after(pool, "gt_ps")
                    if pair:
                        pool.wait_ge(sem("batch_c"), n - 1)
                    gather(0, n, h)
                    power(h)
                    power(h)
                if pair == 0:
                    pool.tensor_tensor(WIH[:, 1], raw_wih, WIH[:, 0].bitcast(F32), ALU.subtract).then_inc(sem("cw_lo"), 1)
                    pool.tensor_tensor(WHH[:, 1], raw_whh, WHH[:, 0].bitcast(F32), ALU.subtract).then_inc(sem("cw_lo"), 1)
                for steps in slot_steps[pair * ITERS:(pair + 1) * ITERS]:
                    for q, it, n, h in steps:
                        power(h)
                    for q, it, n, h in steps:
                        for d in range(C):
                            pool.wait_ge(sem("n_gate"), C * q + d + 1)
                            pool.tensor_tensor(gate_slot(h, d, 0), HT[h][:, d], gate_slot(h, d, 3), ALU.subtract).then_inc(sem("h_minus_n"), 1)
                for n, h in of_pair[pair]:
                    power(h)
                for n, h in of_pair[pair]:
                    scatter(1, n, h)
            pool.wait_ge(sem("m1_table"), 1)
            moe_pool(pool, 1)
            all_stored(1)
            for pair in range(PAIRS):
                for n, h in of_pair[pair]:
                    if pair:
                        pool.wait_ge(sem("combined"), B + n - 1)
                    gather(1, n, h)

        @block.scalar
        def _(act):
            for m in two:
                act.sem_inc(sem(f"m{m}_y"), 1)
                act.sem_inc(sem(f"m{m}_yout"), 1)
            act.wait_ge(sem("const_in"), 32)
            once(act.activation(tanh_g[:], rowv[:, ROWS["g"]:ROWS["g"] + 4], ACT.Tanh), "tanh_g")
            once(act.activation(hbq[:], col("bq", 0, C), ACT.Copy, scale=0.5), "hbq")
            act.wait_ge(sem("w3_in"), 48)
            raw = HB[1][:, 0:3, :]
            once(act.activation(W3[:, 0].rearrange("p w c o -> p w (c o)"), raw, ACT.Copy), "w3_hi")

            def turned_hi(m, n, h):
                act.wait_ge(sem("xnT_ps"), m * B + n + 1)
                act.activation(RT[h][:, 0], banks(h, 2), ACT.Copy).then_inc(sem("xnT_hi"), 1)

            def route_exp(m, n, h):
                act.wait_ge(sem("rt_sub"), m * B + n + 1)
                act.activation(RTM[h][:, 1], RTM[h][:, 0], ACT.Exp).then_inc(sem("rt_exp"), 1)

            for stage, n, h in stages_a("act"):
                if stage == "turn":
                    act.wait_ge(sem("inT_ps"), n + 1)
                    act.activation(RT[h][:, 0], banks(h, 0), ACT.Copy).then_inc(sem("inT_hi"), 1)
                elif stage == "qk":
                    if n == 0:
                        after(act, "wmax")
                        for i in range(TT):
                            ins = act.activation(HB[0][:, i], HB[0][:, i], ACT.Exp, bias=wmax[:, i:i + 1])
                        once(ins, "ew")
                        after(act, "hbq")
                        after(act, "ewT_ps")
                    if n == 1:
                        act.wait_ge(sem("w1_split"), 4)
                    act.wait_ge(sem("qk_ps"), 2 * n + 1)
                    for c in range(C):
                        ins = act.activation(HB[h][:, 6 + c], bank(h, c), ACT.Tanh, bias=hbq[:, c:c + 1], scale=0.5)
                    ins.then_inc(sem("th"), 1)
                    act.wait_ge(sem("kbias"), n + 1)
                    for c in range(C):
                        ins = act.activation(S0[h][:, c], bank(h, 2 + c), ACT.Exp, bias=kb[h][:, 1, c:c + 1])
                    ins.then_inc(sem("ekT"), 1)
                elif stage == "v":
                    act.wait_ge(sem("ek_ps"), n + 1)
                    act.activation(HB[h][:, 0:2], banks(h, 2), ACT.Copy).then_inc(sem("ek"), 1)
                elif stage == "aT":
                    act.wait_ge(sem("aT_ps"), n + 1)
                    for c in range(C):
                        act.activation(RT[h][:, 0, c], bank(h, 2 + c), ACT.Identity, bias=col("beta", c), scale=col("gamma", c))
                        act.activation(S0[h][:, c], bank(h, 2 + c), ACT.Identity, bias=col("beta", c), scale=col("gamma", c))\
                           .then_inc(sem("aT"), 1)
                elif stage == "hid":
                    for m in range(0, HC, 2):
                        act.wait_ge(sem("hid_ps"), HC * n + m + 1)
                        act.activation(HB[h][:, m], bank(h, m % 4), ACT.Relu, bias=col("b1", m)).then_inc(sem("hid_act"), 1)
                elif stage == "xnT":
                    turned_hi(0, n, h)
                elif stage == "logits":
                    route_exp(0, n, h)
                elif stage == "up":
                    for f in range(SC):
                        act.wait_ge(sem("sh_ps"), SC * n + f + 1)
                        act.activation(HB[h][:, f], bank(h, 2 + f % 2), ACT.Relu).then_inc(sem("sh_relu"), 1)
                        act.wait_ge(sem("sh_relu"), SC * n + f + 1)
                        act.activation(HB[h][:, f], HB[h][:, f], ACT.Square).then_inc(sem("sh_sq"), 1)

            act.wait_ge(sem("m0_table"), 1)
            moe_act(act, 0)

            after(act, "gt_ps")
            once(act.activation(GT[:, 0], PS[:, 7, :].rearrange("p (c o) -> p c o", c=C), ACT.Copy), "gt_hi")
            for pair in range(PAIRS):
                for n, h in of_pair[pair]:
                    act.wait_ge(sem("inT_ps"), B + n + 1)
                    for c in range(C):
                        act.activation(S0[h][:, c], bank(h, c), ACT.Copy, scale=col("w_in", c))
                        ins = act.activation(RT[h][:, 0, c], bank(h, c), ACT.Copy, scale=col("w_in", c))
                    ins.then_inc(sem("inT_hi"), 1)
                    act.wait_ge(sem("aT_ps"), B + n + 1)
                    act.activation(HT[h][:], banks(h, 2), ACT.Copy).then_inc(sem("slot_new"), 1)
                    act.activation(HTS[h][:, 0], banks(h, 2), ACT.Copy).then_inc(sem("slot_hi"), 1)
                for n, h in of_pair[pair]:
                    act.wait_ge(sem("kk_ps"), n + 1)
                    act.wait_ge(sem("inT_lo"), B + n + 1)
                    for c in range(C):
                        act.activation(S0[h][:, c], bank(h, c), ACT.Copy, scale=col("w_slot", c))
                        ins = act.activation(KK[h][:, 0, c], bank(h, c), ACT.Copy, scale=col("w_slot", c))
                    ins.then_inc(sem("kk_hi"), 1)
                    act.wait_ge(sem("v_ps"), B + n + 1)
                    act.activation(EMB[h][:], token_banks(h, 2), ACT.Copy).then_inc(sem("v_out"), 1)
                for steps in slot_steps[pair * ITERS:(pair + 1) * ITERS]:
                    for q, it, n, h in steps:
                        if it == 0:
                            act.wait_ge(sem("kk_lo"), n + 1)
                            act.wait_ge(sem("slot_new"), slot_count(n, it))
                        else:
                            act.wait_ge(sem("slot_new"), slot_count(n, it))
                        act.activation(S0[h][:], HT[h][:], ACT.Square).then_inc(sem("slot_sq"), 1)
                    for q, it, n, h in steps:
                        act.wait_ge(sem("sn"), q + 1)
                        act.activation(RT[h][:, 0], S0[h][:], ACT.Copy).then_inc(sem("sn_hi"), 1)
                    for q, it, n, h in steps:
                        if q == 0:
                            act.wait_ge(sem("cw_lo"), 3)
                        for j in range(TT):
                            act.wait_ge(sem("smax"), TT * q + j + 1)
                            act.activation(HB[h][:, j], bank(h, j), ACT.Exp, bias=SM[h][:, 1, j:j + 1], scale=1.0 / 16,
                                           accum_out=SM[h][:, 2, j:j + 1]).then_inc(sem("sexp"), 1)
                    for q, it, n, h in steps:
                        act.wait_ge(sem("uT_ps"), q + 1)
                        act.activation(RT[h][:, 0], banks(h, 0), ACT.Copy).then_inc(sem("uT_hi"), 1)
                    for q, it, n, h in steps:
                        for d in range(C):
                            g = 4 * (C * q + d)
                            act.wait_ge(sem("gru_ps"), g + 1)
                            act.activation(gate_slot(h, d, 1), bank(h, 0), ACT.Identity, bias=gbias[:, 4 + d:5 + d], scale=0.5).then_inc(sem("hn_out"), 1)
                            act.wait_ge(sem("gru_ps"), g + 2)
                            act.activation(gate_slot(h, d, 0), bank(h, 2), ACT.Tanh, bias=gbias[:, d:d + 1], scale=0.5).then_inc(sem("r_out"), 1)
                            act.wait_ge(sem("gru_ps"), g + 4)
                            act.activation(gate_slot(h, d, 2), bank(h, 3), ACT.Tanh, bias=gbias[:, 2 + d:3 + d], scale=0.5).then_inc(sem("z_out"), 1)
                            act.wait_ge(sem("xn_out"), C * q + d + 1)
                            act.activation(gate_slot(h, d, 3), gate_slot(h, d, 3), ACT.Tanh, bias=col("bih", 4 + d)).then_inc(sem("n_gate"), 1)
                    if steps[0][1] < ITERS - 1:
                        for q, it, n, h in steps:
                            act.wait_ge(sem("slot_new"), slot_count(n, it + 1))
                            act.activation(HTS[h][:, 0], HT[h][:], ACT.Copy).then_inc(sem("slot_hi"), 1)
                for n, h in of_pair[pair]:
                    turned_hi(1, n, h)
                for n, h in of_pair[pair]:
                    route_exp(1, n, h)
            act.wait_ge(sem("m1_table"), 1)
            once(act.activation(hbg[:], col("gate_b", 0, E * F2 // P), ACT.Copy, scale=0.5), "hbg")
            after(act, "hbg")
            moe_act(act, 1)

        @block.vector
        def _(dve):
            k = [0]

            def step(ins):
                k[0] += 1
                ins.then_inc(sem("dve_step"), 1)

            def chained():
                dve.wait_ge(sem("dve_step"), k[0])

            ln = [0]

            def normalise(h, src, dst, eps, final):
                for j in range(TT):
                    ins = dve.bn_stats(st6[h][:, j], src[:, j])
                step(ins)
                chained()
                for j in range(TT):
                    ins = dve.bn_aggr(mv[h][:, j], st6[h][:, j])
                step(ins)
                chained()
                dve.tensor_scalar(ve[h][:], mv[h][:, :, 1], eps, None, ALU.add).then_inc(sem("var_ready"), 1)
                ln[0] += 1
                dve.wait_ge(sem("rstd_ready"), ln[0])
                for j in range(TT):
                    ins = dve.tensor_scalar(dst[:, j], src[:, j], mv[h][:, j, 0:1], rstd[h][:, j:j + 1], ALU.subtract, ALU.mult)
                final(ins)

            def lo_part(h, ps, name):
                dve.tensor_tensor(RT[h][:, 1], ps, RT[h][:, 0].bitcast(F32), ALU.subtract).then_inc(sem(name), 1)

            def choose(m, n, h, eps, gate):
                R = RTM[h]
                lg = bank(h, 0)[:, 0:TT * E].rearrange("p (j e) -> p j e", e=E)
                q = m * B + n
                dve.wait_ge(sem("logits_ps"), q + 1)
                step(dve.tensor_reduce(R[:, 7, :, 0], lg, AX, ALU.max))
                chained()
                dve.tensor_tensor(R[:, 0], lg, R[:, 7, :, 0:1].to_broadcast([P, TT, E]), ALU.subtract).then_inc(sem("rt_sub"), 1)
                dve.wait_ge(sem("rt_exp"), q + 1)
                step(dve.tensor_reduce(R[:, 7, :, 1], R[:, 1], AX, ALU.add))
                chained()
                step(dve.reciprocal(R[:, 7, :, 2], R[:, 7, :, 1]))
                chained()
                step(dve.tensor_tensor(R[:, 1], R[:, 1], R[:, 7, :, 2:3].to_broadcast([P, TT, E]), ALU.mult))
                chained()
                for j in range(TT):
                    ins = dve.max(R[:, 2, j], R[:, 1, j])
                step(ins)
                chained()
                for j in range(TT):
                    ins = dve.max_index(rix[h][:, j], R[:, 2, j], R[:, 1, j])
                step(ins)
                chained()
                step(dve.tensor_copy(R[:, 3, :, 0:2], rix[h][:, :, 0:2]))
                step(dve.tensor_copy(expert_of[:, n], rix[h][:, :, 0:2]))
                chained()
                for kk in range(2):
                    step(dve.tensor_tensor(R[:, 4 + kk], iota_e[:].unsqueeze(1).to_broadcast([P, TT, E]),
                                           R[:, 3, :, kk:kk + 1].to_broadcast([P, TT, E]), ALU.is_equal))
                step(dve.tensor_tensor(R[:, 7, :, 3], R[:, 2, :, 0], R[:, 2, :, 1], ALU.add))
                chained()
                step(dve.tensor_tensor(R[:, 6], R[:, 4], R[:, 5], ALU.add))
                step(dve.tensor_scalar(R[:, 7, :, 4], R[:, 7, :, 3], eps, None, ALU.add))
                chained()
                step(dve.tensor_copy(rbf[h][:, 0], R[:, 6]))
                for j in range(TT):
                    step(dve.tensor_tensor(carry[:, j + 1], carry[:, j], R[:, 6, j], ALU.add))
                    chained()
                dve.tensor_copy(rbf[h][:, 1], carry[:, 0:TT]).then_inc(sem("chosen"), 1)
                step(dve.reciprocal(R[:, 7, :, 5], R[:, 7, :, 4]))
                chained()
                step(dve.tensor_scalar(R[:, 7, :, 6], R[:, 7, :, 5], tanh_g[:, gate:gate + 1], None, ALU.mult))
                chained()
                step(dve.tensor_tensor(share[m][:, n], R[:, 2, :, 0:2], R[:, 7, :, 6:7].to_broadcast([P, TT, 2]), ALU.mult))
                dve.wait_ge(sem("chosen"), q + 1)
                step(dve.tensor_copy(carry[:, 0], carry[:, TT]))

            def place(m, n, h):
                R = RTM[h]
                q = m * B + n
                dve.wait_ge(sem("rank_ps"), q + 1)
                rank = bank(h, 1)[:, 0:TT * E].rearrange("p (j e) -> p j e", e=E)
                step(dve.tensor_tensor(R[:, 0], rank, ebase[:].unsqueeze(1).to_broadcast([P, TT, E]), ALU.add))
                chained()
                for kk in range(2):
                    step(dve.tensor_tensor(R[:, 4 + kk], R[:, 4 + kk], R[:, 0], ALU.mult))
                    chained()
                    step(dve.tensor_reduce(R[:, 3, :, kk], R[:, 4 + kk], AX, ALU.add))
                    chained()
                dve.tensor_copy(dest[m][:, n], R[:, 3, :, 0:2]).then_inc(sem("dest"), 1)

            def turned_lo(m, n, h):
                dve.wait_ge(sem("xnT_hi"), m * B + n + 1)
                lo_part(h, banks(h, 2), "xnT_lo")

            def embed(n, h):
                dve.wait_ge(sem("next_in"), 32 * (n + 1))
                if n >= 2:
                    dve.wait_ge(sem("embo"), n - 1)
                    dve.wait_ge(sem("ffn_ps"), n - 1)
                normalise(h, NX, S1[h], 1e-5, step)
                chained()
                dve.tensor_tensor(EMB[h][:], S1[h][:], NC[:], ALU.add).then_inc(sem("emb"), 1)

            dve.wait_ge(sem("pool_c"), 11)
            for h in two:
                embed(h, h)
            after(dve, "w3_hi")
            once(dve.tensor_tensor(W3[:, 1].rearrange("p w c o -> p w (c o)"), HB[1][:, 0:3, :],
                                   W3[:, 0].rearrange("p w c o -> p w (c o)").bitcast(F32), ALU.subtract), "w3_split")
            after(dve, "tanh_g")
            once(dve.tensor_tensor(bb[:], row("beta"), row("b2"), ALU.add), "bb")
            once(dve.tensor_scalar(g1[:], row("gamma"), tanh_g[:, 0:1], None, ALU.mult), "g1")
            once(dve.tensor_scalar(be1[:], row("beta"), tanh_g[:, 0:1], None, ALU.mult), "be1")
            for stage, n, h in stages_a("dve"):
                if stage == "in":
                    embed(n, h)
                elif stage == "turn":
                    dve.wait_ge(sem("inT_hi"), n + 1)
                    lo_part(h, banks(h, 0), "inT_lo")
                elif stage == "qk":
                    if n == 0:
                        dve.wait_ge(sem("pool_c"), 13)
                        once(dve.tensor_reduce(wmax[:], HB[0][:, 0:TT, :], AX, ALU.max), "row_max")
                        after(dve, "row_max")
                        once(dve.tensor_scalar(wmax[:], wmax[:], -1.0, None, ALU.mult), "wmax")
                        after(dve, "ewT_ps")
                        once(dve.tensor_copy(EWT[:], banks(1, 0, 4)), "ewT")
                    dve.wait_ge(sem("qk_ps"), 2 * n + 2)
                    step(dve.tensor_reduce(kb[h][:, 0], banks(h, 2), AX, ALU.max))
                    chained()
                    step(dve.tensor_tensor(kb[h][:, 0], kb[h][:, 0], col("bk", 0, C), ALU.add))
                    chained()
                    dve.tensor_tensor(kb[h][:, 1], col("bk", 0, C), kb[h][:, 0], ALU.subtract).then_inc(sem("kbias"), 1)
                    dve.wait_ge(sem("th"), n + 1)
                    step(dve.tensor_scalar(HB[h][:, 6:8], HB[h][:, 6:8], 0.5, 0.5, ALU.mult, ALU.add))
                elif stage == "v":
                    dve.wait_ge(sem("v_ps"), n + 1)
                    dve.wait_ge(sem("ek"), n + 1)
                    dve.tensor_tensor(HB[h][:, 2:4], HB[h][:, 0:2], banks(h, 0), ALU.mult).then_inc(sem("ekv"), 1)
                elif stage == "den":
                    dve.wait_ge(sem("den_ps"), n + 1)
                    step(dve.reciprocal(S0[h][:], banks(h, 2)))
                elif stage == "num":
                    dve.wait_ge(sem("num_ps"), n + 1)
                    chained()
                    step(dve.tensor_tensor(S0[h][:], banks(h, 0), S0[h][:], ALU.mult))
                    chained()
                    for c in range(C):
                        ins = dve.scalar_tensor_tensor(out=HB[h][:, 4 + c], in0=S0[h][:, c], scalar=col("bv", c),
                                                       in1=HB[h][:, 6 + c], op0=ALU.add, op1=ALU.mult)
                    ins.then_inc(sem("yT"), 1)
                elif stage == "attn":
                    dve.wait_ge(sem("attn_ps"), n + 1)
                    dve.wait_ge(sem("embo"), n + 1)
                    step(dve.tensor_tensor(S1[h][:], token_banks(h, 0), EMB[h][:], ALU.add))
                    chained()
                    if n < 2:
                        dve.wait_ge(sem("w1_split"), 4)
                    else:
                        dve.wait_ge(sem(f"scattered{h}"), 16 * 2 * TT * (n // 2))
                    normalise(h, S1[h], S2[h], 1e-5, lambda ins: ins.then_inc(sem("r_norm"), 1))
                elif stage == "aT":
                    for c in range(C):
                        dve.wait_ge(sem("aT"), C * n + c + 1)
                        dve.tensor_tensor(RT[h][:, 1, c], S0[h][:, c], RT[h][:, 0, c].bitcast(F32), ALU.subtract).then_inc(sem("aT_lo"), 1)
                elif stage == "hid":
                    for m in range(1, HC, 2):
                        dve.wait_ge(sem("hid_ps"), HC * n + m + 1)
                        dve.tensor_scalar(HB[h][:, m], bank(h, m % 4), col("b1", m), 0.0, ALU.add, ALU.max).then_inc(sem("hid_dve"), 1)
                elif stage == "ffn":
                    dve.wait_ge(sem("ffn_ps"), n + 1)
                    dve.wait_ge(sem("atok"), 2 * n + 2)
                    step(dve.tensor_tensor(S2[h][:], token_banks(h, 0), S1[h][:], ALU.add))
                    chained()
                    normalise(h, S2[h], S1[h], 1e-5, step)
                    chained()
                    dve.wait_ge(sem("xbeta"), n + 1)
                    step(dve.tensor_tensor(S1[h][:], S1[h][:], tiles(g1[:]), ALU.mult))
                    chained()
                    step(dve.tensor_tensor(X[h][:], X[h][:], S1[h][:], ALU.add))
                    chained()
                    normalise(h, X[h], S2[h], 1e-5, lambda ins: ins.then_inc(sem("xn"), 1))
                elif stage == "xnT":
                    turned_lo(0, n, h)
                elif stage == "logits":
                    choose(0, n, h, 0.0, 2)
                elif stage == "rank":
                    place(0, n, h)
                elif stage == "down":
                    dve.wait_ge(sem("shared_ps"), n + 1)
                    dve.scalar_tensor_tensor(out=X[h][:].rearrange("p j d -> p (j d)"), in0=banks(h, 2).rearrange("p b t -> p (b t)"),
                                             scalar=tanh_g[:, 2:3],
                                             in1=X[h][:].rearrange("p j d -> p (j d)"), op0=ALU.mult, op1=ALU.add)\
                       .then_inc(sem("batch_a"), 1)
            table_dve(dve, 0, step, chained)
            dve.wait_ge(sem("m0_table"), 1)
            moe_dve(dve, 0)

            def combine(m, n, h):
                dve.wait_ge(sem(f"x_in{h}"), 16 * PAIRS + (32 * (n // 2 + 1) if m == 0 else 32 * PAIRS + 16 * (n // 2 + 1)))
                dve.wait_ge(sem(f"rows{h}"), 16 * 2 * TT * (m * PAIRS + n // 2 + 1))
                for kk in range(2):
                    for j in range(TT):
                        ins = dve.scalar_tensor_tensor(out=X[h][:, j], in0=rows_h[h][:, kk, j], scalar=share[m][:, n, j, kk:kk + 1],
                                                       in1=X[h][:, j], op0=ALU.mult, op1=ALU.add)
                        if kk == 1 and j == TT - 1:
                            ins.then_inc(sem("combined"), 1)
                        elif j == TT - 1:
                            step(ins)
                            chained()

            after(dve, "gt_hi")
            once(dve.tensor_tensor(GT[:, 1], PS[:, 7, :].rearrange("p (c o) -> p c o", c=C), GT[:, 0].bitcast(F32), ALU.subtract), "gt_lo")
            step(dve.tensor_tensor(gbias[:, 0:4], col("bih", 0, 4), col("bhh", 0, 4), ALU.add))
            chained()
            step(dve.tensor_scalar(gbias[:, 0:4], gbias[:, 0:4], 0.5, None, ALU.mult))
            once(dve.tensor_scalar(gbias[:, 4:6], col("bhh", 4, 2), 0.5, None, ALU.mult), "gbias")
            for pair in range(PAIRS):
                for n, h in of_pair[pair]:
                    combine(0, n, h)
                    dve.wait_ge(sem("combined"), n + 1)
                    normalise(h, X[h], S1[h], 1e-5, lambda ins: ins.then_inc(sem("slot0"), 1))
                    ctx_t = S0[h][:].rearrange("p c t -> p (c t)").rearrange("p (j d) -> p j d", d=D)
                    dve.wait_ge(sem("slot0"), n + 1)
                    for j in range(TT):
                        ins = dve.bn_stats(st6[h][:, j], ctx_t[:, j])
                    step(ins)
                    chained()
                    for j in range(TT):
                        ins = dve.bn_aggr(mv[h][:, j], st6[h][:, j])
                    step(ins)
                    chained()
                    step(dve.tensor_tensor(SM[h][:, 0], mv[h][:, :, 0], mv[h][:, :, 0], ALU.mult))
                    chained()
                    dve.scalar_tensor_tensor(out=ve[h][:], in0=mv[h][:, :, 1], scalar=1e-6, in1=SM[h][:, 0], op0=ALU.add, op1=ALU.add)\
                       .then_inc(sem("var_ready"), 1)
                    ln[0] += 1
                    dve.wait_ge(sem("rstd_ready"), ln[0])
                    for j in range(TT):
                        ins = dve.tensor_scalar(S2[h][:, j], ctx_t[:, j], rstd[h][:, j:j + 1], None, ALU.mult)
                    ins.then_inc(sem("pn"), 1)
                for n, h in of_pair[pair]:
                    dve.wait_ge(sem("inT_hi"), B + n + 1)
                    dve.tensor_tensor(RT[h][:, 1], S0[h][:], RT[h][:, 0].bitcast(F32), ALU.subtract).then_inc(sem("inT_lo"), 1)
                    dve.wait_ge(sem("slot_hi"), slot_hi_count(n, 0))
                    dve.tensor_tensor(HTS[h][:, 1], banks(h, 2), HTS[h][:, 0].bitcast(F32), ALU.subtract).then_inc(sem("slot_lo"), 1)
                for n, h in of_pair[pair]:
                    dve.wait_ge(sem("kk_hi"), n + 1)
                    dve.tensor_tensor(KK[h][:, 1], S0[h][:], KK[h][:, 0].bitcast(F32), ALU.subtract).then_inc(sem("kk_lo"), 1)
                for steps in slot_steps[pair * ITERS:(pair + 1) * ITERS]:
                    for q, it, n, h in steps:
                        dve.wait_ge(sem("ss_ps"), q + 1)
                        dve.tensor_scalar(ve[h][:], bank(h, 0)[:, 0:TT], 1.0 / D, 1e-6, ALU.mult, ALU.add).then_inc(sem("var_ready"), 1)
                        ln[0] += 1
                        dve.wait_ge(sem("rstd_ready"), ln[0])
                        for j in range(TT):
                            ins = dve.tensor_scalar(S1[h][:].rearrange("p j d -> p (j d)")[:, j * P:(j + 1) * P], ident[:], rstd[h][:, j:j + 1], None, ALU.mult)
                        ins.then_inc(sem("diag"), 1)
                    for q, it, n, h in steps:
                        dve.wait_ge(sem("rsb_ps"), q + 1)
                        dve.tensor_tensor(S0[h][:], HT[h][:], bank(h, 1).unsqueeze(1).to_broadcast([P, C, T]), ALU.mult).then_inc(sem("sn"), 1)
                    for q, it, n, h in steps:
                        dve.wait_ge(sem("sn_hi"), q + 1)
                        dve.tensor_tensor(RT[h][:, 1], S0[h][:], RT[h][:, 0].bitcast(F32), ALU.subtract).then_inc(sem("sn_lo"), 1)
                    for q, it, n, h in steps:
                        for j in range(TT):
                            dve.wait_ge(sem("score_ps"), TT * q + j + 1)
                            step(dve.tensor_reduce(SM[h][:, 0, j:j + 1], bank(h, j), AX, ALU.max))
                            chained()
                            dve.tensor_scalar(SM[h][:, 1, j:j + 1], SM[h][:, 0, j:j + 1], -1.0 / 16, None, ALU.mult).then_inc(sem("smax"), 1)
                        dve.wait_ge(sem("sexp"), TT * (q + 1))
                        if it == 0:
                            dve.wait_ge(sem("v_out"), n + 1)
                        step(dve.reciprocal(SM[h][:, 3], SM[h][:, 2]))
                        chained()
                        dve.tensor_copy(VP[h][:, :, D:D + 1], SM[h][:, 3].unsqueeze(2))
                        for j in range(TT):
                            ins = dve.tensor_scalar(VP[h][:, j, 0:D], EMB[h][:, j], SM[h][:, 3, j:j + 1], None, ALU.mult)
                        ins.then_inc(sem("vp"), 1)
                    for q, it, n, h in steps:
                        dve.wait_ge(sem("upd_ps"), q + 1)
                        step(dve.tensor_scalar(SM[h][:, 0], banks(h, 0, TT)[:, :, D], 1e-6, None, ALU.add))
                        chained()
                        step(dve.reciprocal(SM[h][:, 4], SM[h][:, 0]))
                        chained()
                        for j in range(TT):
                            ins = dve.tensor_scalar(S2[h][:, j], bank(h, j)[:, 0:D], SM[h][:, 4, j:j + 1], None, ALU.mult)
                        ins.then_inc(sem("upd"), 1)
                    for q, it, n, h in steps:
                        dve.wait_ge(sem("uT_hi"), q + 1)
                        lo_part(h, banks(h, 0), "uT_lo")
                    for q, it, n, h in steps:
                        for d in range(C):
                            g = 4 * (C * q + d)
                            dve.wait_ge(sem("r_out"), C * q + d + 1)
                            step(dve.scalar_tensor_tensor(out=gate_slot(h, d, 3), in0=gate_slot(h, d, 0), scalar=1.0, in1=gate_slot(h, d, 1), op0=ALU.add, op1=ALU.mult))
                            chained()
                            dve.wait_ge(sem("gru_ps"), g + 3)
                            dve.tensor_tensor(gate_slot(h, d, 3), bank(h, 1), gate_slot(h, d, 3), ALU.add).then_inc(sem("xn_out"), 1)
                        for d in range(C):
                            dve.wait_ge(sem("h_minus_n"), C * q + d + 1)
                            dve.wait_ge(sem("z_out"), C * q + d + 1)
                            step(dve.scalar_tensor_tensor(out=gate_slot(h, d, 1), in0=gate_slot(h, d, 2), scalar=1.0, in1=gate_slot(h, d, 0), op0=ALU.add, op1=ALU.mult))
                            chained()
                            ins = dve.scalar_tensor_tensor(out=HT[h][:, d], in0=gate_slot(h, d, 1), scalar=0.5, in1=gate_slot(h, d, 3), op0=ALU.mult, op1=ALU.add)
                        ins.then_inc(sem("slot_new"), 1)
                    if steps[0][1] < ITERS - 1:
                        for q, it, n, h in steps:
                            dve.wait_ge(sem("slot_hi"), slot_hi_count(n, it + 1))
                            dve.tensor_tensor(HTS[h][:, 1], HT[h][:], HTS[h][:, 0].bitcast(F32), ALU.subtract).then_inc(sem("slot_lo"), 1)
                for n, h in of_pair[pair]:
                    dve.wait_ge(sem("final_ps"), n + 1)
                    step(dve.scalar_tensor_tensor(out=X[h][:].rearrange("p j d -> p (j d)"), in0=banks(h, 0).rearrange("p b t -> p (b t)"),
                                                  scalar=tanh_g[:, 1:2], in1=X[h][:].rearrange("p j d -> p (j d)"), op0=ALU.mult, op1=ALU.add))
                    chained()
                    normalise(h, X[h], S2[h], 1e-5, lambda ins: ins.then_inc(sem("batch_c"), 1))
                for n, h in of_pair[pair]:
                    turned_lo(1, n, h)
                for n, h in of_pair[pair]:
                    choose(1, n, h, 1e-9, 3)
                for n, h in of_pair[pair]:
                    place(1, n, h)
            table_dve(dve, 1, step, chained)
            dve.wait_ge(sem("m1_table"), 1)
            dve.wait_ge(sem("db_in"), 16)
            moe_dve(dve, 1)
            for pair in range(PAIRS):
                for n, h in of_pair[pair]:
                    combine(1, n, h)

        @block.tensor
        def _(pe):
            def turn(h, k, src, name):
                for c in range(C):
                    for j in range(TT):
                        ins = pe.transpose(bank(h, k + c)[:, j * P:(j + 1) * P], src[:, j, c * P:(c + 1) * P], ident[:])
                ins.then_inc(sem(name), 1)

            def parts(t, *at):
                return tuple(t[(slice(None), i) + at] for i in two)

            def turn_xn(m, n, h, ready):
                pe.wait_ge(sem(ready), n + 1)
                turn(h, 2, S2[h], "xnT_ps")

            def logits(m, n, h):
                pe.wait_ge(sem("xnT_lo"), m * B + n + 1)
                for j in range(TT):
                    for c in range(C):
                        ins = product(pe, bank(h, 0)[:, j * E:(j + 1) * E], parts(RT[h], c, slice(j * P, (j + 1) * P)),
                                      (rw[2 * m][:, c], rw[2 * m + 1][:, c]), c == 0, c == C - 1)
                ins.then_inc(sem("logits_ps"), 1)

            def ranks(m, n, h):
                pe.wait_ge(sem("chosen"), m * B + n + 1)
                pe.matmul(bank(h, 1)[:, 0:TT * E], tri[:], rbf[h][:, 0].rearrange("p j e -> p (j e)"), start=True, stop=False)
                pe.matmul(bank(h, 1)[:, 0:TT * E], ones_bf[:], rbf[h][:, 1].rearrange("p j e -> p (j e)"), start=False, stop=True)\
                  .then_inc(sem("rank_ps"), 1)

            pe.wait_ge(sem("pool_c"), 11)
            for stage, n, h in stages_a("pe"):
                if stage == "turn":
                    pe.wait_ge(sem("emb"), n + 1)
                    if n >= 2:
                        pe.wait_ge(sem("dest"), n - 1)
                    turn(h, 0, EMB[h], "inT_ps")
                elif stage == "qk":
                    if n == 0:
                        after(pe, "w3_split")
                    if n == 1:
                        after(pe, "ewT")
                    if n >= 2:
                        pe.wait_ge(sem("batch_a"), n - 1)
                    pe.wait_ge(sem("inT_lo"), n + 1)
                    for w in range(2):
                        for c in range(C):
                            for c2 in range(C):
                                ins = product(pe, bank(h, 2 * w + c), parts(W3, w, c2, slice(c * P, (c + 1) * P)),
                                              parts(RT[h], c2), c2 == 0, c2 == C - 1)
                        ins.then_inc(sem("qk_ps"), 1)
                    if n == 0:
                        after(pe, "ew")
                        pe.wait_ge(sem("inT_lo"), 2)
                        for jc in range(TT):
                            for i in range(TT):
                                ins = pe.transpose(bank(1, jc)[:, i * P:(i + 1) * P], HB[0][:, i, jc * P:(jc + 1) * P], ident[:])
                        once(ins, "ewT_ps")
                elif stage == "v":
                    pe.wait_ge(sem("th"), n + 1)
                    for j in range(TT):
                        for c in range(C):
                            ins = product(pe, token_banks(h, 0)[:, j], parts(RT[h], c, slice(j * P, (j + 1) * P)),
                                          parts(W3, 2, c), c == 0, c == C - 1)
                    ins.then_inc(sem("v_ps"), 1)
                    pe.wait_ge(sem("ekT"), n + 1)
                    for j in range(TT):
                        for c in range(C):
                            ins = pe.transpose(token_banks(h, 2)[:, j, c * P:(c + 1) * P], S0[h][:, c, j * P:(j + 1) * P], ident[:])
                    ins.then_inc(sem("ek_ps"), 1)
                elif stage in ("den", "num"):
                    pe.wait_ge(sem("ek" if stage == "den" else "ekv"), n + 1)
                    if n == 0:
                        after(pe, "ewT")
                    b, src = (2, 0) if stage == "den" else (0, 2)
                    w = HB[h][:, src:src + 2].rearrange("p b (a d) -> p (b a) d", d=D)
                    for c in range(C):
                        for j in range(TT):
                            ins = pe.matmul(bank(h, b + c), w[:, j, c * P:(c + 1) * P], EWT[:, j], start=j == 0, stop=j == TT - 1)
                    ins.then_inc(sem(f"{stage}_ps"), 1)
                elif stage == "attn":
                    pe.wait_ge(sem("yT"), n + 1)
                    if n == 0:
                        pe.wait_ge(sem("wplain_in"), 48)
                    for j in range(TT):
                        for c in range(C):
                            ins = pe.matmul(token_banks(h, 0)[:, j], HB[h][:, 4 + c, j * P:(j + 1) * P], WO[:, c], start=c == 0, stop=c == C - 1)
                    ins.then_inc(sem("attn_ps"), 1)
                elif stage == "aT":
                    pe.wait_ge(sem("r_norm"), n + 1)
                    turn(h, 2, S2[h], "aT_ps")
                elif stage == "hid":
                    pe.wait_ge(sem("aT_lo"), C * (n + 1))
                    for m in range(HC):
                        if m >= 4:
                            pe.wait_ge(sem("hid_dve" if m % 2 else "hid_act"), HC // 2 * n + (m - 4) // 2 + 1)
                        for c in range(C):
                            ins = product(pe, bank(h, m % 4), parts(W1, c, slice(m * P, (m + 1) * P)), parts(RT[h], c), c == 0, c == C - 1)
                        ins.then_inc(sem("hid_ps"), 1)
                elif stage == "ffn":
                    pe.wait_ge(sem("hid_act"), HC // 2 * (n + 1))
                    pe.wait_ge(sem("hid_dve"), HC // 2 * (n + 1))
                    for j in range(TT):
                        for m in range(HC):
                            ins = pe.matmul(token_banks(h, 0)[:, j], HB[h][:, m, j * P:(j + 1) * P], W2[:, m], start=m == 0, stop=m == HC - 1)
                    ins.then_inc(sem("ffn_ps"), 1)
                elif stage == "xnT":
                    turn_xn(0, n, h, "xn")
                elif stage == "logits":
                    logits(0, n, h)
                elif stage == "up":
                    for f in range(SC):
                        if f >= 2:
                            pe.wait_ge(sem("sh_relu"), SC * n + f - 1)
                        for c in range(C):
                            ins = product(pe, bank(h, 2 + f % 2), parts(WS1, c, slice(f * P, (f + 1) * P)), parts(RT[h], c), c == 0, c == C - 1)
                        ins.then_inc(sem("sh_ps"), 1)
                elif stage == "rank":
                    ranks(0, n, h)
                elif stage == "down":
                    pe.wait_ge(sem("sh_sq"), SC * (n + 1))
                    for j in range(TT):
                        for f in range(SC):
                            ins = pe.matmul(token_banks(h, 2)[:, j], HB[h][:, f, j * P:(j + 1) * P], WS2[:, f], start=f == 0, stop=f == SC - 1)
                    ins.then_inc(sem("shared_ps"), 1)
            table_pe(pe, 0)
            pe.wait_ge(sem("m0_table"), 1)
            moe_pe(pe, 0)

            pe.wait_ge(sem("cw_raw"), 80)
            for c in range(C):
                for o in range(C):
                    ins = pe.matmul(PS[:, 7, c * D:(c + 1) * D], raw_k[:, o, c * P:(c + 1) * P], raw_q[:, o], start=o == 0, stop=o == C - 1)
            once(ins, "gt_ps")
            for pair in range(PAIRS):
                for n, h in of_pair[pair]:
                    if n == 1:
                        after(pe, "gt_lo")
                    pe.wait_ge(sem("slot0"), n + 1)
                    turn(h, 2, S1[h], "aT_ps")
                    pe.wait_ge(sem("pn"), n + 1)
                    turn(h, 0, S2[h], "inT_ps")
                for n, h in of_pair[pair]:
                    after(pe, "gt_lo")
                    pe.wait_ge(sem("inT_lo"), B + n + 1)
                    for c in range(C):
                        for c2 in range(C):
                            ins = product(pe, bank(h, c), parts(GT, c2, slice(c * P, (c + 1) * P)), parts(RT[h], c2), c2 == 0, c2 == C - 1)
                    ins.then_inc(sem("kk_ps"), 1)
                    pe.wait_ge(sem("cw_lo"), 1)
                    pe.wait_ge(sem("slot_lo"), slot_lo_count(n, 0))
                    for j in range(TT):
                        for c in range(C):
                            ins = product(pe, token_banks(h, 2)[:, j], parts(RT[h], c, slice(j * P, (j + 1) * P)), parts(VW, c), c == 0, c == C - 1)
                    ins.then_inc(sem("v_ps"), 1)
                for steps in slot_steps[pair * ITERS:(pair + 1) * ITERS]:
                    for q, it, n, h in steps:
                        pe.wait_ge(sem("slot_sq"), q + 1)
                        for j in range(TT):
                            for c in range(C):
                                ins = pe.matmul(bank(h, 0)[:, j:j + 1], S0[h][:, c, j * P:(j + 1) * P], ones[:, 0:1], start=c == 0, stop=c == C - 1)
                        ins.then_inc(sem("ss_ps"), 1)
                    for q, it, n, h in steps:
                        pe.wait_ge(sem("diag"), q + 1)
                        pe.matmul(bank(h, 1), ones[:], S1[h][:].rearrange("p j d -> p (j d)")[:, 0:T], start=True, stop=True).then_inc(sem("rsb_ps"), 1)
                    for q, it, n, h in steps:
                        pe.wait_ge(sem("sn_lo"), q + 1)
                        if it == 0:
                            pe.wait_ge(sem("v_out"), n + 1)
                        for j in range(TT):
                            for c in range(C):
                                ins = product(pe, bank(h, j), parts(KK[h], c, slice(j * P, (j + 1) * P)), parts(RT[h], c), c == 0, c == C - 1)
                            ins.then_inc(sem("score_ps"), 1)
                    for q, it, n, h in steps:
                        pe.wait_ge(sem("vp"), q + 1)
                        for j in range(TT):
                            for m in range(TT):
                                ins = pe.matmul(bank(h, j)[:, 0:D + 1], HB[h][:, m, j * P:(j + 1) * P], VP[h][:, m, 0:D + 1], start=m == 0, stop=m == TT - 1)
                        ins.then_inc(sem("upd_ps"), 1)
                    for q, it, n, h in steps:
                        pe.wait_ge(sem("upd"), q + 1)
                        turn(h, 0, S2[h], "uT_ps")
                    for q, it, n, h in steps:
                        if q == 0:
                            pe.wait_ge(sem("cw_lo"), 3)
                            after(pe, "gbias")
                        pe.wait_ge(sem("uT_lo"), q + 1)
                        pe.wait_ge(sem("slot_lo"), slot_lo_count(n, it))
                        for d in range(C):
                            g = C * q + d

                            def gates(b, terms, name):
                                if d:
                                    pe.wait_ge(sem(name), g)
                                k = [(w, o, src, c) for w, o, src in terms for c in range(C)]
                                for i, (w, o, src, c) in enumerate(k):
                                    ins = product(pe, bank(h, b), parts(w, c, slice(o * P, (o + 1) * P)), parts(src, c), i == 0, i == len(k) - 1)
                                ins.then_inc(sem("gru_ps"), 1)

                            gates(0, [(WHH, 4 + d, HTS[h])], "hn_out")
                            gates(2, [(WHH, d, HTS[h]), (WIH, d, RT[h])], "r_out")
                            gates(1, [(WIH, 4 + d, RT[h])], "xn_out")
                            gates(3, [(WHH, 2 + d, HTS[h]), (WIH, 2 + d, RT[h])], "z_out")
                for n, h in of_pair[pair]:
                    pe.wait_ge(sem("slot_new"), slot_count(n, ITERS))
                    for j in range(TT):
                        for c in range(C):
                            ins = pe.transpose(token_banks(h, 0)[:, j, c * P:(c + 1) * P], HT[h][:, c, j * P:(j + 1) * P], ident[:])
                    ins.then_inc(sem("final_ps"), 1)
                for n, h in of_pair[pair]:
                    turn_xn(1, n, h, "batch_c")
                for n, h in of_pair[pair]:
                    logits(1, n, h)
                for n, h in of_pair[pair]:
                    ranks(1, n, h)
            table_pe(pe, 1)
            pe.wait_ge(sem("m1_table"), 1)
            moe_pe(pe, 1)


def lay_out(inputs):
    a = {k: np.asarray(v) for k, v in inputs.items()}
    c = np.ascontiguousarray

    def by_partition(v):
        return v.reshape(-1, P).T

    names = (("bq", "L0_xattn_bq"), ("bk", "L0_xattn_bk"), ("bv", "L0_xattn_bv"), ("gamma", "L0_xattn_gamma"),
             ("beta", "L0_xattn_beta"), ("b1", "L0_xattn_b1"), ("w_in", "L1_xattn_input_norm_w"),
             ("w_slot", "L1_xattn_slot_norm_w"), ("bih", "L1_xattn_gru_bih"), ("bhh", "L1_xattn_gru_bhh"),
             ("gate_b", "L1_ffn_gate_b"), ("up_b", "L1_ffn_up_b"))
    assert [n for n, _ in names] == list(COLS)
    return {
        "x": a["x"], "ctx_in": a["ctx_1024"],
        "cols": c(np.concatenate([by_partition(a[full]) for _, full in names], axis=1)),
        "rows": c(np.concatenate([a["L0_xattn_bo"], a["L0_xattn_gamma"], a["L0_xattn_beta"], a["L0_xattn_b2"],
                                  a["g_xattn"], a["g_ffn"]])),
        "wq": a["L0_xattn_wq"], "wk": a["L0_xattn_wk"], "wv": a["L0_xattn_wv"], "wo": a["L0_xattn_wo"],
        "pos_bias": a["L0_xattn_pos_bias"], "w1": a["L0_xattn_w1"], "w2": a["L0_xattn_w2"],
        "router1": c(a["L0_ffn_w_router"].T), "m1_w1": c(a["L0_ffn_w1_stack"].transpose(0, 2, 1)),
        "m1_w2": c(a["L0_ffn_w2_stack"].transpose(0, 2, 1)), "ws1": c(a["L0_ffn_ws1"].T), "ws2": c(a["L0_ffn_ws2"].T),
        "Wq": a["L1_xattn_Wq"], "Wk": a["L1_xattn_Wk"], "Wv": c(a["L1_xattn_Wv"].T),
        "wih": c(a["L1_xattn_gru_wih"].T), "whh": c(a["L1_xattn_gru_whh"].T), "router2": c(a["L1_ffn_router_w"].T),
        "gate_w": a["L1_ffn_gate_w"], "up_w": a["L1_ffn_up_w"], "down_w": a["L1_ffn_down_w"], "down_b": a["L1_ffn_down_b"],
    }


def program(nc, arrays):
    aps = {name: nc.dram_tensor(name, v.shape, mybir.dt.from_np(v.dtype), kind="ExternalInput").ap()
           for name, v in arrays.items()}
    build(nc, out=nc.dram_tensor("out", (B, T, D), F32, kind="ExternalOutput").ap(), **aps)


def kernel(**inputs):
    import concourse.bacc as _bacc
    from concourse.bass_utils import run_bass_kernel_spmd as _run

    arrays = lay_out(inputs)
    nc = _bacc.Bacc("TRN2", target_bir_lowering=False, num_devices=1)
    program(nc, arrays)
    r = _run(nc, [arrays], core_ids=[0])
    return r.results[0]["out"]
```

```python
from contextlib import ExitStack

import numpy as np
import concourse.bass as bass
from concourse import mybir
from concourse.alu_op_type import AluOpType as ALU

P = 128
F32 = mybir.dt.float32
F32R = mybir.dt.float32r
BF16 = mybir.dt.bfloat16
I32 = mybir.dt.int32
U32 = mybir.dt.uint32
ACT = mybir.ActivationFunctionType
AX = mybir.AxisListType.X

B, T, D = 4, 512, 256
TT = T // P
C = D // P
H = 1024
HC = H // P
BAND = 64
E = 8
FS = 512
SC = FS // P
F1 = 256
F2 = 512
G = 256
CAP = B * T + G
NG = B * T * 2 // G + E
XROWS = E * CAP + 2 * G
ITERS = 3
PAIRS = B // 2

ORDER_A = {
    "pe": "turn0 turn1 qk0 qk1 v0 v1 den0 num0 den1 attn0 num1 attn1 aT0 hid0 aT1 hid1 ffn0 ffn1 "
          "xnT0 logits0 upA0 lt0 upB0 xnT1 logits1 lt1 rank0 upA1 upB1 down0 rank1 table1 down1",
    "act": "turn0 turn1 qk0 qk1 v0 v1 aT0 hid0 aT1 hid1 xnT0 lt0 upA0 upB0 xnT1 logits0 lt1 logits1 upA1 upB1",
    "dve": "turn0 turn1 qk0 qk1 v0 v1 den0 num0 den1 attn0 num1 aT0 attn1 in0 ctx0 aT1 in1 ctx1 ffn0 xnT0 ffn1 "
           "xnT1 logits0 rank0 logits1 rank1 table1 down0 down1",
    "pool": "turn0 turn1 attn0 attn1 in0 ctx0 aT0 in1 ctx1 aT1 ffn0 ffn1 down0 down1",
    "sp": "in0 in1 ctx0 ctx1 down0 down1",
}

ORDER_C = {
    "pe": ("ctxT0 ctxT1 kk0 v0 kk1 v1 slotT0 slotT1 ss0 rsb0",
           "scoreA0 ss1 scoreB0 rsb1 upd0 scoreA1 uT0 scoreB1 ha0 ra0 na0 za0 upd1 hb0 rb0 uT1 nb0 zb0 "
           "ha1 ra1 na1 +ss0 za1 !final0 hb1 +rsb0 rb1 nb1 zb1 !xnT0",
           "logits0 lt0 final1 rank0 >slotT0 >ctxT0 >kk0 xnT1 >v0 logits1 lt1 rank1 >slotT1 >ctxT1 >kk1 >ss0 >v1 >rsb0"),
    "act": ("ctxT0 ctxT1 kk0 v0 kk1 v1 slotT0 sq0 slotT1 sq1 sn0",
            "expA0 expB0 sn1 expA1 uT0 expB1 ha0 ra0 na0 za0 hb0 rb0 uT1 nb0 zb0 "
            "ha1 +sq0 ra1 na1 za1 hb1 +sn0 rb1 nb1 zb1 +sq1 +hi0 +hi1 !xnT0",
            "lt0 exp0 >slotT0 >ctxT0 >kk0 xnT1 >v0 >sq0 lt1 exp1 >slotT1 >ctxT1 >kk1 >v1 >sq1 >sn0"),
    "dve": ("ctxT0 ctxT1 kk0 kk1 combine0 slots0 combine1 slots1 slotT0 ve0 slotT1 sn0 snlo0",
            "maxA0 ve1 maxB0 vp0 sn1 snlo1 upd0 maxA1 uT0 maxB1 0:combine0 0:combine1 vp1 1:ctx0 2:ctx1 "
            "ga0 za0 1:slots0 2:slots1 upd1 gb0 uT1 zb0 ga1 +ve0 za1 !final0 +sn0 +snlo0 gb1 zb1 +lo0 +lo1 !xnT0",
            "choose0 place0 >slotT0 >ctxT0 final1 >kk0 xnT1 choose1 place1 >slotT1 >ctxT1 >ve0 >kk1 >sn0 >snlo0"),
    "pool": ("gather0 gather1 weights0 slots0 slots1 ve0",
             "ve1 0:gather0 0:gather1 1:ctx0 2:ctx1 ha0 1:slots0 2:slots1 hb0 +ve0 ha1 !final0 hb1",
             "scatter0 final1 scatter1 >ve0"),
}

COLS = {}
for _name, _n in (("bq", C), ("bk", C), ("bv", C), ("gamma", C), ("beta", C), ("b1", HC), ("w_in", C), ("w_slot", C),
                  ("bih", 3 * C), ("bhh", 3 * C), ("gate_b", E * F2 // P), ("up_b", E * F2 // P)):
    _at = sum(n for _, n in COLS.values())
    COLS[_name] = (_at, _n)
NCOLS = sum(n for _, n in COLS.values())
ROWS = {"bo": 0, "gamma": D, "beta": 2 * D, "b2": 3 * D, "g": 4 * D}
NROWS = 4 * D + 4


def build(nc, x, ctx_in, cols, rows, wq, wk, wv, wo, pos_bias, w1, w2, router1, m1_w1, m1_w2, ws1, ws2,
          Wq, Wk, Wv, wih, whh, router2, gate_w, up_w, down_w, down_b, out):
    top = ExitStack()
    with top:
        def sb(name, shape, dt=F32, where=None):
            return (where or top).enter_context(nc.sbuf_tensor(name, shape, dt))

        sems = {}

        def sem(name):
            if name not in sems:
                sems[name] = top.enter_context(nc.semaphore(name))
            return sems[name]

        x_base = nc.dram_tensor("x_base", (2, B, T, D), F32, kind="Internal").ap()
        routed = [nc.dram_tensor(f"routed{m}", (XROWS, D), F32, kind="Internal").ap() for m in range(2)]
        outputs = nc.dram_tensor("outputs", (NG * G, D), F32, kind="Internal").ap()

        PS = top.enter_context(nc.psum_tensor("PS", [P, 8, 512], F32))
        ones = sb("ones", [P, P])
        tri = sb("tri", [P, P], BF16)
        ones_bf = sb("ones_bf", [P, P], BF16)
        ident = sb("ident", [P, P])
        zeros = sb("zeros", [P, D])
        no_rows = zeros[:].unsqueeze(1).to_broadcast([P, G // P, D])
        colv = sb("colv", [P, NCOLS])
        rowv = sb("rowv", [P, NROWS])
        minus_half = sb("minus_half", [P, TT])
        hbq = sb("hbq", [P, C])
        tanh_g = sb("tanh_g", [P, 4])
        bb = sb("bb", [P, D])
        g1 = sb("g1", [P, D])
        be1 = sb("be1", [P, D])
        iota_e = sb("iota_e", [P, E])
        ebase = sb("ebase", [P, E])
        iota_g = sb("iota_g", [P, 32])
        rw = [sb(f"rw{m}", [P, C, E], F32R) for m in range(4)]
        dest = [sb(f"dest{m}", [P, B, TT, 2], I32) for m in range(2)]
        share = [sb(f"share{m}", [P, B, TT, 2]) for m in range(2)]
        carry = sb("carry", [P, TT + 1, E])
        expert_of = sb("expert_of", [P, B, TT, 2])
        source = sb("source", [P, B, TT, 2], I32)
        table = [sb(f"table{m}", [1, 64], I32) for m in range(2)]
        tfi = sb("tfi", [P, 2, E], I32)
        two = range(2)
        X = [sb(f"X{h}", [P, TT, D]) for h in two]
        EMB = [sb(f"EMB{h}", [P, TT, D]) for h in two]
        S0 = [sb(f"S0{h}", [P, C, T]) for h in two]
        S1 = [sb(f"S1{h}", [P, TT, D]) for h in two]
        S2 = [sb(f"S2{h}", [P, TT, D]) for h in two]
        HB = [sb(f"HB{h}", [P, HC, T]) for h in two]
        RT = [sb(f"RT{h}", [P, 2, C, T], F32R) for h in two]
        st6 = [sb(f"st6{h}", [P, TT, 6]) for h in two]
        mv = [sb(f"mv{h}", [P, TT, 2]) for h in two]
        ve = [sb(f"ve{h}", [P, TT]) for h in two]
        rstd = [sb(f"rstd{h}", [P, TT]) for h in two]
        SM = [sb(f"SM{h}", [P, 5, TT]) for h in two]
        kb = [sb(f"kb{h}", [P, 2, C]) for h in two]
        RTM = [sb(f"RTM{h}", [P, 8, TT, E]) for h in two]
        rix = [sb(f"rix{h}", [P, TT, E], U32) for h in two]
        rbf = [sb(f"rbf{h}", [P, 2, TT, E], BF16) for h in two]

        ONCE = {"act": ("tanh_g", "hbq", "w3_hi", "ew", "gt_hi", "hbg"),
                "dve": ("w3_split", "bb", "g1", "be1", "row_max", "wmax", "ewT", "gt_lo", "gbias"),
                "pe": ("ewT_ps", "gt_ps")}

        def once(ins, name):
            who = next(k for k in ONCE if name in ONCE[k])
            ins.then_inc(sem(f"{who}_once"), 1)

        def after(eng, name):
            who = next(k for k in ONCE if name in ONCE[k])
            eng.wait_ge(sem(f"{who}_once"), ONCE[who].index(name) + 1)

        def col(name, i=0, n=1):
            return colv[:, COLS[name][0] + i:COLS[name][0] + i + n]

        def row(name, n=D):
            return rowv[:, ROWS[name]:ROWS[name] + n]

        def tiles(ap):
            return ap.unsqueeze(1).to_broadcast([P, TT, D])

        def bank(h, k):
            return PS[:, 4 * h + k, :]

        def banks(h, k, n=2):
            return PS[:, 4 * h + k:4 * h + k + n, :]

        def token_banks(h, k):
            return banks(h, k).rearrange("p b (a d) -> p (b a) d", d=D)

        def product(pe, out_, a, b, first=True, last=True):
            pe.matmul(out_, a[1], b[0], start=first, stop=False)
            pe.matmul(out_, a[0], b[1], start=False, stop=False)
            return pe.matmul(out_, a[0], b[0], start=False, stop=last)

        part_a = ExitStack()
        W3 = sb("W3", [P, 2, 3, C, D], F32R, part_a)
        W1 = sb("W1", [P, 2, C, H], F32R, part_a)
        WS1 = sb("WS1", [P, 2, C, FS], F32R, part_a)
        WO = sb("WO", [P, C, D], F32, part_a)
        W2 = sb("W2", [P, HC, D], F32, part_a)
        WS2 = sb("WS2", [P, SC, D], F32, part_a)
        EWT = sb("EWT", [P, TT, T], F32, part_a)
        wmax = sb("wmax", [P, TT], F32, part_a)
        NX = sb("NX", [P, TT, D], F32, part_a)
        NC = sb("NC", [P, TT, D], F32, part_a)
        part_m = [ExitStack(), ExitStack()]

        class Moe:
            pass

        moe = [Moe(), Moe()]

        def moe_buffers(m, f):
            w = moe[m]
            st = part_m[m]
            w.fc = f // P
            w.ups = m + 1
            w.cols = C * f * w.ups + w.fc * D
            w.raw = sb(f"raw{m}", [P, w.cols], F32, st)
            w.split = [sb(f"split{m}{i}", [P, 2, w.cols], F32R, st) for i in two]
            w.xg = sb(f"xg{m}", [P, G // P, D], F32, st)
            w.xt = sb(f"xt{m}", [P, 2, C, G], F32R, st)
            w.act = sb(f"act{m}", [P, 2, w.ups, G], F32, st)
            w.h = sb(f"h{m}", [P, w.fc, G], F32, st)
            w.hs = sb(f"hs{m}", [P, 2, w.fc, G], F32R, st)
            w.y = sb(f"y{m}", [P, G // P, D], F32, st)

        moe_buffers(0, F1)
        part_m[0].close()
        part_a.close()
        part_c = ExitStack()
        VW = sb("VW", [P, 2, C, D], F32R, part_c)
        GT = sb("GT", [P, 2, C, D], F32R, part_c)
        WIH = sb("WIH", [P, 2, C, 3 * D], F32R, part_c)
        WHH = sb("WHH", [P, 2, C, 3 * D], F32R, part_c)
        KK = [sb(f"KK{h}", [P, 2, C, T], F32R, part_c) for h in two]
        HT = [sb(f"HT{h}", [P, C, T], F32, part_c) for h in two]
        HTS = [sb(f"HTS{h}", [P, 2, C, T], F32R, part_c) for h in two]
        VP = [sb(f"VP{h}", [P, TT, D + 4], F32, part_c) for h in two]
        gbias = sb("gbias", [P, 3 * C], F32, part_c)
        XN = [sb(f"XN{h}", [P, TT, D], F32, part_c) for h in two]
        SN = [sb(f"SN{h}", [P, TT, D], F32, part_c) for h in two]
        CN = [sb(f"CN{h}", [P, TT, D], F32, part_c) for h in two]
        raw_wih = HB[0][:, 0:3, :].rearrange("p a b -> p (a b)").rearrange("p (c o) -> p c o", c=C)
        raw_wv = HB[0][:, 3, :].rearrange("p (c o) -> p c o", c=C)
        raw_whh = HB[1][:, 0:3, :].rearrange("p a b -> p (a b)").rearrange("p (c o) -> p c o", c=C)
        raw_q = HB[1][:, 3, :].rearrange("p (c o) -> p c o", c=C)
        raw_k = HB[1][:, 4, :].rearrange("p (c o) -> p c o", c=C)
        rows_h = [HB[h][:, 4:8, :].rearrange("p a b -> p (a b)").rearrange("p (k j d) -> p k j d", k=2, d=D) for h in two]

        def logits_sb(h):
            return HB[h][0:E, HC - 1]

        def gate_slot(h, d, k):
            if d == 0:
                return HB[h][:, 4 + k]
            return (S1[h][:, 0:2].rearrange("p j d -> p (j d)"), S1[h][:, 2:4].rearrange("p j d -> p (j d)"), S0[h][:, 0], S0[h][:, 1])[k]

        part_c.close()
        moe_buffers(1, F2)
        DB = sb("DB", [P, E, D], F32, part_m[1])
        hbg = sb("hbg", [P, E * F2 // P], F32, part_m[1])
        part_m[1].close()

        pairs = [(pair, 2 * pair + h, h) for pair in range(PAIRS) for h in two]
        of_pair = [[(n, h) for p_, n, h in pairs if p_ == pair] for pair in range(PAIRS)]

        def stages_a(engine):
            for pair in range(PAIRS):
                for item in ORDER_A[engine].split():
                    stage, h = item[:-1], int(item[-1])
                    n = 2 * (pair + (stage == "in")) + h
                    if n < B and (stage not in ("table", "ctx") or pair == PAIRS - 1):
                        yield stage, n, h

        def stages_c(engine):
            before, each, behind = ORDER_C[engine]

            def one(item, pair, it):
                stage, h = item[:-1], int(item[-1])
                if stage[0] == "+":
                    stage, it = stage[1:], it + 1
                elif stage[0] == ">":
                    stage, pair, it = stage[1:], pair + 1, 0
                elif stage[0] == "!":
                    stage, it = stage[1:], it if it == ITERS - 1 else ITERS
                elif ":" in stage:
                    when, stage = stage.split(":")
                    pair, it = (pair + 1, 0) if (pair, it) == (0, int(when)) else (PAIRS, 0)
                if pair < PAIRS and it < ITERS:
                    yield stage, 2 * pair + h, h % 2, it, (pair * ITERS + it) * 2 + h

            for item in before.split():
                yield from one(item, 0, 0)
            for pair in range(PAIRS):
                for it in range(ITERS):
                    for item in each.split():
                        yield from one(item, pair, it)
                for item in behind.split():
                    yield from one(item, pair, ITERS - 1)

        def slot_count(n, it):
            return n // 2 * (ITERS + 1) + it + 1

        def split_count(n, it):
            return n // 2 * ITERS + it + 1

        def residual(n, h):
            return X[h] if n < 2 else XN[h]

        def slots_in(n, h):
            return S2[h] if n < 2 else SN[h]

        def context_in(n, h):
            if n < 2:
                return (NC, NX)[h][:], EMB[h]
            return CN[h][:], CN[h]

        def up_weights(m, w, u, c, f):
            at = (u * C + c) * w.fc * P + f * P
            return slice(at, at + P)

        def down_weights(m, w, f):
            at = w.ups * C * w.fc * P + f * D
            return slice(at, at + D)

        def expert_sources(m, e):
            srcs = (m1_w1, m1_w2) if m == 0 else (gate_w, up_w, down_w)
            at = 0
            for src in srcs:
                ap = src[e].rearrange("(c p) o -> p c o", p=P)
                n = ap.shape[1] * ap.shape[2]
                yield ap, at, n
                at += n

        def bounds(eng, m, e):
            return (eng.value_load(table[m][0:1, e:e + 1], min_val=0, max_val=NG - 1),
                    eng.value_load(table[m][0:1, E + e:E + e + 1], min_val=1, max_val=NG))

        def counted(eng, m):
            eng.wait_ge(sem(f"m{m}_table"), 1)

        def moe_end(eng, m, total):
            for name, value in (("xg", 16 * (total + 2)), ("turned", total + 1), ("xhi", total + 1), ("xlo", total + 1),
                                ("down", total), ("y", total + 1), ("yout", 16 * total + 1)):
                eng.wait_ge(sem(f"m{m}_{name}"), value)
                eng.sem_inc(sem("passed"), 1)

        def raw_in(sp, m, e):
            w = moe[m]
            if e:
                sp.wait_ge(sem(f"m{m}_lo"), e)
            for ap, at, n in expert_sources(m, e):
                sp.dma_start(w.raw[:, at:at + n].rearrange("p (c o) -> p c o", c=ap.shape[1]), ap).then_inc(sem(f"m{m}_raw"), 16)

        def attention_weights(sp):
            for h in two:
                sp.wait_ge(sem(f"x_out{h}"), 16 * PAIRS)
            for dst, src in ((raw_wv, Wv), (raw_q, Wq), (raw_k, Wk), (raw_wih, wih), (raw_whh, whh)):
                sp.dma_start(dst, src.rearrange("(c p) o -> p c o", p=P)).then_inc(sem("cw_raw"), 16)

        def group_in(sp, m, t):
            r = sp.value_load(table[m][0:1, bass.ds(t + 2 * E, 1)], min_val=0, max_val=XROWS - G)
            sp.dma_start(moe[m].xg[:], routed[m][bass.ds(r, G), :].rearrange("(a p) d -> p a d", p=P)).then_inc(sem(f"m{m}_xg"), 16)

        def fill(sp, m, e, name):
            r = sp.value_load(table[m][0:1, 2 * E + 32 + e:2 * E + 33 + e], min_val=0, max_val=XROWS - G)
            sp.dma_start(routed[m][bass.ds(r, G), :].rearrange("(a p) d -> p a d", p=P), no_rows).then_inc(sem(name), 16)

        def first_group_in(sp, m):
            sp.wait_ge(sem(f"m{m}_table"), 1)
            for e in range(3):
                fill(sp, m, e, "first_filled")
            sp.wait_ge(sem("first_filled"), 48 * (m + 1))
            sp.wait_ge(sem("filled"), 16 * (4 + m * (E - 3)))
            sp.wait_ge(sem("outputs_filled"), 48)
            for h in two:
                sp.wait_ge(sem(f"scattered{h}"), 16 * 2 * TT * PAIRS * (m + 1))
            group_in(sp, m, 0)
            for e in range(3, E):
                fill(sp, m, e, "filled")

        def moe_sp(sp, m, more):
            w = moe[m]
            sp.wait_ge(sem(f"m{m}_turned"), 1)
            group_in(sp, m, 1)
            for e in range(E):
                if e == 1:
                    sp.wait_ge(sem("filled"), 16 * (4 + (m + 1) * (E - 3)))
                if e == (2, 0)[m]:
                    more(sp)
                if 1 <= e < E - 1:
                    raw_in(sp, m, e + 1)
                lo, hi = bounds(sp, m, e)
                with sp.Fori(lo, hi) as t:
                    counted(sp, m)
                    sp.wait_ge(sem(f"m{m}_turned"), t + 2)
                    group_in(sp, m, t + 2)
                    counted(sp, m)
                    sp.wait_ge(sem(f"m{m}_y"), t + 2)
                    sp.dma_start(outputs[bass.ds(t * G, G), :].rearrange("(a p) d -> p a d", p=P), w.y[:]).then_inc(sem(f"m{m}_yout"), 16)
            moe_end(sp, m, hi)

        def weights_hi(pool, m, e):
            w = moe[m]
            if e >= 2:
                done = pool.value_load(table[m][0:1, e - 1:e], min_val=1, max_val=NG - 1)
                counted(pool, m)
                pool.wait_ge(sem(f"m{m}_down"), done)
            for ap, at, n in expert_sources(m, e):
                pool.dma_start(w.split[e % 2][:, 0, at:at + n].rearrange("p (c o) -> p c o", c=ap.shape[1]), ap).then_inc(sem(f"m{m}_hi{e % 2}"), 16)

        def weights_lo(eng, m, e):
            w = moe[m]
            k = len(list(expert_sources(m, e)))
            eng.wait_ge(sem(f"m{m}_hi{e % 2}"), 16 * k * (e // 2 + 1))
            eng.wait_ge(sem(f"m{m}_raw"), 16 * k * (e + 1))
            eng.tensor_tensor(w.split[e % 2][:, 1], w.raw[:], w.split[e % 2][:, 0].bitcast(F32), ALU.subtract).then_inc(sem(f"m{m}_lo"), 1)

        def attention_weights_hi(pool):
            for dst, src in ((VW, Wv), (WIH, wih), (WHH, whh)):
                pool.dma_start(dst[:, 0], src.rearrange("(c p) o -> p c o", p=P)).then_inc(sem("cw_hi"), 16)

        def moe_pool(pool, m):
            pool.wait_ge(sem(f"m{m}_table"), 1)
            for e in range(2, E):
                if m == 0 and e == 3:
                    attention_weights_hi(pool)
                weights_hi(pool, m, e)
                weights_lo(pool, m, e)

        def moe_act(act, m):
            w = moe[m]

            def x_hi(n):
                act.wait_ge(sem(f"m{m}_turned"), n)
                act.activation(w.xt[:, 0], PS[:, 4, :].rearrange("p (c g) -> p c g", c=C), ACT.Copy).then_inc(sem(f"m{m}_xhi"), 1)

            x_hi(1)
            for e in range(E):
                lo, hi = bounds(act, m, e)
                with act.Fori(lo, hi) as t:
                    for f in range(w.fc):
                        act.wait_ge(sem(f"m{m}_up"), t * w.fc + f + 1)
                        if m == 0:
                            act.activation(w.act[:, f % 2, 0], PS[:, f, 0:G], ACT.Relu).then_inc(sem(f"m{m}_act"), 1)
                            act.wait_ge(sem(f"m{m}_act"), t * w.fc + f + 1)
                            act.activation(w.hs[:, 0, f], w.act[:, f % 2, 0], ACT.Square).then_inc(sem(f"m{m}_hhi"), 1)
                        else:
                            b = e * w.fc + f
                            act.activation(w.act[:, f % 2, 0], PS[:, f, 0:G], ACT.Tanh, bias=hbg[:, b:b + 1], scale=0.5)
                            act.activation(w.act[:, f % 2, 1], PS[:, f, 0:G], ACT.Identity, bias=hbg[:, b:b + 1], scale=0.5).then_inc(sem(f"m{m}_act"), 1)
                            if f:
                                act.wait_ge(sem(f"m{m}_h"), t * w.fc + f)
                                act.activation(w.hs[:, 0, f - 1], w.h[:, f - 1], ACT.Copy).then_inc(sem(f"m{m}_hhi"), 1)
                    if m == 1:
                        act.wait_ge(sem(f"m{m}_h"), t * w.fc + w.fc)
                        act.activation(w.hs[:, 0, w.fc - 1], w.h[:, w.fc - 1], ACT.Copy).then_inc(sem(f"m{m}_hhi"), 1)
                    x_hi(t + 2)
            if m == 0:
                moe_end(act, m, hi)

        def moe_dve(dve, m):
            w = moe[m]

            def x_lo(n):
                dve.wait_ge(sem(f"m{m}_xhi"), n)
                dve.tensor_tensor(w.xt[:, 1], PS[:, 4, :].rearrange("p (c g) -> p c g", c=C), w.xt[:, 0].bitcast(F32),
                                  ALU.subtract).then_inc(sem(f"m{m}_xlo"), 1)

            x_lo(1)
            for e in range(E):
                lo, hi = bounds(dve, m, e)
                with dve.Fori(lo, hi) as t:
                    for f in range(w.fc):
                        dve.wait_ge(sem(f"m{m}_act"), t * w.fc + f + 1)
                        a = w.act[:, f % 2]
                        if m == 0:
                            dve.scalar_tensor_tensor(out=w.h[:, f], in0=PS[:, f, 0:G], scalar=0.0, in1=a[:, 0],
                                                     op0=ALU.max, op1=ALU.mult).then_inc(sem(f"m{m}_h"), 1)
                        else:
                            dve.scalar_tensor_tensor(out=a[:, 0], in0=a[:, 0], scalar=1.0, in1=a[:, 1],
                                                     op0=ALU.add, op1=ALU.mult).then_inc(sem(f"m{m}_silu"), 1)
                            dve.wait_ge(sem(f"m{m}_silu"), t * w.fc + f + 1)
                            dve.scalar_tensor_tensor(out=w.h[:, f], in0=PS[:, f, G:2 * G], scalar=col("up_b", e * w.fc + f),
                                                     in1=a[:, 0], op0=ALU.add, op1=ALU.mult).then_inc(sem(f"m{m}_h"), 1)
                        if f:
                            dve.wait_ge(sem(f"m{m}_h"), t * w.fc + f)
                            dve.wait_ge(sem(f"m{m}_hhi"), t * w.fc + f)
                            dve.tensor_tensor(w.hs[:, 1, f - 1], w.h[:, f - 1], w.hs[:, 0, f - 1].bitcast(F32), ALU.subtract).then_inc(sem(f"m{m}_hlo"), 1)
                    dve.wait_ge(sem(f"m{m}_h"), t * w.fc + w.fc)
                    dve.wait_ge(sem(f"m{m}_hhi"), t * w.fc + w.fc)
                    dve.tensor_tensor(w.hs[:, 1, w.fc - 1], w.h[:, w.fc - 1], w.hs[:, 0, w.fc - 1].bitcast(F32), ALU.subtract).then_inc(sem(f"m{m}_hlo"), 1)
                    x_lo(t + 2)
                    dve.wait_ge(sem(f"m{m}_down"), t + 1)
                    dve.wait_ge(sem(f"m{m}_yout"), 16 * t + 1)
                    if m == 0:
                        dve.tensor_copy(w.y[:], PS[:, 5:7, 0:D]).then_inc(sem(f"m{m}_y"), 1)
                    else:
                        dve.tensor_tensor(w.y[:], PS[:, 5:7, 0:D], DB[:, e].unsqueeze(1).to_broadcast([P, G // P, D]),
                                          ALU.add).then_inc(sem(f"m{m}_y"), 1)
            moe_end(dve, m, hi)

        def moe_pe(pe, m):
            w = moe[m]

            def turn_rows(n):
                pe.wait_ge(sem(f"m{m}_xg"), 16 * n)
                for c in range(C):
                    for a in range(G // P):
                        ins = pe.transpose(PS[:, 4, c * G + a * P:c * G + (a + 1) * P], w.xg[:, a, c * P:(c + 1) * P], ident[:])
                ins.then_inc(sem(f"m{m}_turned"), 1)

            turn_rows(1)
            for e in range(E):
                s = w.split[e % 2]
                pe.wait_ge(sem(f"m{m}_lo"), e + 1)
                lo, hi = bounds(pe, m, e)
                with pe.Fori(lo, hi) as t:
                    pe.wait_ge(sem(f"m{m}_xlo"), t + 1)
                    for f in range(w.fc):
                        for u in range(w.ups):
                            for c in range(C):
                                at = up_weights(m, w, u, c, f)
                                ins = product(pe, PS[:, f, u * G:(u + 1) * G], (s[:, 0, at], s[:, 1, at]),
                                              (w.xt[:, 0, c], w.xt[:, 1, c]), c == 0, c == C - 1)
                        ins.then_inc(sem(f"m{m}_up"), 1)
                    turn_rows(t + 2)
                    pe.wait_ge(sem(f"m{m}_y"), t + 1)
                    for f in range(w.fc):
                        pe.wait_ge(sem(f"m{m}_hlo"), t * w.fc + f + 1)
                        at = down_weights(m, w, f)
                        for a in range(G // P):
                            tok = slice(a * P, (a + 1) * P)
                            ins = product(pe, PS[:, 5 + a, 0:D], (w.hs[:, 0, f, tok], w.hs[:, 1, f, tok]), (s[:, 0, at], s[:, 1, at]),
                                          f == 0, f == w.fc - 1)
                    ins.then_inc(sem(f"m{m}_down"), 1)
            if m == 0:
                moe_end(pe, m, hi)

        tf = HB[0][:, 4:8, :].rearrange("p a (b k) -> p (a b) k", k=32 * E)

        def table_pe(pe, m):
            pe.wait_ge(sem("total"), m + 1)
            pe.matmul(PS[:, 5, 2 * P:2 * P + E], ones_bf[:], rbf[0][:, 0, 0], start=True, stop=True).then_inc(sem("count_ps"), 1)

        def table_dve(dve, m, step, chained):
            dve.tensor_copy(rbf[0][:, 0, 0], carry[:, 0]).then_inc(sem("total"), 1)
            dve.wait_ge(sem("total"), m + 1)
            step(dve.memset(carry[:, 0], 0.0))
            dve.wait_ge(sem("count_ps"), m + 1)
            step(dve.tensor_scalar(tfi[:, 0], PS[:, 5, 2 * P:2 * P + E], float(G - 1), None, ALU.add))
            chained()
            step(dve.tensor_scalar(tfi[:, 1], tfi[:, 0], G.bit_length() - 1, None, ALU.logical_shift_right))
            chained()
            step(dve.tensor_tensor(tf[:, 7, 0:E], PS[:, 5, 2 * P:2 * P + E], ebase[:], ALU.add))
            step(dve.tensor_copy(tf[:, 0, 0:E], tfi[:, 1]))
            chained()
            step(dve.tensor_scalar(tf[:, 1, 0:E], tf[:, 0, 0:E], 1.0, None, ALU.max))
            chained()
            step(dve.tensor_copy(tf[:, 2, 0:1], tf[:, 1, 0:1]))
            for e in range(1, E):
                chained()
                step(dve.tensor_tensor(tf[:, 2, e:e + 1], tf[:, 2, e - 1:e], tf[:, 1, e:e + 1], ALU.add))
            chained()
            step(dve.tensor_tensor(tf[:, 3, 0:E], tf[:, 2, 0:E], tf[:, 1, 0:E], ALU.subtract))
            shape = [P, 32, E]
            past = tf[:, 4].rearrange("p (t e) -> p t e", e=E)
            step(dve.tensor_tensor(past, iota_g[:].unsqueeze(2).to_broadcast(shape), tf[:, 2, 0:E].unsqueeze(1).to_broadcast(shape), ALU.is_ge))
            chained()
            step(dve.tensor_reduce(tf[:, 5, 0:32], past, AX, ALU.add))
            step(dve.tensor_tensor(tf[:, 6].rearrange("p (t e) -> p t e", e=E), past, tf[:, 1, 0:E].unsqueeze(1).to_broadcast(shape), ALU.mult))
            chained()
            step(dve.tensor_reduce(tf[:, 5, 32:64], tf[:, 6].rearrange("p (t e) -> p t e", e=E), AX, ALU.add))
            chained()
            step(dve.tensor_tensor(tf[:, 5, 64:96], iota_g[:], tf[:, 5, 32:64], ALU.subtract))
            step(dve.tensor_scalar(tf[:, 5, 0:32], tf[:, 5, 0:32], float(CAP), None, ALU.mult))
            chained()
            step(dve.scalar_tensor_tensor(out=tf[:, 5, 96:128], in0=tf[:, 5, 64:96], scalar=float(G), in1=tf[:, 5, 0:32], op0=ALU.mult, op1=ALU.add))
            chained()
            step(dve.tensor_copy(table[m][:, 2 * E + 32:3 * E + 32], tf[0:1, 7, 0:E]))
            step(dve.tensor_copy(table[m][:, 0:E], tf[0:1, 3, 0:E]))
            step(dve.tensor_copy(table[m][:, E:2 * E], tf[0:1, 2, 0:E]))
            dve.tensor_copy(table[m][:, 2 * E:2 * E + 32], tf[0:1, 5, 96:128]).then_inc(sem(f"m{m}_table"), 1)
            step(dve.scalar_tensor_tensor(out=tf[:, 0, 0:E], in0=tf[:, 3, 0:E], scalar=float(G), in1=ebase[:], op0=ALU.mult, op1=ALU.subtract))
            which = tf[:, 4].rearrange("p (q e) -> p q e", e=E)
            shape = [P, B * TT * 2, E]
            step(dve.tensor_tensor(which, iota_e[:].unsqueeze(1).to_broadcast(shape),
                                   expert_of[:].rearrange("p n j k -> p (n j k)").unsqueeze(2).to_broadcast(shape), ALU.is_equal))
            chained()
            step(dve.tensor_tensor(which, which, tf[:, 0, 0:E].unsqueeze(1).to_broadcast(shape), ALU.mult))
            chained()
            step(dve.tensor_reduce(tf[:, 1, 0:B * TT * 2], which, AX, ALU.add))
            chained()
            dve.tensor_tensor(source[:].rearrange("p n j k -> p (n j k)"), tf[:, 1, 0:B * TT * 2],
                              dest[m][:].rearrange("p n j k -> p (n j k)"), ALU.add).then_inc(sem("source"), 1)

        block = top.enter_context(nc.Block())

        @block.sync
        def _(sp):
            sp.dma_start(rowv[:], rows.partition_broadcast(P)).then_inc(sem("const_in"), 16)
            sp.dma_start(colv[:], cols).then_inc(sem("const_in"), 16)

            def load_next(n):
                if n:
                    sp.wait_ge(sem("emb"), n)
                sp.dma_start(NX[:], x[n].rearrange("(j p) d -> p j d", p=P)).then_inc(sem("next_in"), 16)
                sp.dma_start(NC[:], ctx_in[n].rearrange("(j p) d -> p j d", p=P)).then_inc(sem("next_in"), 16)

            def load_residual(n, h):
                if n >= 2:
                    sp.wait_ge(sem(f"x_out{h}"), 16 * (n // 2))
                sp.dma_start(X[h][:], x[n].rearrange("(j p) d -> p j d", p=P)).then_inc(sem(f"x_in{h}"), 16)

            load_next(0)
            for k, src in enumerate((wq, wk, wv)):
                sp.dma_start(HB[1][:, k].rearrange("p (c o) -> p c o", c=C), src.rearrange("(c p) o -> p c o", p=P)).then_inc(sem("w3_in"), 16)
            load_next(1)
            sp.dma_start(HB[0][:, 0:TT, :], pos_bias.rearrange("(i p) j -> p i j", p=P)).then_inc(sem("pb_in"), 16)
            sp.dma_start(HB[1][:, 3:7, :].rearrange("p a b -> p (a b)").rearrange("p (c o) -> p c o", c=C), w1.rearrange("(c p) o -> p c o", p=P)).then_inc(sem("w1_in"), 16)
            sp.dma_start(S2[0][:].rearrange("p j d -> p (j d)").rearrange("p (c o) -> p c o", c=C), ws1.rearrange("(c p) o -> p c o", p=P)).then_inc(sem("w1_in"), 16)
            sp.dma_start(HB[1][:, 7, 0:C * E].rearrange("p (c o) -> p c o", c=C), router1.rearrange("(c p) o -> p c o", p=P)).then_inc(sem("w1_in"), 16)
            sp.dma_start(HB[1][:, 7, C * E:2 * C * E].rearrange("p (c o) -> p c o", c=C), router2.rearrange("(c p) o -> p c o", p=P)).then_inc(sem("w1_in"), 16)
            sp.dma_start(WO[:], wo.rearrange("(c p) o -> p c o", p=P)).then_inc(sem("wplain_in"), 16)
            sp.dma_start(W2[:], w2.rearrange("(c p) o -> p c o", p=P)).then_inc(sem("wplain_in"), 16)
            sp.dma_start(WS2[:], ws2.rearrange("(c p) o -> p c o", p=P)).then_inc(sem("wplain_in"), 16)
            sp.wait_ge(sem("pool_c"), 1)
            for m in two:
                for k in range(2):
                    sp.dma_start(routed[m][E * CAP + k * G:E * CAP + (k + 1) * G].rearrange("(a p) d -> p a d", p=P), no_rows)\
                      .then_inc(sem("filled"), 16)
            for k in range(3):
                sp.dma_start(outputs.rearrange("(k p q) d -> k p q d", k=3, p=P)[k],
                             zeros[:].unsqueeze(1).to_broadcast([P, NG * G // P // 3, D]))\
                  .then_inc(sem("outputs_filled"), 16)
            for n in two:
                load_residual(n, n)
            raw_in(sp, 0, 0)
            for stage, n, h in stages_a("sp"):
                if stage == "in":
                    load_next(n)
                elif stage == "ctx":
                    sp.wait_ge(sem("emb"), B)
                    sp.dma_start(context_in(h, h)[0], ctx_in[h].rearrange("(j p) d -> p j d", p=P)).then_inc(sem("context_in"), 16)
                elif stage == "down":
                    if n == PAIRS * 2 - 2:
                        first_group_in(sp, 0)
                    sp.wait_ge(sem("batch_a"), n + 1)
                    sp.dma_start(x_base[0, n].rearrange("(j p) d -> p j d", p=P), X[h][:]).then_inc(sem(f"x_out{h}"), 16)
                    if n + 2 < B:
                        load_residual(n + 2, h)
                    if n == 1:
                        raw_in(sp, 0, 1)
            moe_sp(sp, 0, attention_weights)
            for pair in range(PAIRS):
                for n, h in of_pair[pair]:
                    loaded = sem(f"x_in{h}" if pair == 0 else f"second_in{h}")
                    sp.dma_start(residual(n, h)[:], x_base[0, n].rearrange("(j p) d -> p j d", p=P)).then_inc(loaded, 16)
                    if pair:
                        sp.dma_start(context_in(n, h)[0], ctx_in[n].rearrange("(j p) d -> p j d", p=P)).then_inc(loaded, 16)
            for pair in range(PAIRS):
                if pair == PAIRS - 1:
                    sp.wait_ge(sem("batch_c"), B)
                    raw_in(sp, 1, 0)
                for n, h in of_pair[pair]:
                    sp.wait_ge(sem("batch_c"), n + 1)
                    sp.dma_start(x_base[1, n].rearrange("(j p) d -> p j d", p=P), X[h][:]).then_inc(sem(f"x_out{h}"), 16)
            for h in two:
                sp.wait_ge(sem(f"x_out{h}"), 16 * 2 * PAIRS)
            sp.dma_start(DB[:], down_b.rearrange("e d -> (e d)").partition_broadcast(P).rearrange("p (e d) -> p e d", d=D)).then_inc(sem("db_in"), 16)
            first_group_in(sp, 1)
            moe_sp(sp, 1, lambda sp: raw_in(sp, 1, 1))
            for pair in range(PAIRS):
                for n, h in of_pair[pair]:
                    if pair:
                        sp.wait_ge(sem(f"x_out{h}"), 16 * (2 * PAIRS + pair))
                    sp.dma_start(X[h][:], x_base[1, n].rearrange("(j p) d -> p j d", p=P)).then_inc(sem(f"x_in{h}"), 16)
                for n, h in of_pair[pair]:
                    sp.wait_ge(sem("combined"), B + n + 1)
                    sp.dma_start(out[n].rearrange("(j p) d -> p j d", p=P), X[h][:]).then_inc(sem(f"x_out{h}"), 16)
            for h in two:
                sp.wait_ge(sem(f"x_out{h}"), 16 * 3 * PAIRS)

        @block.gpsimd
        def _(pool):
            pool.memset(zeros[:], 0.0).then_inc(sem("pool_c"), 1)
            pool.memset(ident[:], 0.0).then_inc(sem("pool_c"), 1)
            pool.memset(ones[:], 1.0).then_inc(sem("pool_c"), 1)
            pool.memset(minus_half[:], -0.5).then_inc(sem("pool_c"), 1)
            pool.memset(ones_bf[:], 1.0).then_inc(sem("pool_c"), 1)
            pool.memset(carry[:], 0.0).then_inc(sem("pool_c"), 1)
            pool.iota(iota_e[:], pattern=[[1, E]], base=0, channel_multiplier=0, allow_small_or_imprecise_dtypes=True).then_inc(sem("pool_c"), 1)
            pool.iota(ebase[:], pattern=[[CAP, E]], base=0, channel_multiplier=0, allow_small_or_imprecise_dtypes=True).then_inc(sem("pool_c"), 1)
            pool.iota(iota_g[:], pattern=[[1, 32]], base=0, channel_multiplier=0, allow_small_or_imprecise_dtypes=True).then_inc(sem("pool_c"), 1)
            pool.wait_ge(sem("pool_c"), 9)
            pool.affine_select(out=ident[:], in_=ident[:], compare_op=ALU.not_equal, fill=1.0, base=0,
                               pattern=[[-1, P]], channel_multiplier=1).then_inc(sem("pool_c"), 1)
            pool.affine_select(out=tri[:], in_=ones_bf[:], compare_op=ALU.is_gt, fill=0.0, base=0,
                               pattern=[[1, P]], channel_multiplier=-1).then_inc(sem("pool_c"), 1)
            pool.wait_ge(sem("pool_c"), 11)

            ln = [0]

            def power(h):
                ln[0] += 1
                pool.wait_ge(sem("var_ready"), ln[0])
                pool.tensor_tensor(rstd[h][:], ve[h][:], minus_half[:], ALU.pow).then_inc(sem("rstd_ready"), 1)

            def scatter(m, n, h):
                pool.wait_ge(sem("dest"), m * B + n + 1)
                for j in range(TT):
                    for kk in range(2):
                        pool.indirect_dma_start(out=routed[m], out_offset=bass.IndirectOffsetOnAxis(ap=dest[m][:, n, j, kk:kk + 1], axis=0),
                                                in_=S2[h][:, j], in_offset=None).then_inc(sem(f"scattered{h}"), 16)

            for h in two:
                power(h)
            pool.wait_ge(sem("pb_in"), 16)
            band = HB[0][:, 0:TT, :]
            pool.affine_select(out=band, in_=band, compare_op=ALU.is_gt, fill=0.0, base=BAND,
                               pattern=[[-P, TT], [1, T]], channel_multiplier=-1).then_inc(sem("pool_c"), 1)
            pool.wait_ge(sem("pool_c"), 12)
            pool.affine_select(out=band, in_=band, compare_op=ALU.is_gt, fill=0.0, base=BAND,
                               pattern=[[P, TT], [-1, T]], channel_multiplier=1).then_inc(sem("pool_c"), 1)
            pool.wait_ge(sem("w1_in"), 64)
            raw_w1 = HB[1][:, 3:7, :].rearrange("p a b -> p (a b)").rearrange("p (c o) -> p c o", c=C)
            raw_ws1 = S2[0][:].rearrange("p j d -> p (j d)").rearrange("p (c o) -> p c o", c=C)
            raw_r = [HB[1][:, 7, m * C * E:(m + 1) * C * E].rearrange("p (c o) -> p c o", c=C) for m in two]
            split = [(raw_r[0], rw[0][:], rw[1][:]), (raw_r[1], rw[2][:], rw[3][:]),
                     (raw_w1, W1[:, 0], W1[:, 1]), (raw_ws1, WS1[:, 0], WS1[:, 1])]
            for raw, hi, lo in split:
                pool.tensor_copy(hi, raw).then_inc(sem("pool_c"), 1)
            for k, (raw, hi, lo) in enumerate(split):
                pool.wait_ge(sem("pool_c"), 13 + k + 1)
                pool.tensor_tensor(lo, raw, hi.bitcast(F32), ALU.subtract).then_inc(sem("w1_split"), 1)

            for stage, n, h in stages_a("pool"):
                if stage == "in":
                    power(h)
                elif stage == "turn":
                    pool.wait_ge(sem("inT_ps"), n + 1)
                    pool.tensor_tensor(EMB[h][:], EMB[h][:], tiles(row("bo")), ALU.add).then_inc(sem("embo"), 1)
                elif stage in ("attn", "ctx"):
                    power(h)
                elif stage == "aT":
                    pool.wait_ge(sem("r_norm"), n + 1)
                    if n == 0:
                        after(pool, "be1")
                    pool.tensor_tensor(S1[h][:], S2[h][:], tiles(row("gamma")), ALU.mult).then_inc(sem("atok"), 1)
                    pool.wait_ge(sem("atok"), 2 * n + 1)
                    pool.tensor_tensor(S1[h][:], S1[h][:], tiles(bb[:]), ALU.add).then_inc(sem("atok"), 1)
                    pool.wait_ge(sem(f"x_in{h}"), 16 * (n // 2 + 1))
                    pool.tensor_tensor(X[h][:], X[h][:], tiles(be1[:]), ALU.add).then_inc(sem("xbeta"), 1)
                elif stage == "ffn":
                    power(h)
                    power(h)
                elif stage == "down":
                    scatter(0, n, h)
                    if n < 2:
                        weights_hi(pool, 0, n)
                        weights_lo(pool, 0, n)
            pool.wait_ge(sem("batch_a"), B)
            moe_pool(pool, 0)

            def gather(m, n, h):
                for j in range(TT):
                    for kk in range(2):
                        pool.indirect_dma_start(out=rows_h[h][:, kk, j], out_offset=None, in_=outputs,
                                                in_offset=bass.IndirectOffsetOnAxis(ap=source[:, n, j, kk:kk + 1], axis=0))\
                            .then_inc(sem(f"rows{h}"), 16)

            def all_stored(m):
                pool.wait_ge(sem("source"), m + 1)
                total = pool.value_load(table[m][0:1, 2 * E - 1:2 * E], min_val=1, max_val=NG)
                moe_end(pool, m, total)

            pool.wait_ge(sem("cw_hi"), 48)
            pool.wait_ge(sem("cw_raw"), 80)
            pool.tensor_tensor(VW[:, 1], raw_wv, VW[:, 0].bitcast(F32), ALU.subtract).then_inc(sem("cw_lo"), 1)
            all_stored(0)
            for stage, n, h, it, q in stages_c("pool"):
                if stage == "gather":
                    if n == 1:
                        after(pool, "gt_ps")
                    if n >= 2:
                        pool.wait_ge(sem("combined"), n - 1)
                    gather(0, n, h)
                elif stage in ("slots", "ctx", "ve"):
                    power(h)
                elif stage == "weights":
                    pool.tensor_tensor(WIH[:, 1], raw_wih, WIH[:, 0].bitcast(F32), ALU.subtract).then_inc(sem("cw_lo"), 1)
                    pool.tensor_tensor(WHH[:, 1], raw_whh, WHH[:, 0].bitcast(F32), ALU.subtract).then_inc(sem("cw_lo"), 1)
                elif stage in ("ha", "hb"):
                    d = "ab".index(stage[1])
                    pool.wait_ge(sem("n_gate"), C * q + d + 1)
                    pool.tensor_tensor(gate_slot(h, d, 0), HT[h][:, d], gate_slot(h, d, 3), ALU.subtract).then_inc(sem("h_minus_n"), 1)
                elif stage == "final":
                    power(h)
                elif stage == "scatter":
                    if n == B - 1:
                        pool.wait_ge(sem("batch_c"), B)
                        weights_hi(pool, 1, 0)
                    scatter(1, n, h)
            weights_hi(pool, 1, 1)
            pool.wait_ge(sem("m1_lo"), 1)
            weights_lo(pool, 1, 1)
            moe_pool(pool, 1)
            all_stored(1)
            for pair in range(PAIRS):
                for n, h in of_pair[pair]:
                    if pair:
                        pool.wait_ge(sem("combined"), B + n - 1)
                    gather(1, n, h)

        @block.scalar
        def _(act):
            for m in two:
                act.sem_inc(sem(f"m{m}_y"), 1)
                act.sem_inc(sem(f"m{m}_yout"), 1)
            act.wait_ge(sem("const_in"), 32)
            once(act.activation(tanh_g[:], rowv[:, ROWS["g"]:ROWS["g"] + 4], ACT.Tanh), "tanh_g")
            once(act.activation(hbq[:], col("bq", 0, C), ACT.Copy, scale=0.5), "hbq")
            act.wait_ge(sem("w3_in"), 48)
            raw = HB[1][:, 0:3, :]
            once(act.activation(W3[:, 0].rearrange("p w c o -> p w (c o)"), raw, ACT.Copy), "w3_hi")

            def turned_hi(m, n, h):
                act.wait_ge(sem("xnT_ps"), m * B + n + 1)
                act.activation(RT[h][:, 0], banks(h, 2), ACT.Copy).then_inc(sem("xnT_hi"), 1)

            def logits_out(m, n, h):
                act.wait_ge(sem("logits_ps"), m * B + n + 1)
                act.activation(logits_sb(h), bank(h, 0)[0:E, :], ACT.Copy).then_inc(sem("logits_out"), 1)

            def route_exp(m, n, h):
                act.wait_ge(sem("rt_sub"), m * B + n + 1)
                act.activation(RTM[h][:, 1], RTM[h][:, 0], ACT.Exp).then_inc(sem("rt_exp"), 1)

            for stage, n, h in stages_a("act"):
                if stage == "turn":
                    act.wait_ge(sem("inT_ps"), n + 1)
                    act.activation(RT[h][:, 0], banks(h, 0), ACT.Copy).then_inc(sem("inT_hi"), 1)
                elif stage == "qk":
                    if n == 0:
                        after(act, "wmax")
                        for i in range(TT):
                            ins = act.activation(HB[0][:, i], HB[0][:, i], ACT.Exp, bias=wmax[:, i:i + 1])
                        once(ins, "ew")
                        after(act, "hbq")
                        after(act, "ewT_ps")
                    if n == 1:
                        act.wait_ge(sem("w1_split"), 4)
                    act.wait_ge(sem("qk_ps"), 2 * n + 1)
                    for c in range(C):
                        ins = act.activation(HB[h][:, 6 + c], bank(h, c), ACT.Tanh, bias=hbq[:, c:c + 1], scale=0.5)
                    ins.then_inc(sem("th"), 1)
                    act.wait_ge(sem("kbias"), n + 1)
                    for c in range(C):
                        ins = act.activation(S0[h][:, c], bank(h, 2 + c), ACT.Exp, bias=kb[h][:, 1, c:c + 1])
                    ins.then_inc(sem("ekT"), 1)
                elif stage == "v":
                    act.wait_ge(sem("ek_ps"), n + 1)
                    act.activation(HB[h][:, 0:2], banks(h, 2), ACT.Copy).then_inc(sem("ek"), 1)
                elif stage == "aT":
                    act.wait_ge(sem("aT_ps"), n + 1)
                    for c in range(C):
                        act.activation(RT[h][:, 0, c], bank(h, 2 + c), ACT.Identity, bias=col("beta", c), scale=col("gamma", c))
                        act.activation(S0[h][:, c], bank(h, 2 + c), ACT.Identity, bias=col("beta", c), scale=col("gamma", c))\
                           .then_inc(sem("aT"), 1)
                elif stage == "hid":
                    for m in range(HC):
                        act.wait_ge(sem("hid_ps"), HC * n + m + 1)
                        act.activation(HB[h][:, m], bank(h, m % 4), ACT.Relu, bias=col("b1", m)).then_inc(sem("hidden"), 1)
                elif stage == "xnT":
                    turned_hi(0, n, h)
                elif stage == "logits":
                    route_exp(0, n, h)
                elif stage == "lt":
                    logits_out(0, n, h)
                elif stage in ("upA", "upB"):
                    for f in (0, 1) if stage == "upA" else (2, 3):
                        act.wait_ge(sem("sh_ps"), SC * n + f + 1)
                        act.activation(HB[h][:, f], bank(h, 2 + f % 2), ACT.Relu).then_inc(sem("sh_relu"), 1)
                        act.wait_ge(sem("sh_relu"), SC * n + f + 1)
                        act.activation(HB[h][:, f], HB[h][:, f], ACT.Square).then_inc(sem("sh_sq"), 1)

            act.wait_ge(sem("m0_table"), 1)
            moe_act(act, 0)

            after(act, "gt_ps")
            once(act.activation(GT[:, 0], PS[:, 7, :].rearrange("p (c o) -> p c o", c=C), ACT.Copy), "gt_hi")
            for stage, n, h, it, q in stages_c("act"):
                if stage == "ctxT":
                    act.wait_ge(sem("inT_ps"), B + n + 1)
                    for c in range(C):
                        act.activation(S0[h][:, c], bank(h, c), ACT.Copy, scale=col("w_in", c))
                        ins = act.activation(RT[h][:, 0, c], bank(h, c), ACT.Copy, scale=col("w_in", c))
                    ins.then_inc(sem("inT_hi"), 1)
                elif stage == "slotT":
                    act.wait_ge(sem("aT_ps"), B + n + 1)
                    act.activation(HT[h][:], banks(h, 2), ACT.Copy).then_inc(sem(f"slot_new{h}"), 1)
                    act.activation(HTS[h][:, 0], banks(h, 2), ACT.Copy).then_inc(sem(f"slot_hi{h}"), 1)
                elif stage == "kk":
                    act.wait_ge(sem("kk_ps"), n + 1)
                    act.wait_ge(sem("inT_lo"), B + n + 1)
                    for c in range(C):
                        act.activation(S0[h][:, c], bank(h, c), ACT.Copy, scale=col("w_slot", c))
                        ins = act.activation(KK[h][:, 0, c], bank(h, c), ACT.Copy, scale=col("w_slot", c))
                    ins.then_inc(sem("kk_hi"), 1)
                elif stage == "v":
                    act.wait_ge(sem("v_ps"), B + n + 1)
                    act.activation(EMB[h][:], token_banks(h, 2), ACT.Copy).then_inc(sem("v_out"), 1)
                elif stage == "sq":
                    if it == 0:
                        act.wait_ge(sem("kk_lo"), n + 1)
                    act.wait_ge(sem(f"slot_new{h}"), slot_count(n, it))
                    act.activation(S0[h][:], HT[h][:], ACT.Square).then_inc(sem("slot_sq"), 1)
                elif stage == "sn":
                    act.wait_ge(sem("sn"), q + 1)
                    act.activation(RT[h][:, 0], S0[h][:], ACT.Copy).then_inc(sem("sn_hi"), 1)
                elif stage in ("expA", "expB"):
                    if q == 0:
                        act.wait_ge(sem("cw_lo"), 3)
                    for j in (0, 1) if stage == "expA" else (2, 3):
                        act.wait_ge(sem("smax"), TT * q + j + 1)
                        act.activation(HB[h][:, j], bank(h, j), ACT.Exp, bias=SM[h][:, 1, j:j + 1], scale=1.0 / 16,
                                       accum_out=SM[h][:, 2, j:j + 1]).then_inc(sem("sexp"), 1)
                elif stage == "uT":
                    act.wait_ge(sem("uT_ps"), q + 1)
                    act.activation(RT[h][:, 0], banks(h, 0), ACT.Copy).then_inc(sem("uT_hi"), 1)
                elif stage in ("ha", "hb"):
                    d = "ab".index(stage[1])
                    if stage == "ha" and n < 2 and it == 0:
                        act.wait_ge(sem("combined"), n + 3)
                    act.wait_ge(sem("gru_ps"), 4 * (C * q + d) + 1)
                    act.activation(gate_slot(h, d, 1), bank(h, 0), ACT.Identity, bias=gbias[:, 4 + d:5 + d], scale=0.5).then_inc(sem("hn_out"), 1)
                elif stage in ("ra", "rb"):
                    d = "ab".index(stage[1])
                    act.wait_ge(sem("gru_ps"), 4 * (C * q + d) + 2)
                    act.activation(gate_slot(h, d, 0), bank(h, 2), ACT.Tanh, bias=gbias[:, d:d + 1], scale=0.5).then_inc(sem("r_out"), 1)
                elif stage in ("na", "nb"):
                    d = "ab".index(stage[1])
                    act.wait_ge(sem("xn_out"), C * q + d + 1)
                    act.activation(gate_slot(h, d, 3), gate_slot(h, d, 3), ACT.Tanh, bias=col("bih", 4 + d)).then_inc(sem("n_gate"), 1)
                elif stage in ("za", "zb"):
                    d = "ab".index(stage[1])
                    act.wait_ge(sem("gru_ps"), 4 * (C * q + d) + 4)
                    act.activation(gate_slot(h, d, 2), bank(h, 3), ACT.Tanh, bias=gbias[:, 2 + d:3 + d], scale=0.5).then_inc(sem("z_out"), 1)
                elif stage == "hi":
                    act.wait_ge(sem(f"slot_new{h}"), slot_count(n, it))
                    act.activation(HTS[h][:, 0], HT[h][:], ACT.Copy).then_inc(sem(f"slot_hi{h}"), 1)
                elif stage == "xnT":
                    turned_hi(1, n, h)
                elif stage == "lt":
                    logits_out(1, n, h)
                elif stage == "exp":
                    route_exp(1, n, h)
            act.wait_ge(sem("m1_table"), 1)
            once(act.activation(hbg[:], col("gate_b", 0, E * F2 // P), ACT.Copy, scale=0.5), "hbg")
            after(act, "hbg")
            moe_act(act, 1)

        @block.vector
        def _(dve):
            k = [0]

            def step(ins):
                k[0] += 1
                ins.then_inc(sem("dve_step"), 1)

            def chained():
                dve.wait_ge(sem("dve_step"), k[0])

            ln = [0]

            def normalise(h, src, dst, eps, final):
                for j in range(TT):
                    ins = dve.bn_stats(st6[h][:, j], src[:, j])
                step(ins)
                chained()
                for j in range(TT):
                    ins = dve.bn_aggr(mv[h][:, j], st6[h][:, j])
                step(ins)
                chained()
                dve.tensor_scalar(ve[h][:], mv[h][:, :, 1], eps, None, ALU.add).then_inc(sem("var_ready"), 1)
                ln[0] += 1
                dve.wait_ge(sem("rstd_ready"), ln[0])
                for j in range(TT):
                    ins = dve.tensor_scalar(dst[:, j], src[:, j], mv[h][:, j, 0:1], rstd[h][:, j:j + 1], ALU.subtract, ALU.mult)
                final(ins)

            def lo_part(h, ps, name):
                dve.tensor_tensor(RT[h][:, 1], ps, RT[h][:, 0].bitcast(F32), ALU.subtract).then_inc(sem(name), 1)

            def choose(m, n, h, eps, gate):
                R = RTM[h]
                lg = bank(h, 1)[:, 2 * TT * E:3 * TT * E].rearrange("p (j e) -> p j e", e=E)
                q = m * B + n
                dve.wait_ge(sem("logits_t"), q + 1)
                step(dve.tensor_reduce(R[:, 7, :, 0], lg, AX, ALU.max))
                chained()
                dve.tensor_tensor(R[:, 0], lg, R[:, 7, :, 0:1].to_broadcast([P, TT, E]), ALU.subtract).then_inc(sem("rt_sub"), 1)
                dve.wait_ge(sem("rt_exp"), q + 1)
                step(dve.tensor_reduce(R[:, 7, :, 1], R[:, 1], AX, ALU.add))
                chained()
                step(dve.reciprocal(R[:, 7, :, 2], R[:, 7, :, 1]))
                chained()
                step(dve.tensor_tensor(R[:, 1], R[:, 1], R[:, 7, :, 2:3].to_broadcast([P, TT, E]), ALU.mult))
                chained()
                for j in range(TT):
                    ins = dve.max(R[:, 2, j], R[:, 1, j])
                step(ins)
                chained()
                for j in range(TT):
                    ins = dve.max_index(rix[h][:, j], R[:, 2, j], R[:, 1, j])
                step(ins)
                chained()
                step(dve.tensor_copy(R[:, 3, :, 0:2], rix[h][:, :, 0:2]))
                step(dve.tensor_copy(expert_of[:, n], rix[h][:, :, 0:2]))
                chained()
                for kk in range(2):
                    step(dve.tensor_tensor(R[:, 4 + kk], iota_e[:].unsqueeze(1).to_broadcast([P, TT, E]),
                                           R[:, 3, :, kk:kk + 1].to_broadcast([P, TT, E]), ALU.is_equal))
                step(dve.tensor_tensor(R[:, 7, :, 3], R[:, 2, :, 0], R[:, 2, :, 1], ALU.add))
                chained()
                step(dve.tensor_tensor(R[:, 6], R[:, 4], R[:, 5], ALU.add))
                step(dve.tensor_scalar(R[:, 7, :, 4], R[:, 7, :, 3], eps, None, ALU.add))
                chained()
                step(dve.tensor_copy(rbf[h][:, 0], R[:, 6]))
                for j in range(TT):
                    step(dve.tensor_tensor(carry[:, j + 1], carry[:, j], R[:, 6, j], ALU.add))
                    chained()
                dve.tensor_copy(rbf[h][:, 1], carry[:, 0:TT]).then_inc(sem("chosen"), 1)
                step(dve.reciprocal(R[:, 7, :, 5], R[:, 7, :, 4]))
                chained()
                step(dve.tensor_scalar(R[:, 7, :, 6], R[:, 7, :, 5], tanh_g[:, gate:gate + 1], None, ALU.mult))
                chained()
                step(dve.tensor_tensor(share[m][:, n], R[:, 2, :, 0:2], R[:, 7, :, 6:7].to_broadcast([P, TT, 2]), ALU.mult))
                dve.wait_ge(sem("chosen"), q + 1)
                step(dve.tensor_copy(carry[:, 0], carry[:, TT]))

            def place(m, n, h):
                R = RTM[h]
                q = m * B + n
                dve.wait_ge(sem("rank_ps"), q + 1)
                rank = bank(h, 1)[:, 0:TT * E].rearrange("p (j e) -> p j e", e=E)
                step(dve.tensor_tensor(R[:, 0], rank, ebase[:].unsqueeze(1).to_broadcast([P, TT, E]), ALU.add))
                chained()
                for kk in range(2):
                    step(dve.tensor_tensor(R[:, 4 + kk], R[:, 4 + kk], R[:, 0], ALU.mult))
                    chained()
                    step(dve.tensor_reduce(R[:, 3, :, kk], R[:, 4 + kk], AX, ALU.add))
                    chained()
                dve.tensor_copy(dest[m][:, n], R[:, 3, :, 0:2]).then_inc(sem("dest"), 1)

            def turned_lo(m, n, h):
                dve.wait_ge(sem("xnT_hi"), m * B + n + 1)
                lo_part(h, banks(h, 2), "xnT_lo")

            def embed(n, h):
                dve.wait_ge(sem("next_in"), 32 * (n + 1))
                normalise(h, NX, EMB[h], 1e-5, step)
                chained()
                dve.tensor_tensor(EMB[h][:], EMB[h][:], NC[:], ALU.add).then_inc(sem("emb"), 1)

            dve.wait_ge(sem("pool_c"), 11)
            for h in two:
                embed(h, h)
            after(dve, "w3_hi")
            once(dve.tensor_tensor(W3[:, 1].rearrange("p w c o -> p w (c o)"), HB[1][:, 0:3, :],
                                   W3[:, 0].rearrange("p w c o -> p w (c o)").bitcast(F32), ALU.subtract), "w3_split")
            after(dve, "tanh_g")
            once(dve.tensor_tensor(bb[:], row("beta"), row("b2"), ALU.add), "bb")
            once(dve.tensor_scalar(g1[:], row("gamma"), tanh_g[:, 0:1], None, ALU.mult), "g1")
            once(dve.tensor_scalar(be1[:], row("beta"), tanh_g[:, 0:1], None, ALU.mult), "be1")
            def context(n, h):
                ctx_t, to = context_in(n, h)
                dve.wait_ge(sem("context_in") if n < 2 else sem(f"second_in{h}"), 32)
                for j in range(TT):
                    ins = dve.bn_stats(st6[h][:, j], ctx_t[:, j])
                step(ins)
                chained()
                for j in range(TT):
                    ins = dve.bn_aggr(mv[h][:, j], st6[h][:, j])
                step(ins)
                chained()
                step(dve.tensor_tensor(SM[h][:, 0], mv[h][:, :, 0], mv[h][:, :, 0], ALU.mult))
                chained()
                dve.scalar_tensor_tensor(out=ve[h][:], in0=mv[h][:, :, 1], scalar=1e-6, in1=SM[h][:, 0], op0=ALU.add, op1=ALU.add)\
                   .then_inc(sem("var_ready"), 1)
                ln[0] += 1
                dve.wait_ge(sem("rstd_ready"), ln[0])
                for j in range(TT):
                    ins = dve.tensor_scalar(to[:, j], ctx_t[:, j], rstd[h][:, j:j + 1], None, ALU.mult)
                ins.then_inc(sem("pn"), 1)

            for stage, n, h in stages_a("dve"):
                if stage == "in":
                    embed(n, h)
                elif stage == "turn":
                    dve.wait_ge(sem("inT_hi"), n + 1)
                    lo_part(h, banks(h, 0), "inT_lo")
                elif stage == "qk":
                    if n == 0:
                        dve.wait_ge(sem("pool_c"), 13)
                        once(dve.tensor_reduce(wmax[:], HB[0][:, 0:TT, :], AX, ALU.max), "row_max")
                        after(dve, "row_max")
                        once(dve.tensor_scalar(wmax[:], wmax[:], -1.0, None, ALU.mult), "wmax")
                        after(dve, "ewT_ps")
                        once(dve.tensor_copy(EWT[:], banks(1, 0, 4)), "ewT")
                    dve.wait_ge(sem("qk_ps"), 2 * n + 2)
                    step(dve.tensor_reduce(kb[h][:, 0], banks(h, 2), AX, ALU.max))
                    chained()
                    step(dve.tensor_tensor(kb[h][:, 0], kb[h][:, 0], col("bk", 0, C), ALU.add))
                    chained()
                    dve.tensor_tensor(kb[h][:, 1], col("bk", 0, C), kb[h][:, 0], ALU.subtract).then_inc(sem("kbias"), 1)
                    dve.wait_ge(sem("th"), n + 1)
                    step(dve.tensor_scalar(HB[h][:, 6:8], HB[h][:, 6:8], 0.5, 0.5, ALU.mult, ALU.add))
                elif stage == "v":
                    dve.wait_ge(sem("v_ps"), n + 1)
                    dve.wait_ge(sem("ek"), n + 1)
                    dve.tensor_tensor(HB[h][:, 2:4], HB[h][:, 0:2], banks(h, 0), ALU.mult).then_inc(sem("ekv"), 1)
                elif stage == "den":
                    dve.wait_ge(sem("den_ps"), n + 1)
                    step(dve.reciprocal(S0[h][:], banks(h, 2)))
                elif stage == "num":
                    dve.wait_ge(sem("num_ps"), n + 1)
                    chained()
                    step(dve.tensor_tensor(S0[h][:], banks(h, 0), S0[h][:], ALU.mult))
                    chained()
                    for c in range(C):
                        ins = dve.scalar_tensor_tensor(out=HB[h][:, 4 + c], in0=S0[h][:, c], scalar=col("bv", c),
                                                       in1=HB[h][:, 6 + c], op0=ALU.add, op1=ALU.mult)
                    ins.then_inc(sem("yT"), 1)
                elif stage == "attn":
                    dve.wait_ge(sem("attn_ps"), n + 1)
                    dve.wait_ge(sem("embo"), n + 1)
                    step(dve.tensor_tensor(S1[h][:], token_banks(h, 0), EMB[h][:], ALU.add))
                    chained()
                    if n < 2:
                        dve.wait_ge(sem("w1_split"), 4)
                    else:
                        dve.wait_ge(sem(f"scattered{h}"), 16 * 2 * TT * (n // 2))
                    normalise(h, S1[h], S2[h], 1e-5, lambda ins: ins.then_inc(sem("r_norm"), 1))
                elif stage == "aT":
                    for c in range(C):
                        dve.wait_ge(sem("aT"), C * n + c + 1)
                        dve.tensor_tensor(RT[h][:, 1, c], S0[h][:, c], RT[h][:, 0, c].bitcast(F32), ALU.subtract).then_inc(sem("aT_lo"), 1)
                elif stage == "ffn":
                    dve.wait_ge(sem("ffn_ps"), n + 1)
                    dve.wait_ge(sem("atok"), 2 * n + 2)
                    step(dve.tensor_tensor(S2[h][:], token_banks(h, 0), S1[h][:], ALU.add))
                    chained()
                    normalise(h, S2[h], S1[h], 1e-5, step)
                    chained()
                    dve.wait_ge(sem("xbeta"), n + 1)
                    step(dve.tensor_tensor(S1[h][:], S1[h][:], tiles(g1[:]), ALU.mult))
                    chained()
                    step(dve.tensor_tensor(X[h][:], X[h][:], S1[h][:], ALU.add))
                    chained()
                    normalise(h, X[h], S2[h], 1e-5, lambda ins: ins.then_inc(sem("xn"), 1))
                elif stage == "xnT":
                    turned_lo(0, n, h)
                elif stage == "logits":
                    choose(0, n, h, 0.0, 2)
                elif stage == "rank":
                    place(0, n, h)
                elif stage == "table":
                    table_dve(dve, 0, step, chained)
                elif stage == "ctx":
                    context(h, h)
                elif stage == "down":
                    dve.wait_ge(sem("shared_ps"), n + 1)
                    dve.scalar_tensor_tensor(out=X[h][:].rearrange("p j d -> p (j d)"), in0=banks(h, 2).rearrange("p b t -> p (b t)"),
                                             scalar=tanh_g[:, 2:3],
                                             in1=X[h][:].rearrange("p j d -> p (j d)"), op0=ALU.mult, op1=ALU.add)\
                       .then_inc(sem("batch_a"), 1)
            dve.wait_ge(sem("m0_table"), 1)
            moe_dve(dve, 0)

            def combine(m, n, h):
                x_t = residual(n, h) if m == 0 else X[h]
                if m == 0 and n >= 2:
                    dve.wait_ge(sem(f"second_in{h}"), 32)
                else:
                    dve.wait_ge(sem(f"x_in{h}"), 16 * (PAIRS + 1) + (m and 16 * (n // 2 + 1)))
                dve.wait_ge(sem(f"rows{h}"), 16 * 2 * TT * (m * PAIRS + n // 2 + 1))
                for kk in range(2):
                    for j in range(TT):
                        ins = dve.scalar_tensor_tensor(out=x_t[:, j], in0=rows_h[h][:, kk, j], scalar=share[m][:, n, j, kk:kk + 1],
                                                       in1=x_t[:, j], op0=ALU.mult, op1=ALU.add)
                        if kk == 1 and j == TT - 1:
                            ins.then_inc(sem("combined"), 1)
                        elif j == TT - 1:
                            step(ins)
                            chained()

            after(dve, "gt_hi")
            once(dve.tensor_tensor(GT[:, 1], PS[:, 7, :].rearrange("p (c o) -> p c o", c=C), GT[:, 0].bitcast(F32), ALU.subtract), "gt_lo")
            step(dve.tensor_tensor(gbias[:, 0:4], col("bih", 0, 4), col("bhh", 0, 4), ALU.add))
            chained()
            step(dve.tensor_scalar(gbias[:, 0:4], gbias[:, 0:4], 0.5, None, ALU.mult))
            once(dve.tensor_scalar(gbias[:, 4:6], col("bhh", 4, 2), 0.5, None, ALU.mult), "gbias")
            for stage, n, h, it, q in stages_c("dve"):
                if stage == "combine":
                    combine(0, n, h)
                elif stage == "slots":
                    dve.wait_ge(sem("combined"), n + 1)
                    if n < 2:
                        dve.wait_ge(sem(f"scattered{h}"), 16 * 2 * TT * PAIRS)
                    normalise(h, residual(n, h), slots_in(n, h), 1e-5, lambda ins: ins.then_inc(sem("slot0"), 1))
                elif stage == "ctx":
                    context(n, h)
                elif stage == "ctxT":
                    dve.wait_ge(sem("inT_hi"), B + n + 1)
                    dve.tensor_tensor(RT[h][:, 1], S0[h][:], RT[h][:, 0].bitcast(F32), ALU.subtract).then_inc(sem("inT_lo"), 1)
                elif stage == "slotT":
                    dve.wait_ge(sem(f"slot_hi{h}"), split_count(n, 0))
                    dve.tensor_tensor(HTS[h][:, 1], banks(h, 2), HTS[h][:, 0].bitcast(F32), ALU.subtract).then_inc(sem(f"slot_lo{h}"), 1)
                elif stage == "kk":
                    dve.wait_ge(sem("kk_hi"), n + 1)
                    dve.tensor_tensor(KK[h][:, 1], S0[h][:], KK[h][:, 0].bitcast(F32), ALU.subtract).then_inc(sem("kk_lo"), 1)
                elif stage == "ve":
                    dve.wait_ge(sem("ss_ps"), q + 1)
                    dve.tensor_scalar(ve[h][:], bank(h, 0)[:, 0:TT], 1.0 / D, 1e-6, ALU.mult, ALU.add).then_inc(sem("var_ready"), 1)
                    ln[0] += 1
                    dve.wait_ge(sem("rstd_ready"), ln[0])
                    for j in range(TT):
                        ins = dve.tensor_scalar(S1[h][:].rearrange("p j d -> p (j d)")[:, j * P:(j + 1) * P], ident[:], rstd[h][:, j:j + 1], None, ALU.mult)
                    ins.then_inc(sem("diag"), 1)
                elif stage == "sn":
                    dve.wait_ge(sem("rsb_ps"), q + 1)
                    dve.tensor_tensor(S0[h][:], HT[h][:], bank(h, 1).unsqueeze(1).to_broadcast([P, C, T]), ALU.mult).then_inc(sem("sn"), 1)
                elif stage == "snlo":
                    dve.wait_ge(sem("sn_hi"), q + 1)
                    dve.tensor_tensor(RT[h][:, 1], S0[h][:], RT[h][:, 0].bitcast(F32), ALU.subtract).then_inc(sem("sn_lo"), 1)
                elif stage in ("maxA", "maxB"):
                    for j in (0, 1) if stage == "maxA" else (2, 3):
                        dve.wait_ge(sem("score_ps"), TT * q + j + 1)
                        step(dve.tensor_reduce(SM[h][:, 0, j:j + 1], bank(h, j), AX, ALU.max))
                        chained()
                        dve.tensor_scalar(SM[h][:, 1, j:j + 1], SM[h][:, 0, j:j + 1], -1.0 / 16, None, ALU.mult).then_inc(sem("smax"), 1)
                elif stage == "vp":
                    dve.wait_ge(sem("sexp"), TT * (q + 1))
                    if it == 0:
                        dve.wait_ge(sem("v_out"), n + 1)
                    step(dve.reciprocal(SM[h][:, 3], SM[h][:, 2]))
                    chained()
                    dve.tensor_copy(VP[h][:, :, D:D + 1], SM[h][:, 3].unsqueeze(2))
                    for j in range(TT):
                        ins = dve.tensor_scalar(VP[h][:, j, 0:D], EMB[h][:, j], SM[h][:, 3, j:j + 1], None, ALU.mult)
                    ins.then_inc(sem("vp"), 1)
                elif stage == "upd":
                    dve.wait_ge(sem("upd_ps"), q + 1)
                    if n >= 2 and it == 0:
                        dve.wait_ge(sem(f"scattered{h}"), 16 * 2 * TT * (PAIRS + 1))
                    step(dve.tensor_scalar(SM[h][:, 0], banks(h, 0, TT)[:, :, D], 1e-6, None, ALU.add))
                    chained()
                    step(dve.reciprocal(SM[h][:, 4], SM[h][:, 0]))
                    chained()
                    for j in range(TT):
                        ins = dve.tensor_scalar(S2[h][:, j], bank(h, j)[:, 0:D], SM[h][:, 4, j:j + 1], None, ALU.mult)
                    ins.then_inc(sem("upd"), 1)
                elif stage == "uT":
                    dve.wait_ge(sem("uT_hi"), q + 1)
                    lo_part(h, banks(h, 0), "uT_lo")
                elif stage in ("ga", "gb"):
                    d = "ab".index(stage[1])
                    dve.wait_ge(sem("r_out"), C * q + d + 1)
                    step(dve.scalar_tensor_tensor(out=gate_slot(h, d, 3), in0=gate_slot(h, d, 0), scalar=1.0, in1=gate_slot(h, d, 1), op0=ALU.add, op1=ALU.mult))
                    chained()
                    dve.wait_ge(sem("gru_ps"), 4 * (C * q + d) + 3)
                    dve.tensor_tensor(gate_slot(h, d, 3), bank(h, 1), gate_slot(h, d, 3), ALU.add).then_inc(sem("xn_out"), 1)
                elif stage in ("za", "zb"):
                    d = "ab".index(stage[1])
                    dve.wait_ge(sem("h_minus_n"), C * q + d + 1)
                    dve.wait_ge(sem("z_out"), C * q + d + 1)
                    step(dve.scalar_tensor_tensor(out=gate_slot(h, d, 1), in0=gate_slot(h, d, 2), scalar=1.0, in1=gate_slot(h, d, 0), op0=ALU.add, op1=ALU.mult))
                    chained()
                    ins = dve.scalar_tensor_tensor(out=HT[h][:, d], in0=gate_slot(h, d, 1), scalar=0.5, in1=gate_slot(h, d, 3), op0=ALU.mult, op1=ALU.add)
                    if stage == "zb":
                        ins.then_inc(sem(f"slot_new{h}"), 1)
                elif stage == "lo":
                    dve.wait_ge(sem(f"slot_hi{h}"), split_count(n, it))
                    dve.tensor_tensor(HTS[h][:, 1], HT[h][:], HTS[h][:, 0].bitcast(F32), ALU.subtract).then_inc(sem(f"slot_lo{h}"), 1)
                elif stage == "final":
                    dve.wait_ge(sem("final_ps"), n + 1)
                    if n >= 2:
                        dve.wait_ge(sem(f"x_out{h}"), 16 * (PAIRS + 1))
                    step(dve.scalar_tensor_tensor(out=X[h][:].rearrange("p j d -> p (j d)"), in0=banks(h, 0).rearrange("p b t -> p (b t)"),
                                                  scalar=tanh_g[:, 1:2], in1=residual(n, h)[:].rearrange("p j d -> p (j d)"), op0=ALU.mult, op1=ALU.add))
                    chained()
                    normalise(h, X[h], S2[h], 1e-5, lambda ins: ins.then_inc(sem("batch_c"), 1))
                elif stage == "xnT":
                    turned_lo(1, n, h)
                elif stage == "choose":
                    choose(1, n, h, 1e-9, 3)
                elif stage == "place":
                    place(1, n, h)
            table_dve(dve, 1, step, chained)
            weights_lo(dve, 1, 0)
            dve.wait_ge(sem("m1_table"), 1)
            dve.wait_ge(sem("db_in"), 16)
            moe_dve(dve, 1)
            for pair in range(PAIRS):
                for n, h in of_pair[pair]:
                    combine(1, n, h)

        @block.tensor
        def _(pe):
            def turn(h, k, src, name):
                for c in range(C):
                    for j in range(TT):
                        ins = pe.transpose(bank(h, k + c)[:, j * P:(j + 1) * P], src[:, j, c * P:(c + 1) * P], ident[:])
                ins.then_inc(sem(name), 1)

            def parts(t, *at):
                return tuple(t[(slice(None), i) + at] for i in two)

            def turn_xn(m, n, h, ready):
                pe.wait_ge(sem(ready), n + 1)
                turn(h, 2, S2[h], "xnT_ps")

            def logits(m, n, h):
                pe.wait_ge(sem("xnT_lo"), m * B + n + 1)
                for c in range(C):
                    ins = product(pe, bank(h, 0)[0:E, :], (rw[2 * m][:, c], rw[2 * m + 1][:, c]), parts(RT[h], c), c == 0, c == C - 1)
                ins.then_inc(sem("logits_ps"), 1)

            def logits_by_token(m, n, h):
                pe.wait_ge(sem("logits_out"), m * B + n + 1)
                for j in range(TT):
                    ins = pe.transpose(bank(h, 1)[:, 2 * TT * E + j * E:2 * TT * E + (j + 1) * E], logits_sb(h)[:, j * P:(j + 1) * P], ident[0:E, 0:E])
                ins.then_inc(sem("logits_t"), 1)

            def ranks(m, n, h):
                pe.wait_ge(sem("chosen"), m * B + n + 1)
                pe.matmul(bank(h, 1)[:, 0:TT * E], tri[:], rbf[h][:, 0].rearrange("p j e -> p (j e)"), start=True, stop=False)
                pe.matmul(bank(h, 1)[:, 0:TT * E], ones_bf[:], rbf[h][:, 1].rearrange("p j e -> p (j e)"), start=False, stop=True)\
                  .then_inc(sem("rank_ps"), 1)

            pe.wait_ge(sem("pool_c"), 11)
            for stage, n, h in stages_a("pe"):
                if stage == "turn":
                    pe.wait_ge(sem("emb"), n + 1)
                    if n >= 2:
                        pe.wait_ge(sem("dest"), n - 1)
                    turn(h, 0, EMB[h], "inT_ps")
                elif stage == "qk":
                    if n == 0:
                        after(pe, "w3_split")
                    if n == 1:
                        after(pe, "ewT")
                    if n >= 2:
                        pe.wait_ge(sem("batch_a"), n - 1)
                    pe.wait_ge(sem("inT_lo"), n + 1)
                    for w in range(2):
                        for c in range(C):
                            for c2 in range(C):
                                ins = product(pe, bank(h, 2 * w + c), parts(W3, w, c2, slice(c * P, (c + 1) * P)),
                                              parts(RT[h], c2), c2 == 0, c2 == C - 1)
                        ins.then_inc(sem("qk_ps"), 1)
                    if n == 0:
                        after(pe, "ew")
                        pe.wait_ge(sem("inT_lo"), 2)
                        for jc in range(TT):
                            for i in range(TT):
                                ins = pe.transpose(bank(1, jc)[:, i * P:(i + 1) * P], HB[0][:, i, jc * P:(jc + 1) * P], ident[:])
                        once(ins, "ewT_ps")
                elif stage == "v":
                    pe.wait_ge(sem("th"), n + 1)
                    for j in range(TT):
                        for c in range(C):
                            ins = product(pe, token_banks(h, 0)[:, j], parts(RT[h], c, slice(j * P, (j + 1) * P)),
                                          parts(W3, 2, c), c == 0, c == C - 1)
                    ins.then_inc(sem("v_ps"), 1)
                    pe.wait_ge(sem("ekT"), n + 1)
                    for j in range(TT):
                        for c in range(C):
                            ins = pe.transpose(token_banks(h, 2)[:, j, c * P:(c + 1) * P], S0[h][:, c, j * P:(j + 1) * P], ident[:])
                    ins.then_inc(sem("ek_ps"), 1)
                elif stage in ("den", "num"):
                    pe.wait_ge(sem("ek" if stage == "den" else "ekv"), n + 1)
                    if n == 0:
                        after(pe, "ewT")
                    b, src = (2, 0) if stage == "den" else (0, 2)
                    w = HB[h][:, src:src + 2].rearrange("p b (a d) -> p (b a) d", d=D)
                    for c in range(C):
                        for j in range(TT):
                            ins = pe.matmul(bank(h, b + c), w[:, j, c * P:(c + 1) * P], EWT[:, j], start=j == 0, stop=j == TT - 1)
                    ins.then_inc(sem(f"{stage}_ps"), 1)
                elif stage == "attn":
                    pe.wait_ge(sem("yT"), n + 1)
                    if n == 0:
                        pe.wait_ge(sem("wplain_in"), 48)
                    for j in range(TT):
                        for c in range(C):
                            ins = pe.matmul(token_banks(h, 0)[:, j], HB[h][:, 4 + c, j * P:(j + 1) * P], WO[:, c], start=c == 0, stop=c == C - 1)
                    ins.then_inc(sem("attn_ps"), 1)
                elif stage == "aT":
                    pe.wait_ge(sem("r_norm"), n + 1)
                    turn(h, 2, S2[h], "aT_ps")
                elif stage == "hid":
                    pe.wait_ge(sem("aT_lo"), C * (n + 1))
                    for m in range(HC):
                        if m >= 4:
                            pe.wait_ge(sem("hidden"), HC * n + m - 3)
                        for c in range(C):
                            ins = product(pe, bank(h, m % 4), parts(W1, c, slice(m * P, (m + 1) * P)), parts(RT[h], c), c == 0, c == C - 1)
                        ins.then_inc(sem("hid_ps"), 1)
                elif stage == "ffn":
                    pe.wait_ge(sem("hidden"), HC * (n + 1))
                    for j in range(TT):
                        for m in range(HC):
                            ins = pe.matmul(token_banks(h, 0)[:, j], HB[h][:, m, j * P:(j + 1) * P], W2[:, m], start=m == 0, stop=m == HC - 1)
                    ins.then_inc(sem("ffn_ps"), 1)
                elif stage == "xnT":
                    turn_xn(0, n, h, "xn")
                elif stage == "logits":
                    logits(0, n, h)
                elif stage == "lt":
                    logits_by_token(0, n, h)
                elif stage in ("upA", "upB"):
                    for f in (0, 1) if stage == "upA" else (2, 3):
                        if f >= 2:
                            pe.wait_ge(sem("sh_relu"), SC * n + f - 1)
                        for c in range(C):
                            ins = product(pe, bank(h, 2 + f % 2), parts(WS1, c, slice(f * P, (f + 1) * P)), parts(RT[h], c), c == 0, c == C - 1)
                        ins.then_inc(sem("sh_ps"), 1)
                elif stage == "rank":
                    ranks(0, n, h)
                elif stage == "table":
                    table_pe(pe, 0)
                elif stage == "down":
                    pe.wait_ge(sem("sh_sq"), SC * (n + 1))
                    for j in range(TT):
                        for f in range(SC):
                            ins = pe.matmul(token_banks(h, 2)[:, j], HB[h][:, f, j * P:(j + 1) * P], WS2[:, f], start=f == 0, stop=f == SC - 1)
                    ins.then_inc(sem("shared_ps"), 1)
            pe.wait_ge(sem("m0_table"), 1)
            moe_pe(pe, 0)

            pe.wait_ge(sem("cw_raw"), 80)
            for c in range(C):
                for o in range(C):
                    ins = pe.matmul(PS[:, 7, c * D:(c + 1) * D], raw_k[:, o, c * P:(c + 1) * P], raw_q[:, o], start=o == 0, stop=o == C - 1)
            once(ins, "gt_ps")
            for stage, n, h, it, q in stages_c("pe"):
                if stage == "slotT":
                    if n < 2:
                        pe.wait_ge(sem("v_out"), n + 1)
                    else:
                        pe.wait_ge(sem("xnT_lo"), B + n - 1)
                    pe.wait_ge(sem("slot0"), n + 1)
                    turn(h, 2, slots_in(n, h), "aT_ps")
                elif stage == "ctxT":
                    if n >= 2:
                        pe.wait_ge(sem("dest"), B + n - 1)
                    pe.wait_ge(sem("pn"), n + 1)
                    turn(h, 0, context_in(n, h)[1], "inT_ps")
                elif stage == "kk":
                    after(pe, "gt_lo")
                    pe.wait_ge(sem("inT_lo"), B + n + 1)
                    for c in range(C):
                        for c2 in range(C):
                            ins = product(pe, bank(h, c), parts(GT, c2, slice(c * P, (c + 1) * P)), parts(RT[h], c2), c2 == 0, c2 == C - 1)
                    ins.then_inc(sem("kk_ps"), 1)
                elif stage == "v":
                    pe.wait_ge(sem("cw_lo"), 1)
                    if n >= 2:
                        pe.wait_ge(sem(f"slot_lo{h}"), split_count(n, 0))
                    for j in range(TT):
                        for c in range(C):
                            ins = product(pe, token_banks(h, 2)[:, j], parts(RT[h], c, slice(j * P, (j + 1) * P)), parts(VW, c), c == 0, c == C - 1)
                    ins.then_inc(sem("v_ps"), 1)
                elif stage == "ss":
                    pe.wait_ge(sem("slot_sq"), q + 1)
                    for j in range(TT):
                        for c in range(C):
                            ins = pe.matmul(bank(h, 0)[:, j:j + 1], S0[h][:, c, j * P:(j + 1) * P], ones[:, 0:1], start=c == 0, stop=c == C - 1)
                    ins.then_inc(sem("ss_ps"), 1)
                elif stage == "rsb":
                    pe.wait_ge(sem("diag"), q + 1)
                    pe.matmul(bank(h, 1), ones[:], S1[h][:].rearrange("p j d -> p (j d)")[:, 0:T], start=True, stop=True).then_inc(sem("rsb_ps"), 1)
                elif stage in ("scoreA", "scoreB"):
                    pe.wait_ge(sem("sn_lo"), q + 1)
                    if it == 0:
                        pe.wait_ge(sem("v_out"), n + 1)
                    for j in (0, 1) if stage == "scoreA" else (2, 3):
                        for c in range(C):
                            ins = product(pe, bank(h, j), parts(KK[h], c, slice(j * P, (j + 1) * P)), parts(RT[h], c), c == 0, c == C - 1)
                        ins.then_inc(sem("score_ps"), 1)
                elif stage == "upd":
                    pe.wait_ge(sem("vp"), q + 1)
                    for j in range(TT):
                        for m in range(TT):
                            ins = pe.matmul(bank(h, j)[:, 0:D + 1], HB[h][:, m, j * P:(j + 1) * P], VP[h][:, m, 0:D + 1], start=m == 0, stop=m == TT - 1)
                    ins.then_inc(sem("upd_ps"), 1)
                elif stage == "uT":
                    pe.wait_ge(sem("upd"), q + 1)
                    turn(h, 0, S2[h], "uT_ps")
                elif stage in ("ha", "hb", "ra", "rb", "na", "nb", "za", "zb"):
                    d = "ab".index(stage[1])
                    if stage == "ha":
                        if q == 0:
                            pe.wait_ge(sem("cw_lo"), 3)
                            after(pe, "gbias")
                        pe.wait_ge(sem("uT_lo"), q + 1)
                        pe.wait_ge(sem(f"slot_lo{h}"), split_count(n, it))
                    b, terms, out_of_bank = {
                        "h": (0, [(WHH, 4 + d, HTS[h])], "hn_out"),
                        "r": (2, [(WHH, d, HTS[h]), (WIH, d, RT[h])], "r_out"),
                        "n": (1, [(WIH, 4 + d, RT[h])], "xn_out"),
                        "z": (3, [(WHH, 2 + d, HTS[h]), (WIH, 2 + d, RT[h])], "z_out")}[stage[0]]
                    if d:
                        pe.wait_ge(sem(out_of_bank), C * q + d)
                    factors = [(w, o, src, c) for w, o, src in terms for c in range(C)]
                    for i, (w, o, src, c) in enumerate(factors):
                        ins = product(pe, bank(h, b), parts(w, c, slice(o * P, (o + 1) * P)), parts(src, c), i == 0, i == len(factors) - 1)
                    ins.then_inc(sem("gru_ps"), 1)
                elif stage == "final":
                    pe.wait_ge(sem(f"slot_new{h}"), slot_count(n, ITERS))
                    for j in range(TT):
                        for c in range(C):
                            ins = pe.transpose(token_banks(h, 0)[:, j, c * P:(c + 1) * P], HT[h][:, c, j * P:(j + 1) * P], ident[:])
                    ins.then_inc(sem("final_ps"), 1)
                elif stage == "xnT":
                    turn_xn(1, n, h, "batch_c")
                elif stage == "logits":
                    logits(1, n, h)
                elif stage == "lt":
                    logits_by_token(1, n, h)
                elif stage == "rank":
                    ranks(1, n, h)
            table_pe(pe, 1)
            pe.wait_ge(sem("m1_table"), 1)
            moe_pe(pe, 1)


def lay_out(inputs):
    a = {k: np.asarray(v) for k, v in inputs.items()}
    c = np.ascontiguousarray

    def by_partition(v):
        return v.reshape(-1, P).T

    names = (("bq", "L0_xattn_bq"), ("bk", "L0_xattn_bk"), ("bv", "L0_xattn_bv"), ("gamma", "L0_xattn_gamma"),
             ("beta", "L0_xattn_beta"), ("b1", "L0_xattn_b1"), ("w_in", "L1_xattn_input_norm_w"),
             ("w_slot", "L1_xattn_slot_norm_w"), ("bih", "L1_xattn_gru_bih"), ("bhh", "L1_xattn_gru_bhh"),
             ("gate_b", "L1_ffn_gate_b"), ("up_b", "L1_ffn_up_b"))
    assert [n for n, _ in names] == list(COLS)
    return {
        "x": a["x"], "ctx_in": a["ctx_1024"],
        "cols": c(np.concatenate([by_partition(a[full]) for _, full in names], axis=1)),
        "rows": c(np.concatenate([a["L0_xattn_bo"], a["L0_xattn_gamma"], a["L0_xattn_beta"], a["L0_xattn_b2"],
                                  a["g_xattn"], a["g_ffn"]])),
        "wq": a["L0_xattn_wq"], "wk": a["L0_xattn_wk"], "wv": a["L0_xattn_wv"], "wo": a["L0_xattn_wo"],
        "pos_bias": a["L0_xattn_pos_bias"], "w1": a["L0_xattn_w1"], "w2": a["L0_xattn_w2"],
        "router1": c(a["L0_ffn_w_router"].T), "m1_w1": c(a["L0_ffn_w1_stack"].transpose(0, 2, 1)),
        "m1_w2": c(a["L0_ffn_w2_stack"].transpose(0, 2, 1)), "ws1": c(a["L0_ffn_ws1"].T), "ws2": c(a["L0_ffn_ws2"].T),
        "Wq": a["L1_xattn_Wq"], "Wk": a["L1_xattn_Wk"], "Wv": c(a["L1_xattn_Wv"].T),
        "wih": c(a["L1_xattn_gru_wih"].T), "whh": c(a["L1_xattn_gru_whh"].T), "router2": c(a["L1_ffn_router_w"].T),
        "gate_w": a["L1_ffn_gate_w"], "up_w": a["L1_ffn_up_w"], "down_w": a["L1_ffn_down_w"], "down_b": a["L1_ffn_down_b"],
    }


def program(nc, arrays):
    aps = {name: nc.dram_tensor(name, v.shape, mybir.dt.from_np(v.dtype), kind="ExternalInput").ap()
           for name, v in arrays.items()}
    build(nc, out=nc.dram_tensor("out", (B, T, D), F32, kind="ExternalOutput").ap(), **aps)


def kernel(**inputs):
    import concourse.bacc as _bacc
    from concourse.bass_utils import run_bass_kernel_spmd as _run

    arrays = lay_out(inputs)
    nc = _bacc.Bacc("TRN2", target_bir_lowering=False, num_devices=1)
    program(nc, arrays)
    r = _run(nc, [arrays], core_ids=[0])
    return r.results[0]["out"]
```
